# Optimizing a Trainium2 kernel written in Bass

```python
import numpy as np
import jax
import jax.numpy as jnp

def _softmax(x, axis=-1):
    return jax.nn.softmax(x, axis=axis)

def _gelu(x):
    return jax.nn.gelu(x, approximate=True)

def _silu(x):
    return jax.nn.silu(x)

def _sigmoid(x):
    return jax.nn.sigmoid(x)

def _layernorm(x, axis=-1, eps=1e-05):
    m = jnp.mean(x, axis=axis, keepdims=True)
    v = jnp.var(x, axis=axis, keepdims=True)
    return (x - m) / jnp.sqrt(v + eps)

def _scatter_add(tgt, idx, src, axis=0):
    return tgt.at[idx].add(src)

def _segment_sum(src, seg, n):
    return jax.ops.segment_sum(src, seg, n)
kernel_name = 'mk_perceiver_d2_seqx_r4_2c201e'

def setup_inputs(seed: int=0):
    np.random.seed(seed)
    _w = jnp.asarray

    def _rec_inputs():
        import jax
        import jax.numpy as jnp
        _rk = jax.random.key(seed)
        x = -0.0002928 + 1 * jax.random.normal(jax.random.fold_in(_rk, 1), (1, 128, 256), jnp.float32)
        _lenS = 128 - jax.random.randint(jax.random.fold_in(_rk, 7), (1,), 0, max(1, 128 // 4) + 1, jnp.int32)
        _lenS2 = 12544 - jax.random.randint(jax.random.fold_in(_rk, 8), (1,), 0, max(1, 12544 // 4) + 1, jnp.int32)
        _ctx_768P = jax.random.normal(jax.random.fold_in(_rk, 11), (1, 16, 192), jnp.float32)
        _ctx_768c = jax.random.dirichlet(jax.random.fold_in(_rk, 511), 0.3 * jnp.ones((16,), jnp.float32), (1, 12544))
        _ctx_768t = jnp.einsum('bsk,bkd->bsd', _ctx_768c, _ctx_768P)
        _ctx_768t = _ctx_768t * jax.lax.rsqrt(jnp.mean(jnp.square(_ctx_768t)) + 1e-12) * 0.953939
        ctx_768 = 2.09791e-05 + 1.00001 * (_ctx_768t + 0.3 * jax.random.normal(jax.random.fold_in(_rk, 611), (1, 12544, 192), jnp.float32))
        return (x, ctx_768)
    x, ctx_768 = _rec_inputs()

    def _L0_xattn_setup():
        import jax, jax.numpy as jnp
        import numpy as np
        H = 8
        D = 64
        SCALE = D ** (-0.5)
        key = jax.random.key(seed)
        ks = jax.random.split(key, 7)
        B, Nq, Nkv = (2, 512, 512)
        Cq, Ck, I = (256, 192, H * D)
        return {'x': jax.random.normal(ks[0], (B, Nq, Cq), jnp.float32), 'context': jax.random.normal(ks[1], (B, Nkv, Ck), jnp.float32), 'Wq': jax.random.normal(ks[2], (Cq, I), jnp.float32) * Cq ** (-0.5), 'Wk': jax.random.normal(ks[3], (Ck, I), jnp.float32) * Ck ** (-0.5), 'Wv': jax.random.normal(ks[4], (Ck, I), jnp.float32) * Ck ** (-0.5), 'Wo': jax.random.normal(ks[5], (I, Cq), jnp.float32) * I ** (-0.5), 'bo': jnp.zeros((Cq,), jnp.float32)}
    _L0_xattn_all = _L0_xattn_setup()
    _L0_xattn_in = {k: v for k, v in _L0_xattn_all.items() if k in ('Wq', 'Wk', 'Wv', 'Wo', 'bo')}
    del _L0_xattn_all

    def _L0_attn_setup():
        import jax, jax.numpy as jnp
        import numpy as np
        EMBED_DIM = 256
        NUM_HEADS = 16
        HEAD_DIM = EMBED_DIM // NUM_HEADS
        WINDOW_SIZE = 64
        SCALE = 1.0 / np.sqrt(HEAD_DIM)

        def _band_mask(T):
            i = jnp.arange(T)[:, None]
            j = jnp.arange(T)[None, :]
            full = j > i
            band = full & (j >= i - (WINDOW_SIZE - 1))
            return band
        key = jax.random.key(seed)
        kx, kq, kk, kv, ko = jax.random.split(key, 5)
        B, T, C = (2, 512, EMBED_DIM)
        x = jax.random.normal(kx, (B, T, C), dtype=jnp.float32)
        s = 1.0 / np.sqrt(C)
        Wq = jax.random.uniform(kq, (C, C), dtype=jnp.float32, minval=-s, maxval=s)
        Wk = jax.random.uniform(kk, (C, C), dtype=jnp.float32, minval=-s, maxval=s)
        Wv = jax.random.uniform(kv, (C, C), dtype=jnp.float32, minval=-s, maxval=s)
        Wo = jax.random.uniform(ko, (C, C), dtype=jnp.float32, minval=-s, maxval=s)
        return {'x': x, 'Wq': Wq, 'Wk': Wk, 'Wv': Wv, 'Wo': Wo}
    _L0_attn_all = _L0_attn_setup()
    _L0_attn_in = {k: v for k, v in _L0_attn_all.items() if k in ('Wq', 'Wk', 'Wv', 'Wo')}
    del _L0_attn_all

    def _L0_ffn_setup():
        import jax, jax.numpy as jnp
        import numpy as np
        B, S, D = (1, 512, 256)
        F = 352
        E = 16
        K = 2
        CAP_FACTOR = 1.25

        def _mlp(h, wg, wu, wd):
            return jax.nn.silu(h @ wg) * (h @ wu) @ wd
        key = jax.random.key(seed)
        ks = jax.random.split(key, 10)
        sd = 0.02
        return {'x': jax.random.normal(ks[0], (B, S, D), jnp.float32), 'router_w': jax.random.normal(ks[1], (D, E), jnp.float32) * sd, 'router_b': jnp.zeros((E,), jnp.float32), 'w_gate': jax.random.normal(ks[2], (E, D, F), jnp.float32) * sd, 'w_up': jax.random.normal(ks[3], (E, D, F), jnp.float32) * sd, 'w_down': jax.random.normal(ks[4], (E, F, D), jnp.float32) * sd, 'sw_gate': jax.random.normal(ks[5], (D, F), jnp.float32) * sd, 'sw_up': jax.random.normal(ks[6], (D, F), jnp.float32) * sd, 'sw_down': jax.random.normal(ks[7], (F, D), jnp.float32) * sd}
    _L0_ffn_all = _L0_ffn_setup()
    _L0_ffn_in = {k: v for k, v in _L0_ffn_all.items() if k in ('router_w', 'router_b', 'w_gate', 'w_up', 'w_down', 'sw_gate', 'sw_up', 'sw_down')}
    del _L0_ffn_all

    def _L1_xattn_setup():
        import jax, jax.numpy as jnp
        import numpy as np
        QUERY_DIM = 256
        KEY_DIM = 192
        NUM_HEADS = 16
        HEAD_DIM = QUERY_DIM // NUM_HEADS
        SCALE = HEAD_DIM ** (-0.5)
        key = jax.random.key(seed)
        ks = jax.random.split(key, 11)
        B, Nq, Nk = (4, 1024, 256)
        s_q = QUERY_DIM ** (-0.5)
        s_k = KEY_DIM ** (-0.5)
        return {'query': jax.random.normal(ks[0], (B, Nq, QUERY_DIM), jnp.float32), 'key': jax.random.normal(ks[1], (B, Nk, KEY_DIM), jnp.float32), 'value': jax.random.normal(ks[2], (B, Nk, KEY_DIM), jnp.float32), 'Wq': jax.random.normal(ks[3], (QUERY_DIM, QUERY_DIM), jnp.float32) * s_q, 'bq': jnp.zeros((QUERY_DIM,), jnp.float32), 'Wk': jax.random.normal(ks[4], (KEY_DIM, QUERY_DIM), jnp.float32) * s_k, 'bk': jnp.zeros((QUERY_DIM,), jnp.float32), 'Wv': jax.random.normal(ks[5], (KEY_DIM, QUERY_DIM), jnp.float32) * s_k, 'bv': jnp.zeros((QUERY_DIM,), jnp.float32), 'Wo': jax.random.normal(ks[6], (QUERY_DIM, QUERY_DIM), jnp.float32) * s_q, 'bo': jnp.zeros((QUERY_DIM,), jnp.float32)}
    _L1_xattn_all = _L1_xattn_setup()
    _L1_xattn_in = {k: v for k, v in _L1_xattn_all.items() if k in ('Wq', 'bq', 'Wk', 'bk', 'Wv', 'bv', 'Wo', 'bo')}
    del _L1_xattn_all

    def _L1_attn_setup():
        import math
        import jax, jax.numpy as jnp
        import numpy as np
        H = 256
        NH = 16
        HD = H // NH
        FF = 1024
        EPS = 1e-12

        def _lin(key, fan_in, fan_out):
            k1, k2 = jax.random.split(key)
            bound = 1.0 / math.sqrt(fan_in)
            W = jax.random.uniform(k1, (fan_in, fan_out), jnp.float32, -bound, bound)
            b = jax.random.uniform(k2, (fan_out,), jnp.float32, -bound, bound)
            return (W, b)

        def _layernorm(x, g, b):
            mu = jnp.mean(x, axis=-1, keepdims=True)
            var = jnp.mean((x - mu) ** 2, axis=-1, keepdims=True)
            return (x - mu) * jax.lax.rsqrt(var + EPS) * g + b

        def _gelu(x):
            return x * 0.5 * (1.0 + jax.lax.erf(x / jnp.sqrt(jnp.float32(2.0))))
        key = jax.random.key(seed)
        ks = jax.random.split(key, 8)
        x = jax.random.normal(ks[0], (4, 1024, H), jnp.float32)
        Wq, bq = _lin(ks[1], H, H)
        Wk, bk = _lin(ks[2], H, H)
        Wv, bv = _lin(ks[3], H, H)
        Wo, bo = _lin(ks[4], H, H)
        W1, b1 = _lin(ks[5], H, FF)
        W2, b2 = _lin(ks[6], FF, H)
        g1 = jnp.ones((H,), jnp.float32)
        be1 = jnp.zeros((H,), jnp.float32)
        g2 = jnp.ones((H,), jnp.float32)
        be2 = jnp.zeros((H,), jnp.float32)
        return dict(x=x, Wq=Wq, bq=bq, Wk=Wk, bk=bk, Wv=Wv, bv=bv, Wo=Wo, bo=bo, g1=g1, be1=be1, W1=W1, b1=b1, W2=W2, b2=b2, g2=g2, be2=be2)
    _L1_attn_all = _L1_attn_setup()
    _L1_attn_in = {k: v for k, v in _L1_attn_all.items() if k in ('Wq', 'bq', 'Wk', 'bk', 'Wv', 'bv', 'Wo', 'bo', 'g1', 'be1', 'W1', 'b1', 'W2', 'b2', 'g2', 'be2')}
    del _L1_attn_all

    def _L1_ffn_setup():
        import jax, jax.numpy as jnp
        import numpy as np
        from math import ceil
        CAPACITY_FACTOR = 2.0
        MIN_CAPACITY = 4
        key = jax.random.key(seed)
        ks = jax.random.split(key, 4)
        B, S, D, Di, E = (4, 512, 256, 1024, 8)
        x = jax.random.normal(ks[0], (B, S, D), dtype=jnp.float32)
        Wr = jax.random.normal(ks[1], (D, E), dtype=jnp.float32) * D ** (-0.5)
        W1 = jax.random.normal(ks[2], (E, D, Di), dtype=jnp.float32) * D ** (-0.5)
        b1 = jnp.zeros((E, Di), dtype=jnp.float32)
        W2 = jax.random.normal(ks[3], (E, Di, D), dtype=jnp.float32) * Di ** (-0.5)
        b2 = jnp.zeros((E, D), dtype=jnp.float32)
        return {'x': x, 'Wr': Wr, 'W1': W1, 'b1': b1, 'W2': W2, 'b2': b2}
    _L1_ffn_all = _L1_ffn_setup()
    _L1_ffn_in = {k: v for k, v in _L1_ffn_all.items() if k in ('Wr', 'W1', 'b1', 'W2', 'b2')}
    del _L1_ffn_all
    return {'x': x, 'ctx_768': ctx_768, 'L0_xattn_Wq': _L0_xattn_in['Wq'], 'L0_xattn_Wk': _L0_xattn_in['Wk'], 'L0_xattn_Wv': _L0_xattn_in['Wv'], 'L0_xattn_Wo': _L0_xattn_in['Wo'], 'L0_xattn_bo': _L0_xattn_in['bo'], 'L0_attn_Wq': _L0_attn_in['Wq'], 'L0_attn_Wk': _L0_attn_in['Wk'], 'L0_attn_Wv': _L0_attn_in['Wv'], 'L0_attn_Wo': _L0_attn_in['Wo'], 'L0_ffn_router_w': _L0_ffn_in['router_w'], 'L0_ffn_router_b': _L0_ffn_in['router_b'], 'L0_ffn_w_gate': _L0_ffn_in['w_gate'], 'L0_ffn_w_up': _L0_ffn_in['w_up'], 'L0_ffn_w_down': _L0_ffn_in['w_down'], 'L0_ffn_sw_gate': _L0_ffn_in['sw_gate'], 'L0_ffn_sw_up': _L0_ffn_in['sw_up'], 'L0_ffn_sw_down': _L0_ffn_in['sw_down'], 'L1_xattn_Wq': _L1_xattn_in['Wq'], 'L1_xattn_bq': _L1_xattn_in['bq'], 'L1_xattn_Wk': _L1_xattn_in['Wk'], 'L1_xattn_bk': _L1_xattn_in['bk'], 'L1_xattn_Wv': _L1_xattn_in['Wv'], 'L1_xattn_bv': _L1_xattn_in['bv'], 'L1_xattn_Wo': _L1_xattn_in['Wo'], 'L1_xattn_bo': _L1_xattn_in['bo'], 'L1_attn_Wq': _L1_attn_in['Wq'], 'L1_attn_bq': _L1_attn_in['bq'], 'L1_attn_Wk': _L1_attn_in['Wk'], 'L1_attn_bk': _L1_attn_in['bk'], 'L1_attn_Wv': _L1_attn_in['Wv'], 'L1_attn_bv': _L1_attn_in['bv'], 'L1_attn_Wo': _L1_attn_in['Wo'], 'L1_attn_bo': _L1_attn_in['bo'], 'L1_attn_g1': _L1_attn_in['g1'], 'L1_attn_be1': _L1_attn_in['be1'], 'L1_attn_W1': _L1_attn_in['W1'], 'L1_attn_b1': _L1_attn_in['b1'], 'L1_attn_W2': _L1_attn_in['W2'], 'L1_attn_b2': _L1_attn_in['b2'], 'L1_attn_g2': _L1_attn_in['g2'], 'L1_attn_be2': _L1_attn_in['be2'], 'L1_ffn_Wr': _L1_ffn_in['Wr'], 'L1_ffn_W1': _L1_ffn_in['W1'], 'L1_ffn_b1': _L1_ffn_in['b1'], 'L1_ffn_W2': _L1_ffn_in['W2'], 'L1_ffn_b2': _L1_ffn_in['b2']}

def reference(x, ctx_768, L0_xattn_Wq, L0_xattn_Wk, L0_xattn_Wv, L0_xattn_Wo, L0_xattn_bo, L0_attn_Wq, L0_attn_Wk, L0_attn_Wv, L0_attn_Wo, L0_ffn_router_w, L0_ffn_router_b, L0_ffn_w_gate, L0_ffn_w_up, L0_ffn_w_down, L0_ffn_sw_gate, L0_ffn_sw_up, L0_ffn_sw_down, L1_xattn_Wq, L1_xattn_bq, L1_xattn_Wk, L1_xattn_bk, L1_xattn_Wv, L1_xattn_bv, L1_xattn_Wo, L1_xattn_bo, L1_attn_Wq, L1_attn_bq, L1_attn_Wk, L1_attn_bk, L1_attn_Wv, L1_attn_bv, L1_attn_Wo, L1_attn_bo, L1_attn_g1, L1_attn_be1, L1_attn_W1, L1_attn_b1, L1_attn_W2, L1_attn_b2, L1_attn_g2, L1_attn_be2, L1_ffn_Wr, L1_ffn_W1, L1_ffn_b1, L1_ffn_W2, L1_ffn_b2):
    import jax
    import jax.numpy as jnp

    def _L0_xattn_ref(x, context, Wq, Wk, Wv, Wo, bo):
        import jax, jax.numpy as jnp
        import numpy as np
        H = 8
        D = 64
        SCALE = D ** (-0.5)
        B, Nq, _ = x.shape
        Nkv = context.shape[1]
        q = (x @ Wq).reshape(B, Nq, H, D)
        k = (context @ Wk).reshape(B, Nkv, H, D)
        v = (context @ Wv).reshape(B, Nkv, H, D)
        sim = jnp.einsum('bihd,bjhd->bhij', q, k) * SCALE
        attn = jax.nn.softmax(sim, axis=-1)
        out = jnp.einsum('bhij,bjhd->bihd', attn, v).reshape(B, Nq, H * D)
        return out @ Wo + bo

    def _L0_attn_ref(x, Wq, Wk, Wv, Wo):
        import jax, jax.numpy as jnp
        import numpy as np
        EMBED_DIM = 256
        NUM_HEADS = 16
        HEAD_DIM = EMBED_DIM // NUM_HEADS
        WINDOW_SIZE = 64
        SCALE = 1.0 / np.sqrt(HEAD_DIM)

        def _band_mask(T):
            i = jnp.arange(T)[:, None]
            j = jnp.arange(T)[None, :]
            full = j > i
            band = full & (j >= i - (WINDOW_SIZE - 1))
            return band
        B, T, C = x.shape
        H, D = (NUM_HEADS, HEAD_DIM)
        q = jnp.einsum('btc,oc->bto', x, Wq).reshape(B, T, H, D)
        k = jnp.einsum('btc,oc->bto', x, Wk).reshape(B, T, H, D)
        v = jnp.einsum('btc,oc->bto', x, Wv).reshape(B, T, H, D)
        att = jnp.einsum('bqhd,bkhd->bhqk', q, k) * SCALE
        mask = _band_mask(T)
        att = jnp.where(mask[None, None, :, :], -jnp.inf, att)
        att = jax.nn.softmax(att, axis=-1)
        out = jnp.einsum('bhqk,bkhd->bqhd', att, v).reshape(B, T, C)
        return jnp.einsum('btc,oc->bto', out, Wo)

    def _L0_ffn_ref(x, router_w, router_b, w_gate, w_up, w_down, sw_gate, sw_up, sw_down):
        import jax, jax.numpy as jnp
        import numpy as np
        B, S, D = (1, 512, 256)
        F = 352
        E = 16
        K = 2
        CAP_FACTOR = 1.25

        def _mlp(h, wg, wu, wd):
            return jax.nn.silu(h @ wg) * (h @ wu) @ wd
        b, s, d = x.shape
        N = b * s
        NK = N * K
        C = int(np.ceil(CAP_FACTOR * NK / E))
        x_tokens = x.reshape(N, d)
        logits = x_tokens @ router_w + router_b
        probs = jax.nn.softmax(logits, axis=-1)
        vals, idx = jax.lax.top_k(probs, K)
        vals = vals / (jnp.sum(vals, axis=-1, keepdims=True) + 1e-09)
        idx_flat = idx.reshape(NK)
        vals_flat = vals.reshape(NK)
        oh_e = jax.nn.one_hot(idx_flat, E, dtype=x.dtype)
        pos = (jnp.cumsum(oh_e, axis=0) * oh_e).sum(axis=1) - 1
        within = (pos < C).astype(x.dtype)
        pos_c = jnp.clip(pos, 0, C - 1).astype(jnp.int32)
        token_ids = jnp.arange(NK) // K
        x_pair = x_tokens[token_ids] * within[:, None]
        expert_inputs = jnp.zeros((E, C, d), x.dtype).at[idx_flat, pos_c].add(x_pair)
        expert_outputs = jax.vmap(_mlp)(expert_inputs, w_gate, w_up, w_down)
        gathered = expert_outputs[idx_flat, pos_c] * (vals_flat * within)[:, None]
        output_tokens = gathered.reshape(N, K, d).sum(axis=1)
        return x + _mlp(x, sw_gate, sw_up, sw_down) + output_tokens.reshape(b, s, d)

    def _L1_xattn_ref(query, key, value, Wq, bq, Wk, bk, Wv, bv, Wo, bo):
        import jax, jax.numpy as jnp
        import numpy as np
        QUERY_DIM = 256
        KEY_DIM = 192
        NUM_HEADS = 16
        HEAD_DIM = QUERY_DIM // NUM_HEADS
        SCALE = HEAD_DIM ** (-0.5)
        B, Nq, _ = query.shape
        Nk = key.shape[1]
        q = (query @ Wq + bq).reshape(B, Nq, NUM_HEADS, HEAD_DIM).transpose(0, 2, 1, 3)
        k = (key @ Wk + bk).reshape(B, Nk, NUM_HEADS, HEAD_DIM).transpose(0, 2, 1, 3)
        v = (value @ Wv + bv).reshape(B, Nk, NUM_HEADS, HEAD_DIM).transpose(0, 2, 1, 3)
        attn = jnp.einsum('bhqd,bhkd->bhqk', q, k) * SCALE
        attn = jax.nn.softmax(attn, axis=-1)
        out = jnp.einsum('bhqk,bhkd->bhqd', attn, v)
        out = out.transpose(0, 2, 1, 3).reshape(B, Nq, QUERY_DIM)
        return out @ Wo + bo

    def _L1_attn_ref(x, Wq, bq, Wk, bk, Wv, bv, Wo, bo, g1, be1, W1, b1, W2, b2, g2, be2):
        import math
        import jax, jax.numpy as jnp
        import numpy as np
        H = 256
        NH = 16
        HD = H // NH
        FF = 1024
        EPS = 1e-12

        def _lin(key, fan_in, fan_out):
            k1, k2 = jax.random.split(key)
            bound = 1.0 / math.sqrt(fan_in)
            W = jax.random.uniform(k1, (fan_in, fan_out), jnp.float32, -bound, bound)
            b = jax.random.uniform(k2, (fan_out,), jnp.float32, -bound, bound)
            return (W, b)

        def _layernorm(x, g, b):
            mu = jnp.mean(x, axis=-1, keepdims=True)
            var = jnp.mean((x - mu) ** 2, axis=-1, keepdims=True)
            return (x - mu) * jax.lax.rsqrt(var + EPS) * g + b

        def _gelu(x):
            return x * 0.5 * (1.0 + jax.lax.erf(x / jnp.sqrt(jnp.float32(2.0))))
        B, S, _ = x.shape

        def heads(W, b):
            return (x @ W + b).reshape(B, S, NH, HD).transpose(0, 2, 1, 3)
        q, k, v = (heads(Wq, bq), heads(Wk, bk), heads(Wv, bv))
        eq = jax.nn.elu(q)
        ek = jax.nn.elu(k)
        qn = eq / jnp.linalg.norm(eq, axis=-1, keepdims=True)
        kn = ek / jnp.linalg.norm(ek, axis=-1, keepdims=True)
        kv = jnp.einsum('bhsd,bhse->bhde', kn, v)
        ctx = jnp.einsum('bhsd,bhde->bhse', qn, kv) / jnp.float32(math.sqrt(HD))
        ctx = ctx.transpose(0, 2, 1, 3).reshape(B, S, H)
        attn_out = _layernorm(ctx @ Wo + bo + x, g1, be1)
        h = _gelu(attn_out @ W1 + b1)
        out = _layernorm(h @ W2 + b2 + attn_out, g2, be2)
        return out

    def _L1_ffn_ref(x, Wr, W1, b1, W2, b2):
        import jax, jax.numpy as jnp
        import numpy as np
        from math import ceil
        CAPACITY_FACTOR = 2.0
        MIN_CAPACITY = 4
        B, S, D = x.shape
        E = Wr.shape[1]
        N = B * S
        k = max(MIN_CAPACITY, ceil(N * CAPACITY_FACTOR / E))
        xt = x.reshape(N, D)
        scores = jax.nn.softmax(xt @ Wr, axis=-1)
        G, idx = jax.lax.top_k(scores.T, k)
        X_in = xt[idx]
        h = jax.nn.gelu(jnp.einsum('ekd,edh->ekh', X_in, W1) + b1[:, None, :], approximate=False)
        X_e = jnp.einsum('ekh,ehd->ekd', h, W2) + b2[:, None, :]
        contrib = (G[..., None] * X_e).reshape(E * k, D)
        out = jnp.zeros((N, D), dtype=x.dtype).at[idx.reshape(-1)].add(contrib)
        return out.reshape(B, S, D)
    x = x + _L0_xattn_ref(_layernorm(x, axis=-1), ctx_768, L0_xattn_Wq, L0_xattn_Wk, L0_xattn_Wv, L0_xattn_Wo, L0_xattn_bo)
    x = x + _L0_attn_ref(_layernorm(x, axis=-1), L0_attn_Wq, L0_attn_Wk, L0_attn_Wv, L0_attn_Wo)
    x = x + _L0_ffn_ref(_layernorm(x, axis=-1), L0_ffn_router_w, L0_ffn_router_b, L0_ffn_w_gate, L0_ffn_w_up, L0_ffn_w_down, L0_ffn_sw_gate, L0_ffn_sw_up, L0_ffn_sw_down)
    x = x + _L1_xattn_ref(_layernorm(x, axis=-1), ctx_768, ctx_768, L1_xattn_Wq, L1_xattn_bq, L1_xattn_Wk, L1_xattn_bk, L1_xattn_Wv, L1_xattn_bv, L1_xattn_Wo, L1_xattn_bo)
    x = x + _L1_attn_ref(_layernorm(x, axis=-1), L1_attn_Wq, L1_attn_bq, L1_attn_Wk, L1_attn_bk, L1_attn_Wv, L1_attn_bv, L1_attn_Wo, L1_attn_bo, L1_attn_g1, L1_attn_be1, L1_attn_W1, L1_attn_b1, L1_attn_W2, L1_attn_b2, L1_attn_g2, L1_attn_be2)
    x = x + _L1_ffn_ref(_layernorm(x, axis=-1), L1_ffn_Wr, L1_ffn_W1, L1_ffn_b1, L1_ffn_W2, L1_ffn_b2)
    return x

_drawn_inputs = setup_inputs


def setup_inputs(seed=0):
    import zlib

    import numpy as np

    out = dict(_drawn_inputs(seed))
    spreads = {'L0_xattn_bo': (0.0, 0.1),
     'L0_ffn_router_b': (0.0, 0.8),
     'L1_xattn_bq': (0.0, 2.0),
     'L1_xattn_bk': (0.0, 2.0),
     'L1_xattn_bv': (0.0, 0.756),
     'L1_xattn_bo': (0.0, 0.764),
     'L1_attn_g1': (1.0, 0.6),
     'L1_attn_be1': (0.0, 0.8),
     'L1_attn_g2': (1.0, 0.6),
     'L1_attn_be2': (0.0, 0.8),
     'L1_ffn_b1': (0.0, 2.0),
     'L1_ffn_b2': (0.0, 2.0)}
    factors = {'L0_attn_Wq': 3.219,
     'L0_attn_Wk': 2.766,
     'L0_ffn_router_w': 8.0,
     'L0_ffn_w_gate': 8.0,
     'L0_ffn_w_up': 8.0,
     'L0_ffn_w_down': 8.0,
     'L0_ffn_sw_gate': 5.301,
     'L0_ffn_sw_up': 5.261,
     'L0_ffn_sw_down': 4.518,
     'L1_attn_bq': 36.038,
     'L1_attn_bo': 18.709,
     'L1_attn_b1': 54.697,
     'L1_attn_b2': 100.576,
     'L1_attn_bk': 8.0,
     'L1_attn_bv': 8.0,
     'L1_attn_W1': 3.215,
     'L1_attn_W2': 2.847}
    for name, (base, spread) in spreads.items():
        noise = np.random.default_rng([zlib.crc32(name.encode()), seed]).standard_normal(out[name].shape)
        drawn = base * np.exp(spread * noise) if base else spread * noise
        out[name] = jnp.asarray(drawn.astype(out[name].dtype))
    for name, factor in factors.items():
        out[name] = (out[name] * factor).astype(out[name].dtype)
    return out
```

```python
from contextlib import ExitStack

import numpy as np

import concourse.bass as bass
from concourse import mybir

F32 = mybir.dt.float32
F32R = mybir.dt.float32r
U32 = mybir.dt.uint32
ALU = mybir.AluOpType
ACT = mybir.ActivationFunctionType
AX = mybir.AxisListType.X

P = 128
D = 256
DK = 2
C = 192
CB = C - P
S = 12544
TILES = S // P
GT = 2
GROUPS = TILES // GT
GK = GT * P
VW = C + 2
RAW = 2 * GK + GT * VW
RAW_KD = 2 * GK
HEADS = (8, 16)
HD = (64, 16)
SLOTS = 2
F0 = 352
F0T = 3
E0 = 16
CAP = 20
W0 = 4 * F0T * P + F0T * D
F1T = 8
E1 = 8
TOPK = 32
W1 = DK * F1T * P + F1T * D + F1T
QS = P + P + CB + 1
LOWEST = -3.0e38


def xq_offsets(layer):
    inner = HEADS[layer] * HD[layer]
    nb = inner // P
    at, o = {}, 0
    for name, n in (("wq", DK * inner), ("wk", nb * QS), ("wva", inner), ("wvb", inner), ("wo", nb * D), ("bo", D),
                    ("bv", D * layer), ("bq", nb * layer)):
        at[name] = o
        o += n
    return at, o


XQ0, XQ0W = xq_offsets(0)
XQ1, XQ1W = xq_offsets(1)
CONST = {"ident": 0, "before": 128, "causal": 256, "mask2": 384, "mask8": 386, "iota": 394, "rb": 410, "rw": 426}
CONSTW = 426 + DK * E0
LA = {"wq": 0, "wk": 512, "wv": 1024, "wo": 1536}
LB = {"wq": 0, "wk": 512, "wv": 1024, "wo": 1536, "wr": 2048, "bqk": 2064, "bv": 2576, "bo": 2832,
      "g1": 3088, "be1": 3344, "b2": 3600, "g2": 3856, "be2": 4112, "b1": 4368}
LBW = 4376
FFW = DK * 1024 + F1T * D


def perceiver(nc, x_in, ctx_in, xq0_in, xq1_in, const_in, la_in, lb_in, ff_in, ex0_in, ex1_in, b2_in, out):
    with ExitStack() as stack:
        def sb(name, shape, dt=F32):
            return stack.enter_context(nc.sbuf_tensor(name, shape, dt))

        names = {}

        def sem(name):
            if name not in names:
                names[name] = stack.enter_context(nc.semaphore(name))
            return names[name]

        ps = stack.enter_context(nc.psum_tensor("ps", [P, 8, 512], F32))
        raw = [sb(f"raw{s}", [P, RAW]) for s in range(SLOTS)]
        t_ha = [sb(f"t_ha{s}", [P, GK], F32R) for s in range(SLOTS)]
        t_la = [sb(f"t_la{s}", [P, GK], F32R) for s in range(SLOTS)]
        t_b = [sb(f"t_b{s}", [P, GK], F32R) for s in range(SLOTS)]
        t_e = [sb(f"t_e{s}", [CB + 1, GK], F32R) for s in range(SLOTS)]
        q_ha = sb("q_ha", [P, 2048], F32R)
        q_la = sb("q_la", [P, 2048], F32R)
        q_b = sb("q_b", [P, 2048], F32R)
        q_he = sb("q_he", [CB + 1, 2048], F32R)
        q_le = sb("q_le", [CB + 1, 2048], F32R)
        probs = sb("probs", [P, W1])
        wide = sb("wide", [P, W1])
        run = wide[:, 0:2048]
        scr = wide[:, 2048:4096]
        ring = sb("ring", [P, 4 * W0])
        wa = sb("wa", [P, XQ0W])
        wx1 = sb("wx1", [P, XQ1W])
        cst = sb("cst", [P, CONSTW])
        wlb = sb("wlb", [P, LBW])
        wv_ha = sb("wv_ha", [P, D], F32R)
        wv_la = sb("wv_la", [P, D], F32R)
        wv_hb = sb("wv_hb", [P, D], F32R)
        wv_lb = sb("wv_lb", [CB, D], F32R)
        v_sb = [sb(f"v_sb{i}", [P, 16, 32]) for i in range(2)]
        x = sb("x", [P, D])
        xn = sb("xn", [P, D])
        xt = sb("xt", [P, D])
        ya = sb("ya", [P, D])
        yb = sb("yb", [P, D])
        qt = sb("qt", [P, 512])
        stat = sb("stat", [P, 8, 12])
        sm = sb("sm", [P, 256])
        idx = sb("idx", [P, 8], U32)
        b2 = sb("b2", [E1, D])
        m_t = sb("m_t", [16, P])
        sel = sb("sel", [E1, 4 * P])

        ident = cst[:, 0:128]
        block = stack.enter_context(nc.Block())

        wq = (wa, wx1)
        XQ = (XQ0, XQ1)

        def chain(eng, name):
            count = [0]

            def link(ins):
                count[0] += 1
                ins.then_inc(sem(name), 1)
                eng.wait_ge(sem(name), count[0])
            return link

        def ctx_count(phase, slot, g):
            per_phase = (GROUPS + 1) // 2 if slot == 0 else GROUPS // 2
            return 16 * (phase * per_phase + 1) + 8 * (g - slot)

        def groups(eng, body):
            body(0, 0, True)
            body(1, 1, True)
            with eng.Fori(1, GROUPS // 2) as i:
                body(2 * i, 0, False)
                body(2 * i + 1, 1, False)
            body(GROUPS - 1, 0, False)

        @block.sync
        def _(sp):
            sp.dma_start(x[:], x_in).then_inc(sem("x_loaded"), 16)
            sp.dma_start(cst[:], const_in).then_inc(sem("const_loaded"), 16)
            sp.dma_start(wa[:], xq0_in).then_inc(sem("xq0_loaded"), 16)
            for layer in range(2):
                units1 = HEADS[layer] // 8
                units2 = HEADS[layer] // 4

                def load_hi(g, slot, first):
                    if not first:
                        sp.wait_ge(sem(f"hi{layer}"), g - 1)
                    sp.dma_start(raw[slot][:, 0:2 * GK], ctx_in[g, :, 0:2 * GK]).then_inc(sem(f"ctx{slot}"), 16)

                def load_all(g, slot, first):
                    if not first:
                        sp.wait_ge(sem(f"split{layer}"), g - 1)
                        sp.wait_ge(sem(f"pv{layer}"), (g - 1) * GT * units2)
                    sp.dma_start(raw[slot][:], ctx_in[g]).then_inc(sem(f"ctx{slot}"), 16)

                if layer == 1:
                    sp.wait_ge(sem("pv0"), TILES * (HEADS[0] // 4))
                groups(sp, load_hi)
                sp.wait_ge(sem(f"hi{layer}"), GROUPS)
                load_all(0, 0, True)
                load_all(1, 1, True)
                sp.wait_ge(sem("max_t"), layer + 1)
                sp.dma_start(scr[CB:CB + 1, 0:HEADS[layer] * P], m_t[0:HEADS[layer], :]).then_inc(sem("max_row"), 16)
                with sp.Fori(1, GROUPS // 2) as i:
                    load_all(2 * i, 0, False)
                    load_all(2 * i + 1, 1, False)
                load_all(GROUPS - 1, 0, False)
            sp.wait_ge(sem("result"), 1)
            sp.dma_start(out, x[:]).then_inc(sem("stored"), 16)
            sp.wait_ge(sem("stored"), 16)

        @block.gpsimd
        def _(pool):
            pool.dma_start(wlb[:, 0:2048], la_in).then_inc(sem("la_loaded"), 16)
            pool.dma_start(wx1[:], xq1_in).then_inc(sem("xq1_loaded"), 16)
            pool.dma_start(b2[:], b2_in).then_inc(sem("b2_loaded"), 16)

            def load0(e, slot):
                pool.dma_start(ring[:, slot * W0:(slot + 1) * W0], ex0_in[e]).then_inc(sem(f"ring{slot}"), 16)

            for e in range(4):
                load0(e, e)
            pool.wait_ge(sem("x_done"), 1)
            pool.dma_start(wa[:, 0:FFW], ff_in).then_inc(sem("ff_loaded"), 16)
            pool.wait_ge(sem("x_done"), 2)
            pool.dma_start(wlb[:], lb_in).then_inc(sem("lb_loaded"), 16)
            with pool.Fori(0, 3) as i:
                for k in range(4):
                    pool.wait_ge(sem("down0"), 4 * i + k + 1)
                    load0(4 * i + k + 4, k)
            pool.wait_ge(sem("down0"), 13)
            load0(16, 0)
            pool.wait_ge(sem("down0"), E0 + 1)
            pool.dma_start(ring[:, 0:W1], ex1_in[0]).then_inc(sem("big0"), 16)
            pool.dma_start(ring[:, W1:2 * W1], ex1_in[1]).then_inc(sem("big1"), 16)
            pool.wait_ge(sem("x_done"), 4)
            pool.dma_start(probs[:], ex1_in[2]).then_inc(sem("big2"), 16)
            pool.dma_start(wide[:], ex1_in[3]).then_inc(sem("big3"), 16)
            big = (ring[:, 0:W1], ring[:, W1:2 * W1], probs[:], wide[:])
            for e in range(4, E1):
                pool.wait_ge(sem("down1"), e - 3)
                pool.dma_start(big[e % 4], ex1_in[e]).then_inc(sem(f"big{e % 4}"), 16)

        @block.scalar
        def _(act):
            def root(n):
                act.wait_ge(sem("var"), n + 1)
                act.activation(stat[:, n, 9:10], stat[:, n, 8:9], ACT.Sqrt).then_inc(sem("std"), 1)

            def cross(layer):
                units1 = HEADS[layer] // 8
                units2 = HEADS[layer] // 4
                root(3 * layer)

                def round_hi(g, slot, first):
                    act.wait_ge(sem(f"ctx{slot}"), ctx_count(2 * layer, slot, g))
                    if not first:
                        act.wait_ge(sem(f"s1_{layer}"), (g - 1) * GT * units1)
                    act.copy(t_ha[slot][:], raw[slot][:, 0:GK])
                    act.copy(t_e[slot][0:CB, :], raw[slot][0:CB, GK:2 * GK]).then_inc(sem(f"hi{layer}"), 1)

                def exps(g, slot, first):
                    for j in range(GT):
                        for u in range(units2):
                            n = (g * GT + j) * units2 + u
                            act.wait_ge(sem(f"s2_{layer}"), n + 1)
                            if not first:
                                act.wait_ge(sem(f"pv{layer}"), n + 1 - 2 * units2)
                            act.activation(probs[:, j * 2048 + u * 512:j * 2048 + (u + 1) * 512], ps[:, u % 2, :],
                                           ACT.Exp).then_inc(sem(f"exp{layer}"), 1)

                def exps_pair(g, slot, first):
                    exps(g, slot, first and slot == 0)

                if layer == 1:
                    act.wait_ge(sem("pv0"), TILES * (HEADS[0] // 4))
                groups(act, round_hi)
                groups(act, exps_pair)

            cross(0)
            root(1)
            act.wait_ge(sem("logit_a"), 1)
            act.activation(run, run, ACT.Exp).then_inc(sem("prob_a"), 1)
            act.wait_ge(sem("pt_psum"), 1)
            act.copy(scr[:, 1024:2048], ps[:, 4:6, :]).then_inc(sem("pt_hi"), 1)
            root(2)
            act.wait_ge(sem("logit_r"), 1)
            act.activation(sm[:, 16:32], sm[:, 0:16], ACT.Exp).then_inc(sem("prob_r"), 1)

            def silu(e, par):
                act.wait_ge(sem("up0"), e + 1)
                if not (isinstance(e, int) and e < 2):
                    act.wait_ge(sem("hid0"), e - 1)
                act.activation(probs[:, par * 1024:par * 1024 + 384], ps[:, par, 0:384], ACT.Silu)\
                   .then_inc(sem("silu"), 1)

            for e in range(5):
                silu(e, e % 2)
            with act.Fori(1, 4) as i:
                for k in range(1, 5):
                    silu(4 * i + k, k % 2)

            cross(1)
            root(4)
            act.wait_ge(sem("elu_in"), 1)
            act.activation(raw[1][:, 0:512], raw[1][:, 0:512], ACT.Exp).then_inc(sem("elu_exp"), 1)
            act.wait_ge(sem("norm_in"), 1)
            act.activation(sm[:, 32:64], sm[:, 0:32], ACT.Sqrt).then_inc(sem("norm_out"), 1)
            root(5)
            act.wait_ge(sem("ff_up"), 1)
            for m in range(F1T):
                last = act.activation(raw[m // 4][:, (m % 4) * P:(m % 4 + 1) * P],
                                      ps[:, m // 4, (m % 4) * P:(m % 4 + 1) * P], ACT.Gelu,
                                      bias=wlb[:, LB["b1"] + m:LB["b1"] + m + 1])
            last.then_inc(sem("ff_hid"), 1)
            root(6)
            root(7)
            act.wait_ge(sem("logit_r"), 2)
            act.activation(sm[:, 16:24], sm[:, 0:8], ACT.Exp).then_inc(sem("prob_r"), 1)
            big = (ring[:, 0:W1], ring[:, W1:2 * W1], probs[:], wide[:])
            for e in range(E1):
                act.wait_ge(sem("up1"), e + 1)
                if e >= 2:
                    act.wait_ge(sem("down1"), e - 1)
                for m in range(F1T):
                    last = act.activation(wa[:, (e % 2) * 1024 + m * P:(e % 2) * 1024 + (m + 1) * P],
                                          ps[:, 2 * (e % 2) + m // 4, (m % 4) * P:(m % 4 + 1) * P], ACT.Gelu,
                                          bias=big[e % 4][:, W1 - F1T + m:W1 - F1T + m + 1])
                last.then_inc(sem("gelu1"), 1)

        @block.tensor
        def _(pe):
            def turn_x(n, k, src):
                pe.wait_ge(sem("xn"), n + 1)
                pe.transpose(ps[:, 7, 0:128], src[:, 0:128], ident)
                pe.transpose(ps[:, 7, 128:256], src[:, 128:256], ident).then_inc(sem("xt_psum"), 1)
                pe.wait_ge(sem("xt"), k + 1)

            def mm(o, l, r, k, n, **more):
                return pe.matmul(o, l, r, start=(k == 0), stop=(k == n - 1), **more)

            def cross(layer):
                heads = HEADS[layer]
                units1 = heads // 8
                units2 = heads // 4
                w, at = wq[layer], XQ[layer]
                inner = heads * HD[layer]
                nb = inner // P
                width = 2048 * layer + 1024 * (1 - layer)
                turn_x(3 * layer, 3 * layer, xn)
                pe.wait_ge(sem(f"xq{layer}_loaded"), 16)
                for b in range(nb):
                    for k in range(DK):
                        c = at["wq"] + k * inner + b * P
                        last = mm(ps[:, 0, b * P:(b + 1) * P], w[:, c:c + P], xt[:, k * P:(k + 1) * P], k, DK)
                last.then_inc(sem("q_psum"), 1)
                pe.wait_ge(sem("q_diag"), layer + 1)
                done = 2 * layer
                for c in range(width // 512):
                    if done + c >= 2 and c >= 2:
                        pe.wait_ge(sem("q_chunk"), done + c - 1)
                    per = width // nb
                    for part, (o, m) in enumerate(((0, P), (P, P), (2 * P, CB + 1))):
                        bank = 1 + 3 * (c % 2) + part
                        for b in range(c * 512 // per, ((c + 1) * 512 - 1) // per + 1):
                            lo, hi = max(b * per, c * 512), min((b + 1) * per, (c + 1) * 512)
                            last = mm(ps[0:m, bank, lo - c * 512:hi - c * 512],
                                      w[:, at["wk"] + b * QS + o:at["wk"] + b * QS + o + m], scr[:, lo:hi], 0, 1)
                    last.then_inc(sem("q_folded"), 1)
                pe.wait_ge(sem("q_chunk"), done + width // 512)

                def scores1(g, slot, first):
                    pe.wait_ge(sem(f"hi{layer}"), g + 1)
                    for j in range(GT):
                        for u in range(units1):
                            n = (g * GT + j) * units1 + u
                            if not (first and slot == 0 and j * units1 + u < 2):
                                pe.wait_ge(sem(f"run{layer}"), n - 1)
                            b = 2 * ((j * units1 + u) % 2)
                            ks = slice(j * P, (j + 1) * P)
                            for h in range(2):
                                cs = slice(u * 1024 + h * 512, u * 1024 + (h + 1) * 512)
                                mm(ps[:, b + h, :], t_ha[slot][:, ks], q_ha[:, cs], 0, 2)
                                last = mm(ps[:, b + h, :], t_e[slot][:, ks], q_he[:, cs], 1, 2)
                            last.then_inc(sem(f"s1_{layer}"), 1)

                groups(pe, scores1)
                pe.wait_ge(sem(f"run{layer}"), TILES * units1)
                for h in range(heads):
                    last = pe.transpose(ps[:, 4 + h // 4, (h % 4) * P:(h % 4 + 1) * P], run[:, h * P:(h + 1) * P], ident)
                last.then_inc(sem("lanes_t"), 1)
                pe.wait_ge(sem("max_q"), layer + 1)
                pe.transpose(ps[0:heads, 2, 0:P], sm[:, 0:heads], ident).then_inc(sem("max_psum"), 1)
                pe.wait_ge(sem("shift"), layer + 1)

                def values(t, j, slot, skip):
                    if not skip:
                        pe.wait_ge(sem("v_sb"), t - 1)
                    ks = slice(j * P, (j + 1) * P)
                    o = ps[:, 2 + j, 0:D]
                    mm(o, t_ha[slot][:, ks], wv_ha[:], 0, 5)
                    mm(o, t_ha[slot][:, ks], wv_la[:], 1, 5)
                    mm(o, t_la[slot][:, ks], wv_ha[:], 2, 5)
                    mm(o, t_b[slot][:, ks], wv_hb[:], 3, 5)
                    mm(o, t_b[slot][0:CB, ks], wv_lb[:], 4, 5).then_inc(sem("v_psum"), 1)

                def scores2(t, j, slot, u, skip):
                    n = t * units2 + u
                    if not skip:
                        pe.wait_ge(sem(f"exp{layer}"), n - 1)
                    ks = slice(j * P, (j + 1) * P)
                    cs = slice(u * 512, (u + 1) * 512)
                    o = ps[:, u % 2, :]
                    mm(o, t_ha[slot][:, ks], q_ha[:, cs], 0, 5)
                    mm(o, t_ha[slot][:, ks], q_la[:, cs], 1, 5)
                    mm(o, t_la[slot][:, ks], q_ha[:, cs], 2, 5)
                    mm(o, t_b[slot][:, ks], q_b[:, cs], 3, 5)
                    mm(o, t_e[slot][:, ks], q_le[:, cs], 4, 5).then_inc(sem(f"s2_{layer}"), 1)

                def products(t, j, slot, u, start, stop):
                    pe.wait_ge(sem(f"exp{layer}"), t * units2 + u + 1)
                    if layer == 1 and u == 0:
                        pe.wait_ge(sem("v_sb"), t + 1)
                    for k in range(4):
                        h = 4 * u + k
                        e = probs[:, j * 2048 + h * P:j * 2048 + (h + 1) * P]
                        if layer == 0:
                            last = pe.matmul(ps[:, 4 + h // 2, (h % 2) * 256:(h % 2) * 256 + C + 1], e,
                                             raw[slot][:, RAW_KD + j * VW:RAW_KD + j * VW + C + 1],
                                             start=(start and h % 2 == 0), stop=stop, skip_group_check=True)
                        else:
                            last = pe.matmul(ps[32 * k:32 * k + 32, 4, u * P:(u + 1) * P], v_sb[j][:, h, :], e,
                                             start=(start and u == 0), stop=stop, skip_group_check=True)
                    last.then_inc(sem(f"pv{layer}"), 1)

                def step(g, slot, j, first=False, last=False):
                    t = g * GT + j
                    ns, nj = (slot, 1) if j == 0 else (1 - slot, 0)
                    if j == 1 and not last:
                        pe.wait_ge(sem(f"split{layer}"), g + 2)
                    if layer == 1 and not last:
                        values(t + 1, nj, ns, first and slot == 0 and j == 0)
                    for u in range(units2):
                        if not last:
                            scores2(t + 1, nj, ns, u, False)
                        products(t, j, slot, u, first and slot == 0 and j == 0, last)

                def pair(g, slot, first):
                    step(g, slot, 0, first)
                    step(g, slot, 1, first)

                pe.wait_ge(sem(f"split{layer}"), 1)
                if layer == 1:
                    values(0, 0, 0, True)
                for u in range(units2):
                    scores2(0, 0, 0, u, u < 2)
                pair(0, 0, True)
                pair(1, 1, True)
                with pe.Fori(1, GROUPS // 2) as i:
                    pair(2 * i, 0, False)
                    pair(2 * i + 1, 1, False)
                step(GROUPS - 1, 0, 0)
                step(GROUPS - 1, 0, 1, last=True)

            cross(0)
            pe.wait_ge(sem("u_sb"), 1)
            for h in range(8):
                pe.transpose(ps[:, h // 4, (h % 4) * P:(h % 4 + 1) * P], probs[:, h * C:h * C + P], ident)
                last = pe.transpose(ps[0:CB, 2 + h // 4, (h % 4) * P:(h % 4 + 1) * P],
                                    probs[:, h * C + P:(h + 1) * C], ident)
            last.then_inc(sem("ut_psum"), 1)
            pe.wait_ge(sem("ut"), 1)
            for h in range(8):
                o = ps[64 * (h % 2):64 * (h % 2) + 64, 4, (h // 2) * P:(h // 2 + 1) * P]
                a, b = XQ0["wva"] + h * 64, XQ0["wvb"] + h * 64
                pe.matmul(o, wa[:, a:a + 64], probs[:, 1536 + h * P:1536 + (h + 1) * P], start=True, stop=False)
                last = pe.matmul(o, wa[0:CB, b:b + 64], probs[0:CB, 2560 + h * P:2560 + (h + 1) * P],
                                 start=False, stop=True)
            last.then_inc(sem("ot_psum"), 1)
            pe.wait_ge(sem("ot"), 1)
            for b in range(4):
                last = mm(ps[:, 5, 0:D], qt[:, b * P:(b + 1) * P], wa[:, XQ0["wo"] + b * D:XQ0["wo"] + (b + 1) * D], b, 4)
            last.then_inc(sem("y"), 1)

            turn_x(1, 1, xn)
            pe.wait_ge(sem("la_loaded"), 16)
            for i, name in enumerate(("wq", "wk")):
                for b in range(2):
                    for k in range(DK):
                        c = LA[name] + k * D + b * P
                        mm(ps[:, 0, i * D + b * P:i * D + (b + 1) * P], wlb[:, c:c + P], xt[:, k * P:(k + 1) * P], k, DK)
            for k in range(DK):
                last = mm(ps[:, 1, 0:D], xt[:, k * P:(k + 1) * P], wlb[:, LA["wv"] + k * D:LA["wv"] + (k + 1) * D], k, DK)
            last.then_inc(sem("qkv_psum"), 1)
            pe.wait_ge(sem("k_diag"), 1)
            for c in range(4):
                last = mm(ps[:, 2 + c, :], qt[:, (c // 2) * P:(c // 2 + 1) * P], probs[:, c * 512:(c + 1) * 512], 0, 1)
            last.then_inc(sem("s_a"), 1)
            pe.wait_ge(sem("prob_a"), 1)
            for h in range(16):
                last = pe.transpose(ps[:, 2 + h // 4, (h % 4) * P:(h % 4 + 1) * P], run[:, h * P:(h + 1) * P], ident)
            last.then_inc(sem("pt_psum"), 1)
            pe.wait_ge(sem("pt_lo"), 1)
            pe.wait_ge(sem("pt_hi"), 1)
            for h in range(16):
                last = mm(ps[:, 6, h * 16:(h + 1) * 16], scr[:, h * P:(h + 1) * P], ya[:, h * 16:(h + 1) * 16], 0, 1)
            last.then_inc(sem("o_a"), 1)

            def project(n, src, w, at):
                pe.wait_ge(sem("head_out"), n + 1)
                pe.transpose(ps[:, 7, 0:128], src[:, 0:128], ident)
                pe.transpose(ps[:, 7, 128:256], src[:, 128:256], ident).then_inc(sem("head_t_psum"), 1)
                pe.wait_ge(sem("head_t"), n + 1)
                for k in range(DK):
                    last = mm(ps[:, 5, 0:D], xt[:, k * P:(k + 1) * P], w[:, at + k * D:at + (k + 1) * D], k, DK)
                last.then_inc(sem("y"), 1)

            project(0, yb, wlb, LA["wo"])

            turn_x(2, 2, xn)
            for k in range(DK):
                last = mm(ps[:, 6, 0:E0], xt[:, k * P:(k + 1) * P], cst[:, CONST["rw"] + k * E0:CONST["rw"] + (k + 1) * E0], k, DK)
            last.then_inc(sem("router"), 1)

            def up0(e, slot, par):
                first = isinstance(e, int)
                pe.wait_ge(sem(f"ring{slot}"), 16 * (e // 4 + 1) if first else 4 * (e - slot) + 16)
                if not (first and e < 2):
                    pe.wait_ge(sem("hid0"), e - 1)
                w = ring[:, slot * W0:(slot + 1) * W0]
                for i in range(2):
                    for m in range(F0T):
                        for k in range(DK):
                            c = (i * DK + k) * F0T * P + m * P
                            last = mm(ps[:, 2 * i + par, m * P:(m + 1) * P], w[:, c:c + P], xt[:, k * P:(k + 1) * P], k, DK)
                last.then_inc(sem("up0"), 1)

            def down0(e, slot, par):
                pe.wait_ge(sem("hid0"), e + 1)
                if not (isinstance(e, int) and e < 2):
                    pe.wait_ge(sem("acc0"), e - 1)
                w = ring[:, slot * W0 + 4 * F0T * P:(slot + 1) * W0]
                for m in range(F0T):
                    last = mm(ps[:, 4 + par, 0:D], probs[:, 2048 + par * 1024 + m * P:2048 + par * 1024 + (m + 1) * P],
                              w[:, m * D:(m + 1) * D], m, F0T)
                last.then_inc(sem("down0"), 1)

            up0(0, 0, 0)
            pe.wait_ge(sem("chosen"), 1)
            pe.matmul(ps[:, 6, 32:32 + E0], cst[:, CONST["before"]:CONST["before"] + P], sm[:, 64:64 + E0],
                      start=True, stop=True).then_inc(sem("rank"), 1)
            for e in range(1, 5):
                up0(e, e % 4, e % 2)
                down0(e - 1, (e - 1) % 4, (e - 1) % 2)
            with pe.Fori(1, 4) as i:
                for k in range(1, 5):
                    up0(4 * i + k, k % 4, k % 2)
                    down0(4 * i + k - 1, (k - 1) % 4, (k - 1) % 2)
            down0(E0, 0, 0)

            pe.wait_ge(sem("v_ready"), 1)
            cross(1)
            pe.wait_ge(sem("o_sb"), 1)
            for u in range(4):
                last = pe.transpose(ps[:, 5, u * P:(u + 1) * P], qt[:, u * P:(u + 1) * P], ident)
            last.then_inc(sem("o_t"), 1)
            project(1, yb, wx1, XQ1["wo"])

            turn_x(4, 4, xn)
            pe.wait_ge(sem("lb_loaded"), 16)
            for i, name in enumerate(("wq", "wk", "wv")):
                for k in range(DK):
                    last = mm(ps[:, i // 2, (i % 2) * D:(i % 2) * D + D], xt[:, k * P:(k + 1) * P],
                              wlb[:, LB[name] + k * D:LB[name] + (k + 1) * D], k, DK)
            last.then_inc(sem("qkv_psum"), 1)
            pe.wait_ge(sem("unit_qk"), 1)
            for b in range(2):
                mm(ps[:, 2, b * P:(b + 1) * P], qt[:, D + b * P:D + (b + 1) * P], ya[:, b * P:(b + 1) * P], 0, 1)
            for b in range(2):
                last = pe.transpose(ps[:, 3, b * P:(b + 1) * P], qt[:, b * P:(b + 1) * P], ident)
            last.then_inc(sem("kv_psum"), 1)
            pe.wait_ge(sem("kv"), 1)
            for b in range(2):
                last = mm(ps[:, 4, b * P:(b + 1) * P], raw[0][:, b * P:(b + 1) * P], raw[0][:, D + b * P:D + (b + 1) * P], 0, 1)
            last.then_inc(sem("lin_psum"), 1)
            pe.wait_ge(sem("lin"), 1)
            for b in range(2):
                last = mm(ps[:, 5, 0:D], yb[:, b * P:(b + 1) * P], wlb[:, LB["wo"] + b * D:LB["wo"] + (b + 1) * D], b, 2)
            last.then_inc(sem("y"), 1)
            turn_x(5, 5, ya)
            pe.wait_ge(sem("ff_loaded"), 16)
            for m in range(F1T):
                for k in range(DK):
                    last = mm(ps[:, m // 4, (m % 4) * P:(m % 4 + 1) * P], wa[:, k * 1024 + m * P:k * 1024 + (m + 1) * P],
                              xt[:, k * P:(k + 1) * P], k, DK)
            last.then_inc(sem("ff_up"), 1)
            pe.wait_ge(sem("ff_hid"), 1)
            for m in range(F1T):
                last = mm(ps[:, 5, 0:D], raw[m // 4][:, (m % 4) * P:(m % 4 + 1) * P],
                          wa[:, 2048 + m * D:2048 + (m + 1) * D], m, F1T)
            last.then_inc(sem("y"), 1)

            turn_x(7, 6, xn)
            for k in range(DK):
                last = mm(ps[:, 6, 0:E1], xt[:, k * P:(k + 1) * P], wlb[:, LB["wr"] + k * E1:LB["wr"] + (k + 1) * E1], k, DK)
            last.then_inc(sem("router"), 1)
            big = (ring[:, 0:W1], ring[:, W1:2 * W1], probs[:], wide[:])

            def up1(e):
                pe.wait_ge(sem(f"big{e % 4}"), 16 * (e // 4 + 1))
                if e >= 2:
                    pe.wait_ge(sem("gelu1"), e - 1)
                for m in range(F1T):
                    for k in range(DK):
                        c = k * F1T * P + m * P
                        last = mm(ps[:, 2 * (e % 2) + m // 4, (m % 4) * P:(m % 4 + 1) * P], big[e % 4][:, c:c + P],
                                  xt[:, k * P:(k + 1) * P], k, DK)
                last.then_inc(sem("up1"), 1)

            def down1(e):
                pe.wait_ge(sem("gelu1"), e + 1)
                if e >= 2:
                    pe.wait_ge(sem("acc1"), e - 1)
                for m in range(F1T):
                    c = DK * F1T * P + m * D
                    last = mm(ps[:, 4 + e % 2, 0:D], wa[:, (e % 2) * 1024 + m * P:(e % 2) * 1024 + (m + 1) * P],
                              big[e % 4][:, c:c + D], m, F1T)
                last.then_inc(sem("down1"), 1)

            up1(0)
            pe.wait_ge(sem("scores_r"), 1)
            pe.transpose(ps[0:E1, 6, 128:256], sm[:, 32:32 + E1], ident).then_inc(sem("scores_t"), 1)
            up1(1)
            pe.wait_ge(sem("picked"), 1)
            pe.transpose(ps[:, 6, 256:256 + E1], sel[:, 3 * P:4 * P], ident[0:E1, 0:E1])
            pe.wait_ge(sem("b2_loaded"), 16)
            mm(ps[:, 7, 0:D], sel[:, 3 * P:4 * P], b2[:], 0, 1).then_inc(sem("weights_psum"), 1)
            for e in range(E1):
                down1(e)
                if e + 2 < E1:
                    up1(e + 2)

        @block.vector
        def _(dve):
            link = chain(dve, "dve_step")
            dve.wait_ge(sem("x_loaded"), 16)

            def norm(n, src, dst, eps, scale=None, shift=None):
                link(dve.bn_stats(stat[:, n, 0:6], src[:]))
                link(dve.bn_aggr(stat[:, n, 6:8], stat[:, n, 0:6]))
                dve.tensor_scalar(stat[:, n, 8:9], stat[:, n, 7:8], eps, None, ALU.add).then_inc(sem("var"), 1)
                dve.wait_ge(sem("std"), n + 1)
                link(dve.reciprocal(stat[:, n, 10:11], stat[:, n, 9:10]))
                last = dve.tensor_scalar(dst[:], src[:], stat[:, n, 6:7], stat[:, n, 10:11], ALU.subtract, ALU.mult)
                if scale is not None:
                    link(last)
                    link(dve.tensor_tensor(dst[:], dst[:], scale, ALU.mult))
                    last = dve.tensor_tensor(dst[:], dst[:], shift, ALU.add)
                last.then_inc(sem("xn"), 1)
                dve.wait_ge(sem("xn"), n + 1)

            def take_xt(k):
                dve.wait_ge(sem("xt_psum"), k + 1)
                dve.tensor_copy(xt[:], ps[:, 7, 0:D]).then_inc(sem("xt"), 1)

            def spread(ap, n):
                return ap.unsqueeze(2).to_broadcast([P, ap.shape[1], n])

            def cross(layer):
                heads = HEADS[layer]
                units1 = heads // 8
                units2 = heads // 4
                w, at = wq[layer], XQ[layer]
                nb = heads * HD[layer] // P
                hpb = heads // nb
                width = heads * P
                norm(3 * layer, x, xn, 1e-5)
                take_xt(3 * layer)
                dve.wait_ge(sem("q_psum"), layer + 1)
                for b in range(nb):
                    bias = w[:, at["bq"] + b:at["bq"] + b + 1] if layer else 0.0
                    link(dve.tensor_scalar(qt[:, b * P:(b + 1) * P], ps[:, 0, b * P:(b + 1) * P], bias,
                                           float(HD[layer]) ** -0.5, ALU.add, ALU.mult))
                mask = cst[:, CONST["mask2"]:CONST["mask2"] + 2] if layer == 0 else cst[:, CONST["mask8"]:CONST["mask8"] + 8]
                for b in range(nb):
                    last = dve.tensor_tensor(
                        scr[:, b * hpb * P:(b + 1) * hpb * P].rearrange("p (h q) -> p h q", h=hpb),
                        qt[:, b * P:(b + 1) * P].unsqueeze(1).to_broadcast([P, hpb, P]), spread(mask, P), ALU.mult)
                last.then_inc(sem("q_diag"), 1)
                for c in range(width // 512):
                    dve.wait_ge(sem("q_folded"), 2 * layer + c + 1)
                    b = 1 + 3 * (c % 2)
                    cs = slice(c * 512, (c + 1) * 512)
                    dve.tensor_copy(q_ha[:, cs], ps[:, b, :])
                    dve.tensor_copy(q_b[:, cs], ps[:, b + 1, :])
                    link(dve.tensor_copy(q_he[:, cs], ps[0:CB + 1, b + 2, :]))
                    dve.tensor_tensor(q_la[:, cs], ps[:, b, :], q_ha[:, cs].bitcast(F32), ALU.subtract)
                    dve.tensor_tensor(q_le[0:CB, cs], ps[0:CB, b + 2, :], q_he[0:CB, cs].bitcast(F32), ALU.subtract)\
                       .then_inc(sem("q_chunk"), 1)
                link(dve.memset(run, LOWEST))

                def maxima(g, slot, first):
                    for j in range(GT):
                        for u in range(units1):
                            n = (g * GT + j) * units1 + u
                            dve.wait_ge(sem(f"s1_{layer}"), n + 1)
                            if not (first and slot == 0 and j * units1 + u < 1):
                                dve.wait_ge(sem(f"run{layer}"), n)
                            b = 2 * ((j * units1 + u) % 2)
                            r = run[:, u * 1024:(u + 1) * 1024]
                            dve.tensor_tensor(r, ps[:, b:b + 2, :].rearrange("p b n -> p (b n)"), r, ALU.max)\
                               .then_inc(sem(f"run{layer}"), 1)

                groups(dve, maxima)
                dve.wait_ge(sem("lanes_t"), layer + 1)
                dve.tensor_reduce(sm[:, 0:heads], ps[:, 4:4 + heads // 4, :].rearrange("p b (h n) -> p (b h) n", n=P), AX,
                                  ALU.max).then_inc(sem("max_q"), 1)
                dve.wait_ge(sem("max_psum"), layer + 1)
                dve.tensor_copy(m_t[0:heads, :], ps[0:heads, 2, 0:P]).then_inc(sem("max_t"), 1)
                dve.wait_ge(sem("max_row"), 16 * (layer + 1))
                dve.tensor_tensor(q_le[CB:CB + 1, 0:width], q_he[CB:CB + 1, 0:width].bitcast(F32),
                                  scr[CB:CB + 1, 0:width], ALU.subtract).then_inc(sem("shift"), 1)

                def split(g, slot, first):
                    dve.wait_ge(sem(f"ctx{slot}"), ctx_count(2 * layer + 1, slot, g))
                    if not first:
                        dve.wait_ge(sem(f"s2_{layer}"), (g - 1) * GT * units2)
                    r = raw[slot]
                    dve.tensor_copy(t_ha[slot][:], r[:, 0:GK])
                    dve.tensor_copy(t_e[slot][0:CB, :], r[0:CB, GK:2 * GK])
                    dve.tensor_copy(t_b[slot][:], r[:, GK:2 * GK]).then_inc(sem(f"part{layer}"), 1)
                    dve.wait_ge(sem(f"part{layer}"), g + 1)
                    dve.tensor_tensor(t_la[slot][:], r[:, 0:GK], t_ha[slot][:].bitcast(F32), ALU.subtract)
                    dve.tensor_tensor(t_b[slot][CB:P, :], r[CB:P, GK:2 * GK], t_b[slot][CB:P, :].bitcast(F32),
                                      ALU.subtract).then_inc(sem(f"split{layer}"), 1)
                    if layer == 1:
                        for j in range(GT):
                            t = g * GT + j
                            dve.wait_ge(sem("v_psum"), t + 1)
                            if not first:
                                dve.wait_ge(sem("pv1"), (t - 1) * units2)
                            dve.tensor_copy(v_sb[j][:, :, 0:16], ps[:, 2 + j, 0:D].rearrange("p (h d) -> p h d", h=16))\
                               .then_inc(sem("v_sb"), 1)

                groups(dve, split)
                dve.wait_ge(sem(f"pv{layer}"), TILES * units2)

            def add_y(n, bias):
                dve.wait_ge(sem("y"), n + 1)
                link(dve.tensor_tensor(ya[:], ps[:, 5, 0:D], bias, ALU.add))
                dve.tensor_tensor(x[:], x[:], ya[:], ALU.add).then_inc(sem("x_done"), 1)

            def head_t(n):
                dve.wait_ge(sem("head_t_psum"), n + 1)
                dve.tensor_copy(xt[:], ps[:, 7, 0:D]).then_inc(sem("head_t"), 1)

            for s in range(SLOTS):
                link(dve.memset(t_e[s][CB:CB + 1, :].bitcast(F32), 1.0))
            dve.wait_ge(sem("const_loaded"), 16)

            cross(0)
            sums = ps[:, 4:8, :].rearrange("p b (h w) -> p (b h) w", w=256)
            link(dve.reciprocal(sm[:, 32:40], sums[:, :, C:C + 1].rearrange("p h o -> p (h o)")))
            dve.tensor_tensor(probs[:, 0:8 * C].rearrange("p (h c) -> p h c", h=8), sums[:, :, 0:C],
                              spread(sm[:, 32:40], C), ALU.mult).then_inc(sem("u_sb"), 1)
            dve.wait_ge(sem("ut_psum"), 1)
            dve.tensor_copy(probs[:, 1536:2560], ps[:, 0:2, :].rearrange("p b n -> p (b n)"))
            dve.tensor_copy(probs[0:CB, 2560:3584], ps[0:CB, 2:4, :].rearrange("p b n -> p (b n)")).then_inc(sem("ut"), 1)
            dve.wait_ge(sem("ot_psum"), 1)
            dve.tensor_copy(qt[:], ps[:, 4, :]).then_inc(sem("ot"), 1)
            add_y(0, wa[:, XQ0["bo"]:XQ0["bo"] + D])
            dve.wait_ge(sem("x_done"), 1)

            norm(1, x, xn, 1e-5)
            take_xt(1)
            dve.wait_ge(sem("qkv_psum"), 1)
            link(dve.tensor_scalar(qt[:, 0:D], ps[:, 0, 0:D], 0.25, None, ALU.mult))
            link(dve.tensor_copy(qt[:, D:2 * D], ps[:, 0, D:2 * D]))
            link(dve.tensor_copy(ya[:], ps[:, 1, 0:D]))
            for b in range(2):
                last = dve.tensor_tensor(probs[:, b * 1024:(b + 1) * 1024].rearrange("p (h q) -> p h q", h=8),
                                         qt[:, D + b * P:D + (b + 1) * P].unsqueeze(1).to_broadcast([P, 8, P]),
                                         spread(cst[:, CONST["mask8"]:CONST["mask8"] + 8], P), ALU.mult)
            last.then_inc(sem("k_diag"), 1)
            dve.wait_ge(sem("s_a"), 1)
            run3 = run.rearrange("p (h n) -> p h n", h=16)
            causal = cst[:, CONST["causal"]:CONST["causal"] + P].unsqueeze(1).to_broadcast([P, 16, P])
            link(dve.tensor_tensor(run3, ps[:, 2:6, :].rearrange("p b (h n) -> p (b h) n", n=P), causal, ALU.add))
            link(dve.tensor_reduce(sm[:, 0:16], run3, AX, ALU.max))
            dve.tensor_tensor(run3, run3, spread(sm[:, 0:16], P), ALU.subtract).then_inc(sem("logit_a"), 1)
            dve.wait_ge(sem("prob_a"), 1)
            link(dve.tensor_reduce(sm[:, 16:32], run3, AX, ALU.add))
            link(dve.reciprocal(sm[:, 32:48], sm[:, 16:32]))
            dve.wait_ge(sem("pt_psum"), 1)
            dve.tensor_copy(scr[:, 0:1024], ps[:, 2:4, :].rearrange("p b n -> p (b n)")).then_inc(sem("pt_lo"), 1)
            dve.wait_ge(sem("o_a"), 1)
            dve.tensor_tensor(yb[:].rearrange("p (h d) -> p h d", h=16), ps[:, 6, 0:D].rearrange("p (h d) -> p h d", h=16),
                              spread(sm[:, 32:48], 16), ALU.mult).then_inc(sem("head_out"), 1)
            head_t(0)
            dve.wait_ge(sem("y"), 2)
            dve.tensor_tensor(x[:], ps[:, 5, 0:D], x[:], ALU.add).then_inc(sem("x_done"), 1)
            dve.wait_ge(sem("x_done"), 2)

            def softmax_small(n, width, bias):
                dve.wait_ge(sem("router"), n + 1)
                lg = sm[:, 0:width]
                if bias is None:
                    link(dve.tensor_copy(lg, ps[:, 6, 0:width]))
                else:
                    link(dve.tensor_tensor(lg, ps[:, 6, 0:width], bias, ALU.add))
                link(dve.tensor_reduce(sm[:, 48:49], lg, AX, ALU.max))
                dve.tensor_scalar(lg, lg, sm[:, 48:49], None, ALU.subtract).then_inc(sem("logit_r"), 1)
                dve.wait_ge(sem("prob_r"), n + 1)
                link(dve.tensor_reduce(sm[:, 49:50], sm[:, 16:16 + width], AX, ALU.add))
                link(dve.reciprocal(sm[:, 50:51], sm[:, 49:50]))
                last = dve.tensor_scalar(sm[:, 32:32 + width], sm[:, 16:16 + width], sm[:, 50:51], None, ALU.mult)
                return last

            norm(2, x, xn, 1e-5)
            take_xt(2)
            link(softmax_small(0, E0, cst[:, CONST["rb"]:CONST["rb"] + E0]))
            pr = sm[:, 32:32 + E0]
            link(dve.max(sm[:, 112:120], pr))
            link(dve.max_index(idx[:], sm[:, 112:120], pr))
            link(dve.tensor_copy(sm[:, 120:122], idx[:, 0:2]))
            iota = cst[:, CONST["iota"]:CONST["iota"] + E0]
            link(dve.tensor_scalar(sm[:, 128:144], iota, sm[:, 120:121], None, ALU.is_equal))
            link(dve.tensor_scalar(sm[:, 144:160], iota, sm[:, 121:122], None, ALU.is_equal))
            dve.tensor_tensor(sm[:, 64:80], sm[:, 128:144], sm[:, 144:160], ALU.add).then_inc(sem("chosen"), 1)
            link(dve.tensor_tensor(sm[:, 51:52], sm[:, 112:113], sm[:, 113:114], ALU.add))
            link(dve.tensor_scalar(sm[:, 52:53], sm[:, 51:52], 1e-9, None, ALU.add))
            link(dve.reciprocal(sm[:, 53:54], sm[:, 52:53]))
            link(dve.tensor_scalar(sm[:, 54:56], sm[:, 112:114], sm[:, 53:54], None, ALU.mult))
            link(dve.tensor_scalar(sm[:, 128:144], sm[:, 128:144], sm[:, 54:55], None, ALU.mult))
            link(dve.scalar_tensor_tensor(sm[:, 160:176], sm[:, 144:160], sm[:, 55:56], sm[:, 128:144], ALU.mult, ALU.add))
            dve.wait_ge(sem("rank"), 1)
            link(dve.scalar_tensor_tensor(sm[:, 176:192], ps[:, 6, 32:32 + E0], float(CAP), sm[:, 160:176],
                                          ALU.is_lt, ALU.mult))

            def hidden0(e, par):
                dve.wait_ge(sem("silu"), e + 1)
                if not (isinstance(e, int) and e < 2):
                    dve.wait_ge(sem("down0"), e - 1)
                dve.tensor_tensor(probs[:, 2048 + par * 1024:2048 + par * 1024 + 384], ps[:, 2 + par, 0:384],
                                  probs[:, par * 1024:par * 1024 + 384], ALU.mult).then_inc(sem("hid0"), 1)

            def sum0(e, par):
                dve.wait_ge(sem("down0"), e + 1)
                if isinstance(e, int) and e == 0:
                    dve.tensor_tensor(ya[:], ps[:, 4, 0:D], xn[:], ALU.add).then_inc(sem("acc0"), 1)
                    return
                dve.wait_ge(sem("acc0"), e)
                w = sm[:, 175 + e:176 + e] if isinstance(e, int) else sm[:, bass.ds(e + 175, 1)]
                dve.scalar_tensor_tensor(ya[:], ps[:, 4 + par, 0:D], w, ya[:], ALU.mult, ALU.add)\
                   .then_inc(sem("acc0"), 1)

            hidden0(0, 0)
            for e in range(1, 5):
                hidden0(e, e % 2)
                sum0(e - 1, (e - 1) % 2)
            with dve.Fori(1, 4) as i:
                for k in range(1, 5):
                    hidden0(4 * i + k, k % 2)
                    sum0(4 * i + k - 1, (k - 1) % 2)
            sum0(E0, 0)
            dve.wait_ge(sem("acc0"), E0 + 1)
            dve.tensor_tensor(x[:], x[:], ya[:], ALU.add).then_inc(sem("x_done"), 1)
            dve.wait_ge(sem("x_done"), 3)

            dve.wait_ge(sem("xq1_loaded"), 16)
            va, vb = wx1[:, XQ1["wva"]:XQ1["wva"] + D], wx1[:, XQ1["wvb"]:XQ1["wvb"] + D]
            link(dve.tensor_copy(wv_ha[:], va))
            link(dve.tensor_copy(wv_hb[:], vb))
            link(dve.tensor_tensor(wv_la[:], va, wv_ha[:].bitcast(F32), ALU.subtract))
            link(dve.tensor_tensor(wv_lb[:], vb[0:CB, :], wv_hb[0:CB, :].bitcast(F32), ALU.subtract))
            for i in range(2):
                link(dve.memset(v_sb[i][:], 0.0))
                link(dve.memset(v_sb[i][:, :, 16:17], 1.0))
            dve.tensor_copy(sm[:, 240:241], sm[:, 176:177]).then_inc(sem("v_ready"), 1)
            cross(1)
            dve.tensor_copy(qt[:], ps[:, 4, :]).then_inc(sem("o_sb"), 1)
            dve.wait_ge(sem("o_t"), 1)
            heads = ps[:, 5, :].rearrange("p (h w) -> p h w", w=32)
            link(dve.reciprocal(sm[:, 32:48], heads[:, :, 16:17].rearrange("p h o -> p (h o)")))
            link(dve.tensor_tensor(yb[:].rearrange("p (h d) -> p h d", h=16), heads[:, :, 0:16], spread(sm[:, 32:48], 16),
                                   ALU.mult))
            dve.tensor_tensor(yb[:], yb[:], wx1[:, XQ1["bv"]:XQ1["bv"] + D], ALU.add).then_inc(sem("head_out"), 1)
            head_t(1)
            add_y(2, wx1[:, XQ1["bo"]:XQ1["bo"] + D])
            dve.wait_ge(sem("x_done"), 4)

            def lb(name, n=D):
                return wlb[:, LB[name]:LB[name] + n]

            norm(4, x, xn, 1e-5)
            take_xt(4)
            dve.wait_ge(sem("qkv_psum"), 2)
            link(dve.tensor_tensor(qt[:], ps[:, 0, :], lb("bqk", 512), ALU.add))
            link(dve.tensor_tensor(ya[:], ps[:, 1, 0:D], lb("bv"), ALU.add))
            dve.tensor_scalar(raw[1][:, 0:512], qt[:], 0.0, None, ALU.min).then_inc(sem("elu_in"), 1)
            dve.wait_ge(sem("elu_exp"), 1)
            link(dve.tensor_scalar(raw[0][:, 0:512], raw[1][:, 0:512], -1.0, None, ALU.add))
            link(dve.scalar_tensor_tensor(qt[:], qt[:], 0.0, raw[0][:, 0:512], ALU.max, ALU.add))
            link(dve.tensor_tensor(raw[0][:, 0:512], qt[:], qt[:], ALU.mult))
            dve.tensor_reduce(sm[:, 0:32], raw[0][:, 0:512].rearrange("p (h d) -> p h d", h=32), AX, ALU.add)\
               .then_inc(sem("norm_in"), 1)
            dve.wait_ge(sem("norm_out"), 1)
            link(dve.reciprocal(sm[:, 64:96], sm[:, 32:64]))
            qt3 = qt[:].rearrange("p (h d) -> p h d", h=32)
            dve.tensor_tensor(qt3, qt3, spread(sm[:, 64:96], 16), ALU.mult).then_inc(sem("unit_qk"), 1)
            dve.wait_ge(sem("kv_psum"), 1)
            diag = spread(cst[:, CONST["mask8"]:CONST["mask8"] + 8], 16)
            for b in range(2):
                link(dve.scalar_tensor_tensor(raw[0][:, b * P:(b + 1) * P].rearrange("p (h d) -> p h d", h=8),
                                              ps[:, 2, b * P:(b + 1) * P].rearrange("p (h d) -> p h d", h=8), 0.25, diag,
                                              ALU.mult, ALU.mult))
            dve.tensor_copy(raw[0][:, D:2 * D], ps[:, 3, 0:D]).then_inc(sem("kv"), 1)
            dve.wait_ge(sem("lin_psum"), 1)
            dve.tensor_copy(yb[:], ps[:, 4, 0:D]).then_inc(sem("lin"), 1)
            dve.wait_ge(sem("y"), 4)
            link(dve.tensor_tensor(ya[:], ps[:, 5, 0:D], lb("bo"), ALU.add))
            link(dve.tensor_tensor(yb[:], ya[:], xn[:], ALU.add))
            norm(5, yb, ya, 1e-12, lb("g1"), lb("be1"))
            take_xt(5)
            dve.wait_ge(sem("y"), 5)
            link(dve.tensor_tensor(yb[:], ps[:, 5, 0:D], lb("b2"), ALU.add))
            link(dve.tensor_tensor(yb[:], yb[:], ya[:], ALU.add))
            norm(6, yb, ya, 1e-12, lb("g2"), lb("be2"))
            dve.tensor_tensor(x[:], x[:], ya[:], ALU.add).then_inc(sem("x_done"), 1)
            dve.wait_ge(sem("x_done"), 5)

            norm(7, x, xn, 1e-5)
            take_xt(6)
            softmax_small(1, E1, None).then_inc(sem("scores_r"), 1)
            dve.wait_ge(sem("scores_t"), 1)
            link(dve.tensor_copy(sel[:, 0:P], ps[0:E1, 6, 128:256]))
            link(dve.tensor_copy(sel[:, P:2 * P], ps[0:E1, 6, 128:256]))
            for r in range(TOPK // 8):
                cur, nxt = 1 + r % 2, 1 + (r + 1) % 2
                link(dve.max(sm[0:E1, 64:72], sel[:, cur * P:(cur + 1) * P]))
                link(dve.match_replace(sel[:, nxt * P:(nxt + 1) * P], sm[0:E1, 64:72], sel[:, cur * P:(cur + 1) * P], -1.0))
            dve.scalar_tensor_tensor(sel[:, 3 * P:4 * P], sel[:, nxt * P:(nxt + 1) * P], 0.0, sel[:, 0:P],
                                     ALU.is_lt, ALU.mult).then_inc(sem("picked"), 1)
            dve.wait_ge(sem("weights_psum"), 1)
            link(dve.tensor_copy(sm[:, 80:88], ps[:, 6, 256:264]))
            link(dve.tensor_tensor(x[:], ps[:, 7, 0:D], x[:], ALU.add))
            for e in range(E1):
                dve.wait_ge(sem("down1"), e + 1)
                if e:
                    dve.wait_ge(sem("acc1"), e)
                dve.scalar_tensor_tensor(x[:], ps[:, 4 + e % 2, 0:D], sm[:, 80 + e:81 + e], x[:], ALU.mult, ALU.add)\
                   .then_inc(sem("acc1"), 1)
            dve.wait_ge(sem("acc1"), E1)
            dve.tensor_copy(ya[:], x[:]).then_inc(sem("result"), 1)


def tiles(w, n=P):
    k = w.shape[0] // n
    return w.reshape(k, n, w.shape[1]).transpose(1, 0, 2).reshape(n, -1)


def rows(v):
    return np.broadcast_to(np.asarray(v).reshape(1, -1), (P, np.asarray(v).size))


def xq_pack(layer, wq, wk, wv, wo, bo, bq=None, bk=None, bv=None):
    inner = wq.shape[1]
    nb = inner // P
    kt = wk.T.reshape(nb, P, C)
    tail = (np.zeros((nb, P, 1), wk.dtype) if bk is None else bk.reshape(nb, P, 1))
    wkp = np.concatenate([kt[:, :, 0:P], kt[:, :, P:], kt[:, :, P:], kt[:, :, P:], tail], 2).transpose(1, 0, 2).reshape(P, -1)
    parts = [tiles(wq), wkp, wv[0:P], np.concatenate([wv[P:], wv[P:]], 0), tiles(wo), rows(bo)]
    if layer:
        parts += [rows(bv), bq.reshape(nb, P).T]
    return np.ascontiguousarray(np.concatenate(parts, 1))


def constants():
    p = np.arange(P)
    f = np.float32
    return (np.eye(P, dtype=f), (p[:, None] < p[None, :]).astype(f),
            np.where(p[None, :] > p[:, None], f(-1e30), f(0)).astype(f),
            (p[:, None] // 64 == np.arange(2)[None, :]).astype(f),
            (p[:, None] // 16 == np.arange(8)[None, :]).astype(f),
            np.broadcast_to(np.arange(E0, dtype=f)[None, :], (P, E0)))


def kernel(**inputs):
    import concourse.bacc as bacc
    from concourse.bass_utils import run_bass_kernel_spmd

    a = {k: np.asarray(v) for k, v in inputs.items()}
    ctx = a["ctx_768"].reshape(GROUPS, P, GT, C)
    turned = ctx.transpose(0, 3, 2, 1)
    ones = np.ones((GROUPS, P, GT, VW - C), ctx.dtype)
    pack = np.concatenate([turned[:, 0:P].reshape(GROUPS, P, GK),
                           np.concatenate([turned[:, P:], turned[:, P:]], 1).reshape(GROUPS, P, GK),
                           np.concatenate([ctx, ones], 3).reshape(GROUPS, P, GT * VW)], 2)

    def wide_f(w):
        return np.concatenate([w, np.zeros((*w.shape[:-1], F0T * P - F0), w.dtype)], -1)

    def expert0(g, u, d):
        dp = np.concatenate([d, np.zeros((F0T * P - F0, D), d.dtype)], 0)
        return np.concatenate([tiles(wide_f(g)), tiles(wide_f(u)), tiles(dp)], 1)

    ex0 = np.stack([expert0(a["L0_ffn_sw_gate"], a["L0_ffn_sw_up"], a["L0_ffn_sw_down"])]
                   + [expert0(a["L0_ffn_w_gate"][e], a["L0_ffn_w_up"][e], a["L0_ffn_w_down"][e]) for e in range(E0)])
    ex1 = np.stack([np.concatenate([tiles(a["L1_ffn_W1"][e]), tiles(a["L1_ffn_W2"][e]), a["L1_ffn_b1"][e].reshape(F1T, P).T], 1)
                    for e in range(E1)])
    L1 = {k[8:]: v for k, v in a.items() if k.startswith("L1_attn_")}
    arrays = {
        "x_in": a["x"][0],
        "ctx_in": pack,
        "xq0_in": xq_pack(0, a["L0_xattn_Wq"], a["L0_xattn_Wk"], a["L0_xattn_Wv"], a["L0_xattn_Wo"], a["L0_xattn_bo"]),
        "xq1_in": xq_pack(1, *(a["L1_xattn_" + n] for n in ("Wq", "Wk", "Wv", "Wo", "bo", "bq", "bk", "bv"))),
        "const_in": np.concatenate([*constants(), rows(a["L0_ffn_router_b"]), tiles(a["L0_ffn_router_w"])], 1),
        "la_in": np.concatenate([tiles(a["L0_attn_" + n].T) for n in ("Wq", "Wk", "Wv", "Wo")], 1),
        "lb_in": np.concatenate([tiles(L1["Wq"]), tiles(L1["Wk"]), tiles(L1["Wv"]), tiles(L1["Wo"]), tiles(a["L1_ffn_Wr"]),
                                 rows(L1["bq"]), rows(L1["bk"]), rows(L1["bv"]), rows(L1["bo"]), rows(L1["g1"]),
                                 rows(L1["be1"]), rows(L1["b2"]), rows(L1["g2"]), rows(L1["be2"]),
                                 L1["b1"].reshape(F1T, P).T], 1),
        "ff_in": np.concatenate([tiles(L1["W1"]), tiles(L1["W2"])], 1),
        "ex0_in": ex0,
        "ex1_in": ex1,
        "b2_in": a["L1_ffn_b2"],
    }
    nc = bacc.Bacc("TRN2", target_bir_lowering=False, num_devices=1)
    given, aps = {}, []
    for name, v in arrays.items():
        v = np.ascontiguousarray(v)
        given[name] = v
        aps.append(nc.dram_tensor(name, v.shape, mybir.dt.from_np(v.dtype), kind="ExternalInput").ap())
    out = nc.dram_tensor("out", (P, D), F32, kind="ExternalOutput").ap()
    perceiver(nc, *aps, out)
    r = run_bass_kernel_spmd(nc, [given], core_ids=[0])
    return r.results[0]["out"].reshape(1, P, D)
```

```python
from contextlib import ExitStack

import numpy as np

import concourse.bass as bass
from concourse import mybir

F32 = mybir.dt.float32
F32R = mybir.dt.float32r
U32 = mybir.dt.uint32
BF16 = mybir.dt.bfloat16
ALU = mybir.AluOpType
ACT = mybir.ActivationFunctionType
AX = mybir.AxisListType.X

P = 128
D = 256
DK = 2
C = 192
CB = C - P
S = 12544
TILES = S // P
GT = 2
GROUPS = TILES // GT
GK = GT * P
RAW = 2 * GK
UNITS = 4
HEADS = (8, 16)
HD = (64, 16)
SLOTS = 2
F0 = 352
F0T = 3
E0 = 16
CAP = 20
W0 = 4 * F0T * P + F0T * D
F1T = 8
E1 = 8
TOPK = 32
W1 = DK * F1T * P + F1T * D + F1T
QS = P + P + CB + 1
LOWEST = -3.0e38


def xq_offsets(layer):
    inner = HEADS[layer] * HD[layer]
    nb = inner // P
    at, o = {}, 0
    for name, n in ((("wq", DK * inner), ("wk", nb * QS)) if layer == 0 else
                    (("wq", DK * 512), ("wka", D), ("wkb", D), ("bk", D), ("bv", D), ("bq", UNITS))) + (
                    ("wva", inner), ("wvb", inner), ("wo", nb * D), ("bo", D)):
        at[name] = o
        o += n
    return at, o


XQ0, XQ0W = xq_offsets(0)
XQ1, XQ1W = xq_offsets(1)
CONST = {"ident": 0, "before": 128, "causal": 256, "mask2": 384, "mask8": 386, "iota": 394, "rb": 410, "rw": 426,
         "mask4": 458, "pick": 462}
CONSTW = 464
LA = {"wq": 0, "wk": 512, "wv": 1024, "wo": 1536}
LB = {"wq": 0, "wk": 512, "wv": 1024, "wo": 1536, "wr": 2048, "bqk": 2064, "bv": 2576, "bo": 2832,
      "g1": 3088, "be1": 3344, "b2": 3600, "g2": 3856, "be2": 4112, "b1": 4368}
LBW = 4376
FFW = DK * 1024 + F1T * D


def perceiver(nc, x_in, ctx_in, xq0_in, xq1_in, const_in, la_in, lb_in, ff_in, ex0_in, ex1_in, b2_in, out):
    with ExitStack() as stack:
        def sb(name, shape, dt=F32):
            return stack.enter_context(nc.sbuf_tensor(name, shape, dt))

        names = {}

        def sem(name):
            if name not in names:
                names[name] = stack.enter_context(nc.semaphore(name))
            return names[name]

        ps = stack.enter_context(nc.psum_tensor("ps", [P, 8, 512], F32))
        raw = [sb(f"raw{s}", [P, RAW]) for s in range(SLOTS)]
        t_ha = [sb(f"t_ha{s}", [P, GK], F32R) for s in range(SLOTS)]
        t_la = [sb(f"t_la{s}", [P, GK], F32R) for s in range(SLOTS)]
        t_b = [sb(f"t_b{s}", [P, GK], F32R) for s in range(SLOTS)]
        t_e = [sb(f"t_e{s}", [CB + 2, GK], F32R) for s in range(SLOTS)]
        q_ha = sb("q_ha", [P, 2048], F32R)
        q_la = sb("q_la", [P, 1024], F32R)
        q_b = sb("q_b", [P, 1024], F32R)
        q_he = sb("q_he", [CB + 1, 1024], F32R)
        q_le = sb("q_le", [CB + 1, 2048], F32R)
        kk = (q_la, q_b)
        ke = (q_he, sb("ke", [CB + 1, 1024], F32R))
        probs = sb("probs", [P, W1])
        wide = sb("wide", [P, W1])
        run = wide[:, 0:2048]
        scr = wide[:, 2048:4096]
        half16 = scr.bitcast(BF16)
        ring = sb("ring", [P, 4 * W0])
        wa = sb("wa", [P, XQ0W])
        wx1 = sb("wx1", [P, XQ1W])
        cst = sb("cst", [P, CONSTW])
        wlb = sb("wlb", [P, LBW])
        wv_ha = sb("wv_ha", [P, 512], F32R)
        wv_la = sb("wv_la", [P, 512], F32R)
        wv_hb = sb("wv_hb", [P, 512], F32R)
        wv_lb = sb("wv_lb", [CB, 512], F32R)
        wk_ha = sb("wk_ha", [P, D], F32R)
        wk_la = sb("wk_la", [P, D], F32R)
        wk_hb = sb("wk_hb", [P, D], F32R)
        wk_he = sb("wk_he", [CB + 2, D], F32R)
        wk_le = sb("wk_le", [CB + 2, D], F32R)
        v_sb = [sb(f"v_sb{i}", [P, 512]) for i in range(2)]
        ones = sb("ones", [P, CB])
        x = sb("x", [P, D])
        xn = sb("xn", [P, D])
        xt = sb("xt", [P, D])
        ya = sb("ya", [P, D])
        yb = sb("yb", [P, D])
        qt = sb("qt", [P, 512])
        stat = sb("stat", [P, 8, 12])
        sm = sb("sm", [P, 256])
        idx = sb("idx", [P, 8], U32)
        b2 = sb("b2", [E1, D])
        m_t = sb("m_t", [16, P])
        sel = sb("sel", [E1, 4 * P])

        ident = cst[:, 0:128]
        s_bank = ((0, 1), (0, 1, 3, 7))
        v_bank = ((2, 3), (2, 2))
        block = stack.enter_context(nc.Block())

        UNITS1 = (1, 2)
        DEPTH1 = (4, 2)
        BACK1 = (4, 1)

        def tile_buffer(layer, slot, j):
            return 2 * slot + j if layer == 0 else j

        def front_bank(layer, q):
            return q if layer == 0 else 4 * q

        def back_bank(layer, q):
            return 4 + q if layer == 0 else 2

        def unit_halves(tile, odd, rows=slice(0, CB)):
            return tile[rows, :].rearrange("p (b w k) -> p w b k", w=2, k=GK)[:, odd]

        def chain(eng, name):
            count = [0]

            def link(ins):
                count[0] += 1
                ins.then_inc(sem(name), 1)
                eng.wait_ge(sem(name), count[0])
            return link

        def ctx_count(phase, slot, g):
            per_phase = (GROUPS + 1) // 2 if slot == 0 else GROUPS // 2
            return 16 * (phase * per_phase + 1) + 8 * (g - slot)

        def groups(eng, body):
            body(0, 0, True)
            body(1, 1, True)
            with eng.Fori(1, GROUPS // 2) as i:
                body(2 * i, 0, False)
                body(2 * i + 1, 1, False)
            body(GROUPS - 1, 0, False)

        @block.sync
        def _(sp):
            sp.dma_start(x[:], x_in).then_inc(sem("x_loaded"), 16)
            sp.dma_start(cst[:], const_in).then_inc(sem("const_loaded"), 16)
            sp.dma_start(wa[:], xq0_in).then_inc(sem("xq0_loaded"), 16)
            for layer in range(2):
                def load_hi(g, slot, first):
                    if not first:
                        sp.wait_ge(sem(f"hi{layer}"), g - 1)
                    sp.dma_start(raw[slot][:], ctx_in[g]).then_inc(sem(f"ctx{slot}"), 16)

                def load_all(g, slot, first):
                    if not first:
                        sp.wait_ge(sem(f"split{layer}"), g - 1)
                    sp.dma_start(raw[slot][:], ctx_in[g]).then_inc(sem(f"ctx{slot}"), 16)

                if layer == 1:
                    sp.wait_ge(sem("split0"), GROUPS)
                groups(sp, load_hi)
                sp.wait_ge(sem(f"hi{layer}"), GROUPS)
                load_all(0, 0, True)
                load_all(1, 1, True)
                sp.wait_ge(sem("max_t"), layer + 1)
                sp.dma_start(scr[CB:CB + 1, 0:HEADS[layer] * P], m_t[0:HEADS[layer], :]).then_inc(sem("max_row"), 16)
                with sp.Fori(1, GROUPS // 2) as i:
                    load_all(2 * i, 0, False)
                    load_all(2 * i + 1, 1, False)
                load_all(GROUPS - 1, 0, False)
            sp.wait_ge(sem("result"), 1)
            sp.dma_start(out, x[:]).then_inc(sem("stored"), 16)
            sp.wait_ge(sem("stored"), 16)

        @block.gpsimd
        def _(pool):
            pool.dma_start(wlb[:, 0:2048], la_in).then_inc(sem("la_loaded"), 16)
            pool.dma_start(wx1[:], xq1_in).then_inc(sem("xq1_loaded"), 16)
            pool.dma_start(b2[:], b2_in).then_inc(sem("b2_loaded"), 16)

            def load0(e, slot):
                pool.dma_start(ring[:, slot * W0:(slot + 1) * W0], ex0_in[e]).then_inc(sem(f"ring{slot}"), 16)

            for e in range(4):
                load0(e, e)

            def round_hi(layer):
                def body(g, slot, first):
                    pool.wait_ge(sem(f"ctx{slot}"), ctx_count(2 * layer, slot, g))
                    if not first:
                        pool.wait_ge(sem("s1_0" if layer == 0 else "k1"), (g - 1) * (GT if layer == 0 else 1))
                    b = raw[slot][0:CB, GK:2 * GK]
                    pool.tensor_tensor(t_e[slot][0:CB, :], b, ones[0:CB, 0:1].to_broadcast([CB, GK]), ALU.mult)
                    pool.tensor_copy(t_ha[slot][:], raw[slot][:, 0:GK]).then_inc(sem(f"hi{layer}"), 1)
                groups(pool, body)

            pool.wait_ge(sem("ones"), 1)
            round_hi(0)
            pool.wait_ge(sem("x_done"), 1)
            pool.dma_start(wa[:, 0:FFW], ff_in).then_inc(sem("ff_loaded"), 16)
            pool.wait_ge(sem("x_done"), 2)
            pool.dma_start(wlb[:], lb_in).then_inc(sem("lb_loaded"), 16)
            with pool.Fori(0, 3) as i:
                for k in range(4):
                    pool.wait_ge(sem("down0"), 4 * i + k + 1)
                    load0(4 * i + k + 4, k)
            pool.wait_ge(sem("down0"), 13)
            load0(16, 0)
            pool.wait_ge(sem("down0"), E0 + 1)
            pool.dma_start(ring[:, 0:W1], ex1_in[0]).then_inc(sem("big0"), 16)
            pool.dma_start(ring[:, W1:2 * W1], ex1_in[1]).then_inc(sem("big1"), 16)
            pool.wait_ge(sem("split0"), GROUPS)
            pool.wait_ge(sem("pv0"), 2 * TILES)
            round_hi(1)
            pool.wait_ge(sem("x_done"), 4)
            pool.dma_start(probs[:], ex1_in[2]).then_inc(sem("big2"), 16)
            pool.dma_start(wide[:], ex1_in[3]).then_inc(sem("big3"), 16)
            big = (ring[:, 0:W1], ring[:, W1:2 * W1], probs[:], wide[:])
            for e in range(4, E1):
                pool.wait_ge(sem("down1"), e - 3)
                pool.dma_start(big[e % 4], ex1_in[e]).then_inc(sem(f"big{e % 4}"), 16)

        @block.scalar
        def _(act):
            def root(n):
                act.wait_ge(sem("var"), n + 1)
                act.activation(stat[:, n, 9:10], stat[:, n, 8:9], ACT.Sqrt).then_inc(sem("std"), 1)

            def keep_half(layer, t, q, first):
                units, depth = UNITS1[layer], DEPTH1[layer]
                if not first:
                    act.wait_ge(sem(f"run{layer}"), t - depth + 1)
                for u in range(units):
                    act.wait_ge(sem(f"s1b_{layer}"), t * units + u + 1)
                    c = (q * units + u) * 512
                    act.copy(half16[:, c:c + 512], ps[:, back_bank(layer, q) + u, :]).then_inc(sem(f"half{layer}"), 1)

            def exps(layer, t, j, first):
                units = HEADS[layer] // 4
                if layer == 0:
                    act.wait_ge(sem("v_psum0"), t + 1)
                    if not first:
                        act.wait_ge(sem("pv0"), (t - 1) * units)
                    act.copy(v_sb[j][:], ps[:, v_bank[0][j], :]).then_inc(sem("v_sb0"), 1)
                    if not first:
                        act.wait_ge(sem("lsum"), t - 1)
                for u in range(units):
                    n = t * units + u
                    act.wait_ge(sem(f"s2_{layer}"), n + 1)
                    if not first:
                        act.wait_ge(sem(f"pv{layer}"), n + 1 - 2 * units)
                    act.activation(probs[:, j * 2048 + u * 512:j * 2048 + (u + 1) * 512], ps[:, s_bank[layer][u], :],
                                   ACT.Exp).then_inc(sem(f"exp{layer}"), 1)

            def keep_keys(g, slot, first):
                act.wait_ge(sem("k1"), g + 1)
                if not first:
                    act.wait_ge(sem("s1_1"), (g - 1) * GT)
                act.copy(t_la[slot][:], ps[:, 6, 0:GK])
                act.copy(t_b[slot][:], ps[:, 6, GK:2 * GK]).then_inc(sem("keys1"), 1)

            def pass1(layer):
                def body(g, slot, first, last=False):
                    if layer == 1 and not last:
                        keep_keys(g + 1, 1 - slot, first and slot == 0)
                    for j in range(GT):
                        q = tile_buffer(layer, slot, j)
                        keep_half(layer, g * GT + j, q, first and (slot == 0 or layer == 0))
                if layer == 1:
                    keep_keys(0, 0, True)
                body(0, 0, True)
                body(1, 1, True)
                with act.Fori(1, GROUPS // 2) as i:
                    body(2 * i, 0, False)
                    body(2 * i + 1, 1, False)
                body(GROUPS - 1, 0, False, True)

            def pass2(layer):
                def body(g, slot, first):
                    for j in range(GT):
                        exps(layer, g * GT + j, j, first and slot == 0)
                groups(act, body)

            def cross(layer):
                root(3 * layer)
                if layer == 1:
                    act.wait_ge(sem("q_diag"), 2)
                pass1(layer)
                pass2(layer)

            cross(0)
            root(1)
            act.wait_ge(sem("logit_a"), 1)
            act.activation(run, run, ACT.Exp).then_inc(sem("prob_a"), 1)
            act.wait_ge(sem("pt_psum"), 1)
            act.copy(scr[:, 1024:2048], ps[:, 4:6, :]).then_inc(sem("pt_hi"), 1)
            root(2)
            act.wait_ge(sem("logit_r"), 1)
            act.activation(sm[:, 16:32], sm[:, 0:16], ACT.Exp).then_inc(sem("prob_r"), 1)

            def silu(e, par):
                act.wait_ge(sem("up0"), e + 1)
                if not (isinstance(e, int) and e < 2):
                    act.wait_ge(sem("hid0"), e - 1)
                act.activation(probs[:, par * 1024:par * 1024 + 384], ps[:, par, 0:384], ACT.Silu)\
                   .then_inc(sem("silu"), 1)

            for e in range(5):
                silu(e, e % 2)
            with act.Fori(1, 4) as i:
                for k in range(1, 5):
                    silu(4 * i + k, k % 2)

            cross(1)
            root(4)
            act.wait_ge(sem("elu_in"), 1)
            act.activation(raw[1][:, 0:512], raw[1][:, 0:512], ACT.Exp).then_inc(sem("elu_exp"), 1)
            act.wait_ge(sem("norm_in"), 1)
            act.activation(sm[:, 32:64], sm[:, 0:32], ACT.Sqrt).then_inc(sem("norm_out"), 1)
            root(5)
            act.wait_ge(sem("ff_up"), 1)
            for m in range(F1T):
                last = act.activation(raw[m // 4][:, (m % 4) * P:(m % 4 + 1) * P],
                                      ps[:, m // 4, (m % 4) * P:(m % 4 + 1) * P], ACT.Gelu,
                                      bias=wlb[:, LB["b1"] + m:LB["b1"] + m + 1])
            last.then_inc(sem("ff_hid"), 1)
            root(6)
            root(7)
            act.wait_ge(sem("logit_r"), 2)
            act.activation(sm[:, 16:24], sm[:, 0:8], ACT.Exp).then_inc(sem("prob_r"), 1)
            big = (ring[:, 0:W1], ring[:, W1:2 * W1], probs[:], wide[:])
            for e in range(E1):
                act.wait_ge(sem("up1"), e + 1)
                if e >= 2:
                    act.wait_ge(sem("down1"), e - 1)
                for m in range(F1T):
                    last = act.activation(wa[:, (e % 2) * 1024 + m * P:(e % 2) * 1024 + (m + 1) * P],
                                          ps[:, 2 * (e % 2) + m // 4, (m % 4) * P:(m % 4 + 1) * P], ACT.Gelu,
                                          bias=big[e % 4][:, W1 - F1T + m:W1 - F1T + m + 1])
                last.then_inc(sem("gelu1"), 1)

        @block.tensor
        def _(pe):
            def turn_x(n, k, src):
                pe.wait_ge(sem("xn"), n + 1)
                pe.transpose(ps[:, 7, 0:128], src[:, 0:128], ident)
                pe.transpose(ps[:, 7, 128:256], src[:, 128:256], ident).then_inc(sem("xt_psum"), 1)
                pe.wait_ge(sem("xt"), k + 1)

            def mm(o, l, r, k, n, **more):
                return pe.matmul(o, l, r, start=(k == 0), stop=(k == n - 1), **more)

            def fold():
                pe.wait_ge(sem("xq0_loaded"), 16)
                inner = HEADS[0] * HD[0]
                for b in range(4):
                    for k in range(DK):
                        c = XQ0["wq"] + k * inner + b * P
                        last = mm(ps[:, 0, b * P:(b + 1) * P], wa[:, c:c + P], xt[:, k * P:(k + 1) * P], k, DK)
                last.then_inc(sem("q_psum"), 1)
                pe.wait_ge(sem("q_diag"), 1)
                for c in range(2):
                    for part, (o, m) in enumerate(((0, P), (P, P), (2 * P, CB + 1))):
                        for b in range(2 * c, 2 * c + 2):
                            last = mm(ps[0:m, 1 + 3 * c + part, (b % 2) * 256:(b % 2) * 256 + 256],
                                      wa[:, XQ0["wk"] + b * QS + o:XQ0["wk"] + b * QS + o + m],
                                      scr[:, b * 256:(b + 1) * 256], 0, 1)
                    last.then_inc(sem("q_folded"), 1)
                pe.wait_ge(sem("q_chunk"), 2)

            def queries1():
                pe.wait_ge(sem("xq1_loaded"), 16)
                for u in range(UNITS):
                    for k in range(DK):
                        c = XQ1["wq"] + k * 512 + u * P
                        last = mm(ps[:, 0, u * P:(u + 1) * P], wx1[:, c:c + P], xt[:, k * P:(k + 1) * P], k, DK)
                last.then_inc(sem("q_psum"), 1)
                pe.wait_ge(sem("q_diag"), 2)

            def keys1(g, slot, first):
                pe.wait_ge(sem("hi1"), g + 1)
                if not first:
                    pe.wait_ge(sem("keys1"), g)
                for b in range(2):
                    o = ps[:, 6, b * GK:(b + 1) * GK]
                    ws = slice(b * P, (b + 1) * P)
                    mm(o, wk_ha[:, ws], t_ha[slot][:], 0, 2)
                    last = mm(o, wk_he[:, ws], t_e[slot][:], 1, 2)
                last.then_inc(sem("k1"), 1)

            def keys2(g, slot, first):
                if not first:
                    pe.wait_ge(sem("kk"), g)
                pe.wait_ge(sem("split1"), g + 1)
                for b in range(2):
                    o = ps[:, 5, b * GK:(b + 1) * GK]
                    ws = slice(b * P, (b + 1) * P)
                    mm(o, wk_ha[:, ws], t_ha[slot][:], 0, 5)
                    mm(o, wk_la[:, ws], t_ha[slot][:], 1, 5)
                    mm(o, wk_ha[:, ws], t_la[slot][:], 2, 5)
                    mm(o, wk_hb[:, ws], t_b[slot][:], 3, 5)
                    last = mm(o, wk_le[:, ws], t_e[slot][:], 4, 5)
                last.then_inc(sem("k2"), 1)

            def cross(layer):
                heads = HEADS[layer]
                units2 = heads // 4
                turn_x(3 * layer, 3 * layer, xn)
                if layer == 0:
                    fold()
                else:
                    queries1()

                def scores1(g, slot, first, last=False):
                    if layer == 0:
                        pe.wait_ge(sem("hi0"), g + 1)
                    else:
                        if not last:
                            keys1(g + 1, 1 - slot, False)
                        pe.wait_ge(sem("keys1"), g + 1)
                    units, depth = UNITS1[layer], DEPTH1[layer]
                    for j in range(GT):
                        t = g * GT + j
                        q = tile_buffer(layer, slot, j)
                        ks = slice(j * P, (j + 1) * P)
                        fresh = first and t < depth
                        for n in (*range(units, 2 * units), *range(units)):
                            cs = slice(n * 512, (n + 1) * 512)
                            if n >= units:
                                u = n - units
                                o = ps[:, back_bank(layer, q) + u, :]
                                if not (first and t < BACK1[layer]):
                                    pe.wait_ge(sem(f"half{layer}"), (t - BACK1[layer]) * units + u + 1)
                            else:
                                o = ps[:, front_bank(layer, q) + n, :]
                                if n == 0 and not fresh:
                                    pe.wait_ge(sem(f"run{layer}"), t - depth + 1)
                            if layer == 0:
                                mm(o, t_ha[slot][:, ks], q_ha[:, cs], 0, 2)
                                last = mm(o, t_e[slot][0:CB + 1, ks], q_he[:, cs], 1, 2)
                            else:
                                keys, queries = ((t_la[slot], q_la), (t_b[slot], q_b))[n // 2]
                                last = mm(o, keys[:, ks], queries[:, (n % 2) * 512:(n % 2 + 1) * 512], 0, 1)
                            if n >= units:
                                last.then_inc(sem(f"s1b_{layer}"), 1)
                        last.then_inc(sem(f"s1_{layer}"), 1)

                if layer == 1:
                    keys1(0, 0, True)
                scores1(0, 0, True)
                scores1(1, 1, True)
                with pe.Fori(1, GROUPS // 2) as i:
                    scores1(2 * i, 0, False)
                    scores1(2 * i + 1, 1, False)
                scores1(GROUPS - 1, 0, False, True)
                pe.wait_ge(sem("lanes"), layer + 1)
                for h in range(heads):
                    last = pe.transpose(ps[:, 4 + h // 4, (h % 4) * P:(h % 4 + 1) * P], run[:, h * P:(h + 1) * P], ident)
                last.then_inc(sem("lanes_t"), 1)
                pe.wait_ge(sem("max_q"), layer + 1)
                pe.transpose(ps[0:heads, 2, 0:P], sm[:, 0:heads], ident).then_inc(sem("max_psum"), 1)
                pe.wait_ge(sem("shift"), layer + 1)

                def values(t, j, slot, skip):
                    if not skip:
                        pe.wait_ge(sem(f"v_sb{layer}"), t - 1 + layer)
                    ks = slice(j * P, (j + 1) * P)
                    n = heads * HD[layer]
                    o = ps[:, v_bank[layer][j], 0:n]
                    mm(o, t_ha[slot][:, ks], wv_ha[:, 0:n], 0, 5)
                    mm(o, t_ha[slot][:, ks], wv_la[:, 0:n], 1, 5)
                    mm(o, t_la[slot][:, ks], wv_ha[:, 0:n], 2, 5)
                    mm(o, t_b[slot][:, ks], wv_hb[:, 0:n], 3, 5)
                    mm(o, t_b[slot][0:CB, ks], wv_lb[:, 0:n], 4, 5).then_inc(sem(f"v_psum{layer}"), 1)

                def scores2(t, j, slot, u, skip):
                    n = t * units2 + u
                    if not skip:
                        pe.wait_ge(sem(f"exp{layer}"), n + 1 - units2)
                    ks = slice(j * P, (j + 1) * P)
                    cs = slice(u * 512, (u + 1) * 512)
                    o = ps[:, s_bank[layer][u], :]
                    if layer == 0:
                        mm(o, t_ha[slot][:, ks], q_ha[:, cs], 0, 5)
                        mm(o, t_ha[slot][:, ks], q_la[:, cs], 1, 5)
                        mm(o, t_la[slot][:, ks], q_ha[:, cs], 2, 5)
                        mm(o, t_b[slot][:, ks], q_b[:, cs], 3, 5)
                        last = mm(o, t_e[slot][0:CB + 1, ks], q_le[:, cs], 4, 5)
                    else:
                        us = slice(u * GK + j * P, u * GK + (j + 1) * P)
                        mm(o, kk[slot][:, us], q_ha[:, cs], 0, 2)
                        last = mm(o, ke[slot][:, us], q_le[:, cs], 1, 2)
                    last.then_inc(sem(f"s2_{layer}"), 1)

                def products(t, j, slot, u, start, stop):
                    pe.wait_ge(sem(f"exp{layer}"), t * units2 + u + 1)
                    if u == 0:
                        pe.wait_ge(sem(f"v_sb{layer}"), t + 1)
                    for k in range(4):
                        h = 4 * u + k
                        e = probs[:, j * 2048 + h * P:j * 2048 + (h + 1) * P]
                        if layer == 0:
                            last = pe.matmul(ps[64 * (k % 2):64 * (k % 2) + 64, 4, (h // 2) * P:(h // 2 + 1) * P],
                                             v_sb[j][:, h * 64:(h + 1) * 64], e,
                                             start=(start and h < 2), stop=stop, skip_group_check=True)
                        else:
                            last = pe.matmul(ps[32 * k:32 * k + 32, 4, u * P:(u + 1) * P], v_sb[j][:, h * 32:(h + 1) * 32],
                                             e, start=(start and u == 0), stop=stop, skip_group_check=True)
                    last.then_inc(sem(f"pv{layer}"), 1)

                def step(g, slot, j, first=False, last=False, keys=True):
                    t = g * GT + j
                    ns, nj = (slot, 1) if j == 0 else (1 - slot, 0)
                    if j == 1 and not last:
                        pe.wait_ge(sem(f"split{layer}"), g + 2)
                    if not last:
                        values(t + 1, nj, ns, layer == 0 and first and slot == 0 and j == 0)
                    if layer == 1 and j == 0 and keys:
                        keys2(g + 1, 1 - slot, False)
                    if layer == 1 and j == 1 and not last:
                        pe.wait_ge(sem("kk"), g + 2)
                    for u in range(units2):
                        if not last:
                            scores2(t + 1, nj, ns, u, False)
                    for u in range(units2):
                        products(t, j, slot, u, first and slot == 0 and j == 0, last)

                def pair(g, slot, first):
                    step(g, slot, 0, first)
                    step(g, slot, 1, first)

                pe.wait_ge(sem(f"split{layer}"), 1)
                if layer == 1:
                    keys2(0, 0, True)
                values(0, 0, 0, True)
                if layer == 1:
                    pe.wait_ge(sem("kk"), 1)
                for u in range(units2):
                    scores2(0, 0, 0, u, True)
                pair(0, 0, True)
                pair(1, 1, True)
                with pe.Fori(1, GROUPS // 2) as i:
                    pair(2 * i, 0, False)
                    pair(2 * i + 1, 1, False)
                step(GROUPS - 1, 0, 0, keys=False)
                step(GROUPS - 1, 0, 1, last=True)

            cross(0)
            pe.wait_ge(sem("lsum"), TILES)
            for h in range(8):
                last = pe.matmul(ps[64 * (h % 2):64 * (h % 2) + 64, 5, (h // 2) * P:(h // 2 + 1) * P], ones[:],
                                 run[:, h * P:(h + 1) * P], start=(h < 2), stop=True, skip_group_check=True)
            last.then_inc(sem("den_psum"), 1)
            pe.wait_ge(sem("ot"), 1)
            for b in range(4):
                last = mm(ps[:, 6, 0:D], qt[:, b * P:(b + 1) * P], wa[:, XQ0["wo"] + b * D:XQ0["wo"] + (b + 1) * D], b, 4)
            last.then_inc(sem("y"), 1)

            turn_x(1, 1, xn)
            pe.wait_ge(sem("la_loaded"), 16)
            for i, name in enumerate(("wq", "wk")):
                for b in range(2):
                    for k in range(DK):
                        c = LA[name] + k * D + b * P
                        mm(ps[:, 0, i * D + b * P:i * D + (b + 1) * P], wlb[:, c:c + P], xt[:, k * P:(k + 1) * P], k, DK)
            for k in range(DK):
                last = mm(ps[:, 1, 0:D], xt[:, k * P:(k + 1) * P], wlb[:, LA["wv"] + k * D:LA["wv"] + (k + 1) * D], k, DK)
            last.then_inc(sem("qkv_psum"), 1)
            pe.wait_ge(sem("k_diag"), 1)
            for c in range(4):
                last = mm(ps[:, 2 + c, :], qt[:, (c // 2) * P:(c // 2 + 1) * P], probs[:, c * 512:(c + 1) * 512], 0, 1)
            last.then_inc(sem("s_a"), 1)
            pe.wait_ge(sem("prob_a"), 1)
            for h in range(16):
                last = pe.transpose(ps[:, 2 + h // 4, (h % 4) * P:(h % 4 + 1) * P], run[:, h * P:(h + 1) * P], ident)
            last.then_inc(sem("pt_psum"), 1)
            pe.wait_ge(sem("pt_lo"), 1)
            pe.wait_ge(sem("pt_hi"), 1)
            for h in range(16):
                last = mm(ps[:, 6, h * 16:(h + 1) * 16], scr[:, h * P:(h + 1) * P], ya[:, h * 16:(h + 1) * 16], 0, 1)
            last.then_inc(sem("o_a"), 1)

            def project(n, src, w, at):
                pe.wait_ge(sem("head_out"), n + 1)
                pe.transpose(ps[:, 7, 0:128], src[:, 0:128], ident)
                pe.transpose(ps[:, 7, 128:256], src[:, 128:256], ident).then_inc(sem("head_t_psum"), 1)
                pe.wait_ge(sem("head_t"), n + 1)
                for k in range(DK):
                    last = mm(ps[:, 5, 0:D], xt[:, k * P:(k + 1) * P], w[:, at + k * D:at + (k + 1) * D], k, DK)
                last.then_inc(sem("y"), 1)

            project(0, yb, wlb, LA["wo"])

            turn_x(2, 2, xn)
            for k in range(DK):
                last = mm(ps[:, 6, 0:E0], xt[:, k * P:(k + 1) * P], cst[:, CONST["rw"] + k * E0:CONST["rw"] + (k + 1) * E0], k, DK)
            last.then_inc(sem("router"), 1)

            def up0(e, slot, par):
                first = isinstance(e, int)
                pe.wait_ge(sem(f"ring{slot}"), 16 * (e // 4 + 1) if first else 4 * (e - slot) + 16)
                if not (first and e < 2):
                    pe.wait_ge(sem("hid0"), e - 1)
                w = ring[:, slot * W0:(slot + 1) * W0]
                for i in range(2):
                    for m in range(F0T):
                        for k in range(DK):
                            c = (i * DK + k) * F0T * P + m * P
                            last = mm(ps[:, 2 * i + par, m * P:(m + 1) * P], w[:, c:c + P], xt[:, k * P:(k + 1) * P], k, DK)
                last.then_inc(sem("up0"), 1)

            def down0(e, slot, par):
                pe.wait_ge(sem("hid0"), e + 1)
                if not (isinstance(e, int) and e < 2):
                    pe.wait_ge(sem("acc0"), e - 1)
                w = ring[:, slot * W0 + 4 * F0T * P:(slot + 1) * W0]
                for m in range(F0T):
                    last = mm(ps[:, 4 + par, 0:D], probs[:, 2048 + par * 1024 + m * P:2048 + par * 1024 + (m + 1) * P],
                              w[:, m * D:(m + 1) * D], m, F0T)
                last.then_inc(sem("down0"), 1)

            up0(0, 0, 0)
            pe.wait_ge(sem("chosen"), 1)
            pe.matmul(ps[:, 6, 32:32 + E0], cst[:, CONST["before"]:CONST["before"] + P], sm[:, 64:64 + E0],
                      start=True, stop=True).then_inc(sem("rank"), 1)
            for e in range(1, 5):
                up0(e, e % 4, e % 2)
                down0(e - 1, (e - 1) % 4, (e - 1) % 2)
            with pe.Fori(1, 4) as i:
                for k in range(1, 5):
                    up0(4 * i + k, k % 4, k % 2)
                    down0(4 * i + k - 1, (k - 1) % 4, (k - 1) % 2)
            down0(E0, 0, 0)

            cross(1)
            pe.wait_ge(sem("o_sb"), 1)
            for u in range(4):
                last = pe.transpose(ps[:, 5, u * P:(u + 1) * P], qt[:, u * P:(u + 1) * P], ident)
            last.then_inc(sem("o_t"), 1)
            project(1, yb, wx1, XQ1["wo"])

            turn_x(4, 4, xn)
            pe.wait_ge(sem("lb_loaded"), 16)
            for i, name in enumerate(("wq", "wk", "wv")):
                for k in range(DK):
                    last = mm(ps[:, i // 2, (i % 2) * D:(i % 2) * D + D], xt[:, k * P:(k + 1) * P],
                              wlb[:, LB[name] + k * D:LB[name] + (k + 1) * D], k, DK)
            last.then_inc(sem("qkv_psum"), 1)
            pe.wait_ge(sem("unit_qk"), 1)
            for b in range(2):
                mm(ps[:, 2, b * P:(b + 1) * P], qt[:, D + b * P:D + (b + 1) * P], ya[:, b * P:(b + 1) * P], 0, 1)
            for b in range(2):
                last = pe.transpose(ps[:, 3, b * P:(b + 1) * P], qt[:, b * P:(b + 1) * P], ident)
            last.then_inc(sem("kv_psum"), 1)
            pe.wait_ge(sem("kv"), 1)
            for b in range(2):
                last = mm(ps[:, 4, b * P:(b + 1) * P], raw[0][:, b * P:(b + 1) * P], raw[0][:, D + b * P:D + (b + 1) * P], 0, 1)
            last.then_inc(sem("lin_psum"), 1)
            pe.wait_ge(sem("lin"), 1)
            for b in range(2):
                last = mm(ps[:, 5, 0:D], yb[:, b * P:(b + 1) * P], wlb[:, LB["wo"] + b * D:LB["wo"] + (b + 1) * D], b, 2)
            last.then_inc(sem("y"), 1)
            turn_x(5, 5, ya)
            pe.wait_ge(sem("ff_loaded"), 16)
            for m in range(F1T):
                for k in range(DK):
                    last = mm(ps[:, m // 4, (m % 4) * P:(m % 4 + 1) * P], wa[:, k * 1024 + m * P:k * 1024 + (m + 1) * P],
                              xt[:, k * P:(k + 1) * P], k, DK)
            last.then_inc(sem("ff_up"), 1)
            pe.wait_ge(sem("ff_hid"), 1)
            for m in range(F1T):
                last = mm(ps[:, 5, 0:D], raw[m // 4][:, (m % 4) * P:(m % 4 + 1) * P],
                          wa[:, 2048 + m * D:2048 + (m + 1) * D], m, F1T)
            last.then_inc(sem("y"), 1)

            turn_x(7, 6, xn)
            for k in range(DK):
                last = mm(ps[:, 6, 0:E1], xt[:, k * P:(k + 1) * P], wlb[:, LB["wr"] + k * E1:LB["wr"] + (k + 1) * E1], k, DK)
            last.then_inc(sem("router"), 1)
            big = (ring[:, 0:W1], ring[:, W1:2 * W1], probs[:], wide[:])

            def up1(e):
                pe.wait_ge(sem(f"big{e % 4}"), 16 * (e // 4 + 1))
                if e >= 2:
                    pe.wait_ge(sem("gelu1"), e - 1)
                for m in range(F1T):
                    for k in range(DK):
                        c = k * F1T * P + m * P
                        last = mm(ps[:, 2 * (e % 2) + m // 4, (m % 4) * P:(m % 4 + 1) * P], big[e % 4][:, c:c + P],
                                  xt[:, k * P:(k + 1) * P], k, DK)
                last.then_inc(sem("up1"), 1)

            def down1(e):
                pe.wait_ge(sem("gelu1"), e + 1)
                if e >= 2:
                    pe.wait_ge(sem("acc1"), e - 1)
                for m in range(F1T):
                    c = DK * F1T * P + m * D
                    last = mm(ps[:, 4 + e % 2, 0:D], wa[:, (e % 2) * 1024 + m * P:(e % 2) * 1024 + (m + 1) * P],
                              big[e % 4][:, c:c + D], m, F1T)
                last.then_inc(sem("down1"), 1)

            up1(0)
            pe.wait_ge(sem("scores_r"), 1)
            pe.transpose(ps[0:E1, 6, 128:256], sm[:, 32:32 + E1], ident).then_inc(sem("scores_t"), 1)
            up1(1)
            pe.wait_ge(sem("picked"), 1)
            pe.transpose(ps[:, 6, 256:256 + E1], sel[:, 3 * P:4 * P], ident[0:E1, 0:E1])
            pe.wait_ge(sem("b2_loaded"), 16)
            mm(ps[:, 7, 0:D], sel[:, 3 * P:4 * P], b2[:], 0, 1).then_inc(sem("weights_psum"), 1)
            for e in range(E1):
                down1(e)
                if e + 2 < E1:
                    up1(e + 2)

        @block.vector
        def _(dve):
            link = chain(dve, "dve_step")
            dve.wait_ge(sem("x_loaded"), 16)

            def norm(n, src, dst, eps, scale=None, shift=None):
                link(dve.bn_stats(stat[:, n, 0:6], src[:]))
                link(dve.bn_aggr(stat[:, n, 6:8], stat[:, n, 0:6]))
                dve.tensor_scalar(stat[:, n, 8:9], stat[:, n, 7:8], eps, None, ALU.add).then_inc(sem("var"), 1)
                dve.wait_ge(sem("std"), n + 1)
                link(dve.reciprocal(stat[:, n, 10:11], stat[:, n, 9:10]))
                last = dve.tensor_scalar(dst[:], src[:], stat[:, n, 6:7], stat[:, n, 10:11], ALU.subtract, ALU.mult)
                if scale is not None:
                    link(last)
                    link(dve.tensor_tensor(dst[:], dst[:], scale, ALU.mult))
                    last = dve.tensor_tensor(dst[:], dst[:], shift, ALU.add)
                last.then_inc(sem("xn"), 1)
                dve.wait_ge(sem("xn"), n + 1)

            def take_xt(k):
                dve.wait_ge(sem("xt_psum"), k + 1)
                dve.tensor_copy(xt[:], ps[:, 7, 0:D]).then_inc(sem("xt"), 1)

            def spread(ap, n):
                return ap.unsqueeze(2).to_broadcast([P, ap.shape[1], n])

            def fold():
                dve.wait_ge(sem("q_psum"), 1)
                link(dve.tensor_scalar(qt[:], ps[:, 0, :], float(HD[0]) ** -0.5, None, ALU.mult))
                for b in range(4):
                    last = dve.tensor_tensor(
                        scr[:, b * 2 * P:(b + 1) * 2 * P].rearrange("p (h q) -> p h q", h=2),
                        qt[:, b * P:(b + 1) * P].unsqueeze(1).to_broadcast([P, 2, P]),
                        spread(cst[:, CONST["mask2"]:CONST["mask2"] + 2], P), ALU.mult)
                last.then_inc(sem("q_diag"), 1)
                for c in range(2):
                    dve.wait_ge(sem("q_folded"), c + 1)
                    b = 1 + 3 * c
                    cs = slice(c * 512, (c + 1) * 512)
                    dve.tensor_copy(q_ha[:, cs], ps[:, b, :])
                    dve.tensor_copy(q_b[:, cs], ps[:, b + 1, :])
                    link(dve.tensor_copy(q_he[:, cs], ps[0:CB + 1, b + 2, :]))
                    dve.tensor_tensor(q_la[:, cs], ps[:, b, :], q_ha[:, cs].bitcast(F32), ALU.subtract)
                    dve.tensor_tensor(q_le[0:CB, cs], ps[0:CB, b + 2, :], q_he[0:CB, cs].bitcast(F32), ALU.subtract)\
                       .then_inc(sem("q_chunk"), 1)

            def queries1():
                dve.wait_ge(sem("q_psum"), 2)
                for u in range(UNITS):
                    link(dve.tensor_scalar(qt[:, u * P:(u + 1) * P], ps[:, 0, u * P:(u + 1) * P],
                                           wx1[:, XQ1["bq"] + u:XQ1["bq"] + u + 1], float(HD[1]) ** -0.5, ALU.add, ALU.mult))
                for u in range(UNITS):
                    last = dve.tensor_tensor(
                        scr[:, u * 512:(u + 1) * 512].rearrange("p (h q) -> p h q", h=4),
                        qt[:, u * P:(u + 1) * P].unsqueeze(1).to_broadcast([P, 4, P]),
                        spread(cst[:, CONST["mask4"]:CONST["mask4"] + 4], P), ALU.mult)
                link(last)
                link(dve.tensor_copy(q_ha[:], scr))
                for b, q in enumerate((q_la, q_b)):
                    dve.tensor_copy(q[0:CB, 0:512], scr[0:CB, b * 1024:b * 1024 + 512])
                    dve.tensor_copy(q[CB:P, 512:1024], scr[CB:P, b * 1024 + 512:(b + 1) * 1024])
                    dve.memset(q[CB:P, 0:512].bitcast(F32), 0.0)
                    dve.memset(q[0:CB, 512:1024].bitcast(F32), 0.0)
                dve.tensor_tensor(q_le[0:CB, :], scr[0:CB, :], q_ha[0:CB, :].bitcast(F32), ALU.subtract)\
                   .then_inc(sem("q_diag"), 1)
                dve.wait_ge(sem("q_diag"), 2)

            def value_parts(n, va, vb):
                link(dve.tensor_copy(wv_ha[:, 0:n], va))
                link(dve.tensor_copy(wv_hb[:, 0:n], vb))
                link(dve.tensor_tensor(wv_la[:, 0:n], va, wv_ha[:, 0:n].bitcast(F32), ALU.subtract))
                link(dve.tensor_tensor(wv_lb[:, 0:n], vb[0:CB, :], wv_hb[0:CB, 0:n].bitcast(F32), ALU.subtract))

            def key_parts():
                ka, kb = wx1[:, XQ1["wka"]:XQ1["wka"] + D], wx1[:, XQ1["wkb"]:XQ1["wkb"] + D]
                two = slice(CB, CB + 2)
                bk = wx1[two, XQ1["bk"]:XQ1["bk"] + D]
                link(dve.tensor_copy(wk_ha[:], ka))
                link(dve.tensor_copy(wk_hb[:], kb))
                link(dve.tensor_copy(wk_he[0:CB, :], kb[0:CB, :]))
                link(dve.tensor_tensor(wk_la[:], ka, wk_ha[:].bitcast(F32), ALU.subtract))
                link(dve.tensor_tensor(wk_le[0:CB, :], kb[0:CB, :], wk_he[0:CB, :].bitcast(F32), ALU.subtract))
                link(dve.tensor_copy(wk_he[two, :], bk))
                link(dve.tensor_tensor(qt[two, 0:D], bk, wk_he[two, :].bitcast(F32), ALU.subtract))
                link(dve.tensor_scalar(qt[two, 0:D], qt[two, 0:D], cst[two, CONST["pick"] + 1:CONST["pick"] + 2], None, ALU.mult))
                link(dve.scalar_tensor_tensor(wk_le[two, :], wk_he[two, :].bitcast(F32),
                                              cst[two, CONST["pick"]:CONST["pick"] + 1], qt[two, 0:D], ALU.mult, ALU.add))
                link(dve.tensor_copy(wk_he[two, :], wk_le[two, :].bitcast(F32)))

            def cross(layer):
                heads = HEADS[layer]
                units2 = heads // 4
                half = heads * 64
                norm(3 * layer, x, xn, 1e-5)
                take_xt(3 * layer)
                if layer == 0:
                    fold()
                else:
                    queries1()
                link(dve.memset(run[:, 0:half], LOWEST))
                run16 = half16[:, 2048:2048 + half]
                link(dve.memset(run16, LOWEST))

                def maxima(g, slot, first):
                    for j in range(GT):
                        t = g * GT + j
                        dve.wait_ge(sem(f"s1_{layer}"), t + 1)
                        if not (first and slot == 0 and j == 0):
                            dve.wait_ge(sem(f"run{layer}"), t)
                        r = run[:, 0:half]
                        q = tile_buffer(layer, slot, j)
                        b = front_bank(layer, q)
                        dve.tensor_tensor(r, ps[:, b:b + half // 512, :].rearrange("p b n -> p (b n)"), r, ALU.max)
                        dve.wait_ge(sem(f"half{layer}"), (t + 1) * UNITS1[layer])
                        dve.tensor_tensor(run16, half16[:, q * half:(q + 1) * half], run16, ALU.max)\
                           .then_inc(sem(f"run{layer}"), 1)

                groups(dve, maxima)
                dve.wait_ge(sem(f"run{layer}"), TILES)
                dve.tensor_copy(run[:, half:2 * half], run16).then_inc(sem("lanes"), 1)
                if layer == 0:
                    value_parts(512, wa[:, XQ0["wva"]:XQ0["wva"] + 512], wa[:, XQ0["wvb"]:XQ0["wvb"] + 512])
                else:
                    value_parts(D, wx1[:, XQ1["wva"]:XQ1["wva"] + D], wx1[:, XQ1["wvb"]:XQ1["wvb"] + D])
                dve.wait_ge(sem("lanes_t"), layer + 1)
                dve.tensor_reduce(sm[:, 0:heads], ps[:, 4:4 + heads // 4, :].rearrange("p b (h n) -> p (b h) n", n=P), AX,
                                  ALU.max).then_inc(sem("max_q"), 1)
                dve.wait_ge(sem("max_psum"), layer + 1)
                dve.tensor_copy(m_t[0:heads, :], ps[0:heads, 2, 0:P]).then_inc(sem("max_t"), 1)

                def split(g, slot, first):
                    dve.wait_ge(sem(f"ctx{slot}"), ctx_count(2 * layer + 1, slot, g))
                    if not first:
                        dve.wait_ge(sem(f"v_psum{layer}"), (g - 1) * GT)
                        if layer == 0:
                            dve.wait_ge(sem("s2_0"), (g - 1) * GT * units2)
                        else:
                            dve.wait_ge(sem("k2"), g - 1)
                    r = raw[slot]
                    dve.tensor_copy(t_ha[slot][:], r[:, 0:GK])
                    dve.tensor_copy(t_e[slot][0:CB, :], r[0:CB, GK:2 * GK])
                    dve.tensor_copy(t_b[slot][:], r[:, GK:2 * GK]).then_inc(sem(f"part{layer}"), 1)
                    dve.wait_ge(sem(f"part{layer}"), g + 1)
                    dve.tensor_tensor(t_la[slot][:], r[:, 0:GK], t_ha[slot][:].bitcast(F32), ALU.subtract)
                    dve.tensor_tensor(t_b[slot][CB:P, :], r[CB:P, GK:2 * GK], t_b[slot][CB:P, :].bitcast(F32),
                                      ALU.subtract).then_inc(sem(f"split{layer}"), 1)

                def keep_values(t, j, first):
                    dve.wait_ge(sem("v_psum1"), t + 1)
                    if not first:
                        dve.wait_ge(sem("pv1"), (t - 1) * units2)
                    dve.tensor_copy(v_sb[j][:].rearrange("p (h w) -> p h w", w=32)[:, :, 0:16],
                                    ps[:, v_bank[1][j], 0:D].rearrange("p (h d) -> p h d", h=16)).then_inc(sem("v_sb1"), 1)

                def keep_keys(g, slot, first):
                    dve.wait_ge(sem("k2"), g + 1)
                    if not first:
                        dve.wait_ge(sem("s2_1"), (g - 1) * GT * units2)
                    keys = [ps[w * CB:(w + 1) * CB, 5, :].rearrange("p (b k) -> p b k", b=2) for w in range(2)]
                    dve.tensor_copy(unit_halves(kk[slot], 0), keys[0])
                    dve.tensor_copy(unit_halves(kk[slot], 1), keys[1]).then_inc(sem("kk_hi"), 1)
                    dve.wait_ge(sem("kk_hi"), g + 1)
                    for w in range(2):
                        dve.tensor_tensor(unit_halves(kk[slot], w, slice(CB, P)), keys[w],
                                          unit_halves(kk[slot], w).bitcast(F32), ALU.subtract)
                    dve.tensor_copy(ke[slot][0:CB, :], kk[slot][0:CB, :].bitcast(F32)).then_inc(sem("kk"), 1)

                def sum_lanes(t, j, first):
                    dve.wait_ge(sem("exp0"), (t + 1) * units2)
                    e = probs[:, j * 2048:j * 2048 + 1024]
                    if first:
                        dve.tensor_copy(run[:, 0:1024], e).then_inc(sem("lsum"), 1)
                    else:
                        dve.wait_ge(sem("lsum"), t)
                        dve.tensor_tensor(run[:, 0:1024], run[:, 0:1024], e, ALU.add).then_inc(sem("lsum"), 1)

                def tile(t, j, first):
                    if layer == 0:
                        sum_lanes(t, j, first and j == 0)
                    else:
                        keep_values(t, j, first)

                def body(g, slot, first, last=False):
                    start = first and slot == 0
                    tile(g * GT, 0, start)
                    if not last:
                        split(g + 1, 1 - slot, start)
                    tile(g * GT + 1, 1, start)
                    if not last and layer == 1:
                        keep_keys(g + 1, 1 - slot, start)

                split(0, 0, True)
                dve.wait_ge(sem("max_row"), 16 * (layer + 1))
                if layer == 0:
                    dve.tensor_tensor(q_le[CB:CB + 1, 0:1024], q_he[CB:CB + 1, :].bitcast(F32),
                                      scr[CB:CB + 1, 0:1024], ALU.subtract).then_inc(sem("shift"), 1)
                else:
                    dve.tensor_scalar(q_le[CB:CB + 1, :], scr[CB:CB + 1, :], -1.0, None, ALU.mult).then_inc(sem("shift"), 1)
                    for s in range(SLOTS):
                        link(dve.memset(ke[s][CB:CB + 1, :].bitcast(F32), 1.0))
                    keep_keys(0, 0, True)
                body(0, 0, True)
                body(1, 1, True)
                with dve.Fori(1, GROUPS // 2) as i:
                    body(2 * i, 0, False)
                    body(2 * i + 1, 1, False)
                body(GROUPS - 1, 0, False, True)
                if layer == 0:
                    dve.wait_ge(sem("xq1_loaded"), 16)
                    key_parts()
                dve.wait_ge(sem(f"pv{layer}"), TILES * units2)

            def add_y(n, bank, bias):
                dve.wait_ge(sem("y"), n + 1)
                link(dve.tensor_tensor(ya[:], ps[:, bank, 0:D], bias, ALU.add))
                dve.tensor_tensor(x[:], x[:], ya[:], ALU.add).then_inc(sem("x_done"), 1)

            def head_t(n):
                dve.wait_ge(sem("head_t_psum"), n + 1)
                dve.tensor_copy(xt[:], ps[:, 7, 0:D]).then_inc(sem("head_t"), 1)

            for s in range(SLOTS):
                link(dve.memset(t_e[s][CB:CB + 2, :].bitcast(F32), 1.0))
            dve.memset(ones[:], 1.0).then_inc(sem("ones"), 1)
            dve.wait_ge(sem("const_loaded"), 16)

            cross(0)
            dve.wait_ge(sem("den_psum"), 1)
            link(dve.reciprocal(probs[:, 0:512], ps[:, 5, :]))
            dve.tensor_tensor(qt[:], ps[:, 4, :], probs[:, 0:512], ALU.mult).then_inc(sem("ot"), 1)
            add_y(0, 6, wa[:, XQ0["bo"]:XQ0["bo"] + D])
            dve.wait_ge(sem("x_done"), 1)

            norm(1, x, xn, 1e-5)
            take_xt(1)
            dve.wait_ge(sem("qkv_psum"), 1)
            link(dve.tensor_scalar(qt[:, 0:D], ps[:, 0, 0:D], 0.25, None, ALU.mult))
            link(dve.tensor_copy(qt[:, D:2 * D], ps[:, 0, D:2 * D]))
            link(dve.tensor_copy(ya[:], ps[:, 1, 0:D]))
            for b in range(2):
                last = dve.tensor_tensor(probs[:, b * 1024:(b + 1) * 1024].rearrange("p (h q) -> p h q", h=8),
                                         qt[:, D + b * P:D + (b + 1) * P].unsqueeze(1).to_broadcast([P, 8, P]),
                                         spread(cst[:, CONST["mask8"]:CONST["mask8"] + 8], P), ALU.mult)
            last.then_inc(sem("k_diag"), 1)
            dve.wait_ge(sem("s_a"), 1)
            run3 = run.rearrange("p (h n) -> p h n", h=16)
            causal = cst[:, CONST["causal"]:CONST["causal"] + P].unsqueeze(1).to_broadcast([P, 16, P])
            link(dve.tensor_tensor(run3, ps[:, 2:6, :].rearrange("p b (h n) -> p (b h) n", n=P), causal, ALU.add))
            link(dve.tensor_reduce(sm[:, 0:16], run3, AX, ALU.max))
            dve.tensor_tensor(run3, run3, spread(sm[:, 0:16], P), ALU.subtract).then_inc(sem("logit_a"), 1)
            dve.wait_ge(sem("prob_a"), 1)
            link(dve.tensor_reduce(sm[:, 16:32], run3, AX, ALU.add))
            link(dve.reciprocal(sm[:, 32:48], sm[:, 16:32]))
            dve.wait_ge(sem("pt_psum"), 1)
            dve.tensor_copy(scr[:, 0:1024], ps[:, 2:4, :].rearrange("p b n -> p (b n)")).then_inc(sem("pt_lo"), 1)
            dve.wait_ge(sem("o_a"), 1)
            dve.tensor_tensor(yb[:].rearrange("p (h d) -> p h d", h=16), ps[:, 6, 0:D].rearrange("p (h d) -> p h d", h=16),
                              spread(sm[:, 32:48], 16), ALU.mult).then_inc(sem("head_out"), 1)
            head_t(0)
            dve.wait_ge(sem("y"), 2)
            dve.tensor_tensor(x[:], ps[:, 5, 0:D], x[:], ALU.add).then_inc(sem("x_done"), 1)
            dve.wait_ge(sem("x_done"), 2)

            def softmax_small(n, width, bias):
                dve.wait_ge(sem("router"), n + 1)
                lg = sm[:, 0:width]
                if bias is None:
                    link(dve.tensor_copy(lg, ps[:, 6, 0:width]))
                else:
                    link(dve.tensor_tensor(lg, ps[:, 6, 0:width], bias, ALU.add))
                link(dve.tensor_reduce(sm[:, 48:49], lg, AX, ALU.max))
                dve.tensor_scalar(lg, lg, sm[:, 48:49], None, ALU.subtract).then_inc(sem("logit_r"), 1)
                dve.wait_ge(sem("prob_r"), n + 1)
                link(dve.tensor_reduce(sm[:, 49:50], sm[:, 16:16 + width], AX, ALU.add))
                link(dve.reciprocal(sm[:, 50:51], sm[:, 49:50]))
                last = dve.tensor_scalar(sm[:, 32:32 + width], sm[:, 16:16 + width], sm[:, 50:51], None, ALU.mult)
                return last

            norm(2, x, xn, 1e-5)
            take_xt(2)
            link(softmax_small(0, E0, cst[:, CONST["rb"]:CONST["rb"] + E0]))
            pr = sm[:, 32:32 + E0]
            link(dve.max(sm[:, 112:120], pr))
            link(dve.max_index(idx[:], sm[:, 112:120], pr))
            link(dve.tensor_copy(sm[:, 120:122], idx[:, 0:2]))
            iota = cst[:, CONST["iota"]:CONST["iota"] + E0]
            link(dve.tensor_scalar(sm[:, 128:144], iota, sm[:, 120:121], None, ALU.is_equal))
            link(dve.tensor_scalar(sm[:, 144:160], iota, sm[:, 121:122], None, ALU.is_equal))
            dve.tensor_tensor(sm[:, 64:80], sm[:, 128:144], sm[:, 144:160], ALU.add).then_inc(sem("chosen"), 1)
            link(dve.tensor_tensor(sm[:, 51:52], sm[:, 112:113], sm[:, 113:114], ALU.add))
            link(dve.tensor_scalar(sm[:, 52:53], sm[:, 51:52], 1e-9, None, ALU.add))
            link(dve.reciprocal(sm[:, 53:54], sm[:, 52:53]))
            link(dve.tensor_scalar(sm[:, 54:56], sm[:, 112:114], sm[:, 53:54], None, ALU.mult))
            link(dve.tensor_scalar(sm[:, 128:144], sm[:, 128:144], sm[:, 54:55], None, ALU.mult))
            link(dve.scalar_tensor_tensor(sm[:, 160:176], sm[:, 144:160], sm[:, 55:56], sm[:, 128:144], ALU.mult, ALU.add))
            dve.wait_ge(sem("rank"), 1)
            link(dve.scalar_tensor_tensor(sm[:, 176:192], ps[:, 6, 32:32 + E0], float(CAP), sm[:, 160:176],
                                          ALU.is_lt, ALU.mult))

            def hidden0(e, par):
                dve.wait_ge(sem("silu"), e + 1)
                if not (isinstance(e, int) and e < 2):
                    dve.wait_ge(sem("down0"), e - 1)
                dve.tensor_tensor(probs[:, 2048 + par * 1024:2048 + par * 1024 + 384], ps[:, 2 + par, 0:384],
                                  probs[:, par * 1024:par * 1024 + 384], ALU.mult).then_inc(sem("hid0"), 1)

            def sum0(e, par):
                dve.wait_ge(sem("down0"), e + 1)
                if isinstance(e, int) and e == 0:
                    dve.tensor_tensor(ya[:], ps[:, 4, 0:D], xn[:], ALU.add).then_inc(sem("acc0"), 1)
                    return
                dve.wait_ge(sem("acc0"), e)
                w = sm[:, 175 + e:176 + e] if isinstance(e, int) else sm[:, bass.ds(e + 175, 1)]
                dve.scalar_tensor_tensor(ya[:], ps[:, 4 + par, 0:D], w, ya[:], ALU.mult, ALU.add)\
                   .then_inc(sem("acc0"), 1)

            hidden0(0, 0)
            for e in range(1, 5):
                hidden0(e, e % 2)
                sum0(e - 1, (e - 1) % 2)
            with dve.Fori(1, 4) as i:
                for k in range(1, 5):
                    hidden0(4 * i + k, k % 2)
                    sum0(4 * i + k - 1, (k - 1) % 2)
            sum0(E0, 0)
            dve.wait_ge(sem("acc0"), E0 + 1)
            dve.tensor_tensor(x[:], x[:], ya[:], ALU.add).then_inc(sem("x_done"), 1)
            dve.wait_ge(sem("x_done"), 3)

            for s in range(SLOTS):
                link(dve.memset(ke[s][CB:CB + 1, :].bitcast(F32), 0.0))
            for i in range(2):
                link(dve.memset(v_sb[i][:], 0.0))
                link(dve.memset(v_sb[i][:].rearrange("p (h w) -> p h w", w=32)[:, :, 16:17], 1.0))
            cross(1)
            dve.tensor_copy(qt[:], ps[:, 4, :]).then_inc(sem("o_sb"), 1)
            dve.wait_ge(sem("o_t"), 1)
            heads = ps[:, 5, :].rearrange("p (h w) -> p h w", w=32)
            link(dve.reciprocal(sm[:, 32:48], heads[:, :, 16:17].rearrange("p h o -> p (h o)")))
            link(dve.tensor_tensor(yb[:].rearrange("p (h d) -> p h d", h=16), heads[:, :, 0:16], spread(sm[:, 32:48], 16),
                                   ALU.mult))
            dve.tensor_tensor(yb[:], yb[:], wx1[:, XQ1["bv"]:XQ1["bv"] + D], ALU.add).then_inc(sem("head_out"), 1)
            head_t(1)
            add_y(2, 5, wx1[:, XQ1["bo"]:XQ1["bo"] + D])
            dve.wait_ge(sem("x_done"), 4)

            def lb(name, n=D):
                return wlb[:, LB[name]:LB[name] + n]

            norm(4, x, xn, 1e-5)
            take_xt(4)
            dve.wait_ge(sem("qkv_psum"), 2)
            link(dve.tensor_tensor(qt[:], ps[:, 0, :], lb("bqk", 512), ALU.add))
            link(dve.tensor_tensor(ya[:], ps[:, 1, 0:D], lb("bv"), ALU.add))
            dve.tensor_scalar(raw[1][:, 0:512], qt[:], 0.0, None, ALU.min).then_inc(sem("elu_in"), 1)
            dve.wait_ge(sem("elu_exp"), 1)
            link(dve.tensor_scalar(raw[0][:, 0:512], raw[1][:, 0:512], -1.0, None, ALU.add))
            link(dve.scalar_tensor_tensor(qt[:], qt[:], 0.0, raw[0][:, 0:512], ALU.max, ALU.add))
            link(dve.tensor_tensor(raw[0][:, 0:512], qt[:], qt[:], ALU.mult))
            dve.tensor_reduce(sm[:, 0:32], raw[0][:, 0:512].rearrange("p (h d) -> p h d", h=32), AX, ALU.add)\
               .then_inc(sem("norm_in"), 1)
            dve.wait_ge(sem("norm_out"), 1)
            link(dve.reciprocal(sm[:, 64:96], sm[:, 32:64]))
            qt3 = qt[:].rearrange("p (h d) -> p h d", h=32)
            dve.tensor_tensor(qt3, qt3, spread(sm[:, 64:96], 16), ALU.mult).then_inc(sem("unit_qk"), 1)
            dve.wait_ge(sem("kv_psum"), 1)
            diag = spread(cst[:, CONST["mask8"]:CONST["mask8"] + 8], 16)
            for b in range(2):
                link(dve.scalar_tensor_tensor(raw[0][:, b * P:(b + 1) * P].rearrange("p (h d) -> p h d", h=8),
                                              ps[:, 2, b * P:(b + 1) * P].rearrange("p (h d) -> p h d", h=8), 0.25, diag,
                                              ALU.mult, ALU.mult))
            dve.tensor_copy(raw[0][:, D:2 * D], ps[:, 3, 0:D]).then_inc(sem("kv"), 1)
            dve.wait_ge(sem("lin_psum"), 1)
            dve.tensor_copy(yb[:], ps[:, 4, 0:D]).then_inc(sem("lin"), 1)
            dve.wait_ge(sem("y"), 4)
            link(dve.tensor_tensor(ya[:], ps[:, 5, 0:D], lb("bo"), ALU.add))
            link(dve.tensor_tensor(yb[:], ya[:], xn[:], ALU.add))
            norm(5, yb, ya, 1e-12, lb("g1"), lb("be1"))
            take_xt(5)
            dve.wait_ge(sem("y"), 5)
            link(dve.tensor_tensor(yb[:], ps[:, 5, 0:D], lb("b2"), ALU.add))
            link(dve.tensor_tensor(yb[:], yb[:], ya[:], ALU.add))
            norm(6, yb, ya, 1e-12, lb("g2"), lb("be2"))
            dve.tensor_tensor(x[:], x[:], ya[:], ALU.add).then_inc(sem("x_done"), 1)
            dve.wait_ge(sem("x_done"), 5)

            norm(7, x, xn, 1e-5)
            take_xt(6)
            softmax_small(1, E1, None).then_inc(sem("scores_r"), 1)
            dve.wait_ge(sem("scores_t"), 1)
            link(dve.tensor_copy(sel[:, 0:P], ps[0:E1, 6, 128:256]))
            link(dve.tensor_copy(sel[:, P:2 * P], ps[0:E1, 6, 128:256]))
            for r in range(TOPK // 8):
                cur, nxt = 1 + r % 2, 1 + (r + 1) % 2
                link(dve.max(sm[0:E1, 64:72], sel[:, cur * P:(cur + 1) * P]))
                link(dve.match_replace(sel[:, nxt * P:(nxt + 1) * P], sm[0:E1, 64:72], sel[:, cur * P:(cur + 1) * P], -1.0))
            dve.scalar_tensor_tensor(sel[:, 3 * P:4 * P], sel[:, nxt * P:(nxt + 1) * P], 0.0, sel[:, 0:P],
                                     ALU.is_lt, ALU.mult).then_inc(sem("picked"), 1)
            dve.wait_ge(sem("weights_psum"), 1)
            link(dve.tensor_copy(sm[:, 80:88], ps[:, 6, 256:264]))
            link(dve.tensor_tensor(x[:], ps[:, 7, 0:D], x[:], ALU.add))
            for e in range(E1):
                dve.wait_ge(sem("down1"), e + 1)
                if e:
                    dve.wait_ge(sem("acc1"), e)
                dve.scalar_tensor_tensor(x[:], ps[:, 4 + e % 2, 0:D], sm[:, 80 + e:81 + e], x[:], ALU.mult, ALU.add)\
                   .then_inc(sem("acc1"), 1)
            dve.wait_ge(sem("acc1"), E1)
            dve.tensor_copy(ya[:], x[:]).then_inc(sem("result"), 1)


def tiles(w, n=P):
    k = w.shape[0] // n
    return w.reshape(k, n, w.shape[1]).transpose(1, 0, 2).reshape(n, -1)


def rows(v):
    return np.broadcast_to(np.asarray(v).reshape(1, -1), (P, np.asarray(v).size))


def twice(w):
    u = w.reshape(w.shape[0], UNITS, 1, CB)
    return np.broadcast_to(u, (w.shape[0], UNITS, 2, CB)).reshape(w.shape[0], -1)


def xq0_pack(wq, wk, wv, wo, bo):
    nb = wq.shape[1] // P
    kt = wk.T.reshape(nb, P, C)
    kt = np.concatenate([kt[:, :, 0:P], kt[:, :, P:], kt[:, :, P:], kt[:, :, P:], np.zeros((nb, P, 1), wk.dtype)], 2)
    return np.concatenate([tiles(wq), kt.transpose(1, 0, 2).reshape(P, -1), wv[0:P], np.concatenate([wv[P:], wv[P:]], 0),
                           tiles(wo), rows(bo)], 1)


def xq1_pack(wq, wk, wv, wo, bo, bq, bk, bv):
    return np.concatenate([tiles(twice(wq)), wk[0:P], np.concatenate([wk[P:], wk[P:]], 0), rows(bk),
                           rows(bv), twice(bq.reshape(1, -1)).reshape(UNITS, P).T, wv[0:P],
                           np.concatenate([wv[P:], wv[P:]], 0), tiles(wo), rows(bo)], 1)


def constants():
    p = np.arange(P)
    f = np.float32
    return (np.eye(P, dtype=f), (p[:, None] < p[None, :]).astype(f),
            np.where(p[None, :] > p[:, None], f(-1e30), f(0)).astype(f),
            (p[:, None] // 64 == np.arange(2)[None, :]).astype(f),
            (p[:, None] // 16 == np.arange(8)[None, :]).astype(f),
            np.broadcast_to(np.arange(E0, dtype=f)[None, :], (P, E0))), (
            (p[:, None] % 64 // 16 == np.arange(4)[None, :]).astype(f),
            (p[:, None] == CB + np.arange(2)[None, :]).astype(f))


def kernel(**inputs):
    import concourse.bacc as bacc
    from concourse.bass_utils import run_bass_kernel_spmd

    a = {k: np.asarray(v) for k, v in inputs.items()}
    ctx = a["ctx_768"].reshape(GROUPS, P, GT, C)
    turned = ctx.transpose(0, 3, 2, 1)
    pack = np.concatenate([turned[:, 0:P].reshape(GROUPS, P, GK),
                           np.concatenate([turned[:, P:], turned[:, P:]], 1).reshape(GROUPS, P, GK)], 2)
    first, last = constants()

    def wide_f(w):
        return np.concatenate([w, np.zeros((*w.shape[:-1], F0T * P - F0), w.dtype)], -1)

    def expert0(g, u, d):
        dp = np.concatenate([d, np.zeros((F0T * P - F0, D), d.dtype)], 0)
        return np.concatenate([tiles(wide_f(g)), tiles(wide_f(u)), tiles(dp)], 1)

    ex0 = np.stack([expert0(a["L0_ffn_sw_gate"], a["L0_ffn_sw_up"], a["L0_ffn_sw_down"])]
                   + [expert0(a["L0_ffn_w_gate"][e], a["L0_ffn_w_up"][e], a["L0_ffn_w_down"][e]) for e in range(E0)])
    ex1 = np.stack([np.concatenate([tiles(a["L1_ffn_W1"][e]), tiles(a["L1_ffn_W2"][e]), a["L1_ffn_b1"][e].reshape(F1T, P).T], 1)
                    for e in range(E1)])
    L1 = {k[8:]: v for k, v in a.items() if k.startswith("L1_attn_")}
    arrays = {
        "x_in": a["x"][0],
        "ctx_in": pack,
        "xq0_in": xq0_pack(a["L0_xattn_Wq"], a["L0_xattn_Wk"], a["L0_xattn_Wv"], a["L0_xattn_Wo"], a["L0_xattn_bo"]),
        "xq1_in": xq1_pack(*(a["L1_xattn_" + n] for n in ("Wq", "Wk", "Wv", "Wo", "bo", "bq", "bk", "bv"))),
        "const_in": np.concatenate([*first, rows(a["L0_ffn_router_b"]), tiles(a["L0_ffn_router_w"]), *last], 1),
        "la_in": np.concatenate([tiles(a["L0_attn_" + n].T) for n in ("Wq", "Wk", "Wv", "Wo")], 1),
        "lb_in": np.concatenate([tiles(L1["Wq"]), tiles(L1["Wk"]), tiles(L1["Wv"]), tiles(L1["Wo"]), tiles(a["L1_ffn_Wr"]),
                                 rows(L1["bq"]), rows(L1["bk"]), rows(L1["bv"]), rows(L1["bo"]), rows(L1["g1"]),
                                 rows(L1["be1"]), rows(L1["b2"]), rows(L1["g2"]), rows(L1["be2"]),
                                 L1["b1"].reshape(F1T, P).T], 1),
        "ff_in": np.concatenate([tiles(L1["W1"]), tiles(L1["W2"])], 1),
        "ex0_in": ex0,
        "ex1_in": ex1,
        "b2_in": a["L1_ffn_b2"],
    }
    nc = bacc.Bacc("TRN2", target_bir_lowering=False, num_devices=1)
    given, aps = {}, []
    for name, v in arrays.items():
        v = np.ascontiguousarray(v)
        given[name] = v
        aps.append(nc.dram_tensor(name, v.shape, mybir.dt.from_np(v.dtype), kind="ExternalInput").ap())
    out = nc.dram_tensor("out", (P, D), F32, kind="ExternalOutput").ap()
    perceiver(nc, *aps, out)
    r = run_bass_kernel_spmd(nc, [given], core_ids=[0])
    return r.results[0]["out"].reshape(1, P, D)
```

```python
from contextlib import ExitStack

import numpy as np

import concourse.bass as bass
from concourse import mybir

F32 = mybir.dt.float32
F32R = mybir.dt.float32r
U32 = mybir.dt.uint32
BF16 = mybir.dt.bfloat16
ALU = mybir.AluOpType
ACT = mybir.ActivationFunctionType
AX = mybir.AxisListType.X

P = 128
D = 256
DK = 2
C = 192
CB = C - P
S = 12544
TILES = S // P
GT = 2
GROUPS = TILES // GT
GK = GT * P
RAW = 2 * GK
UNITS = 4
HEADS = (8, 16)
HD = (64, 16)
SLOTS = 2
F0 = 352
F0T = 3
E0 = 16
CAP = 20
W0 = 4 * F0T * P + F0T * D
F1T = 8
E1 = 8
TOPK = 32
W1 = DK * F1T * P + F1T * D
QS = P + P + CB + 1
LOWEST = -3.0e38


def xq_offsets(layer):
    inner = HEADS[layer] * HD[layer]
    nb = inner // P
    at, o = {}, 0
    for name, n in ((("wq", DK * inner), ("wk", nb * QS)) if layer == 0 else
                    (("wq", DK * 512), ("wka", D), ("wkb", D), ("bk", D), ("bv", D), ("bq", UNITS))) + (
                    ("wva", inner), ("wvb", inner), ("wo", nb * D), ("bo", D)):
        at[name] = o
        o += n
    return at, o


XQ0, XQ0W = xq_offsets(0)
XQ1, XQ1W = xq_offsets(1)
CONST = {"ident": 0, "before": 128, "causal": 256, "mask2": 384, "mask8": 386, "iota": 394, "rb": 410, "rw": 426,
         "mask4": 458, "pick": 462, "slot": 464}
CONSTW = 464 + TOPK
LA = {"wq": 0, "wk": 512, "wv": 1024, "wo": 1536}
LB = {"wq": 0, "wk": 512, "wv": 1024, "wo": 1536, "wr": 2048, "bqk": 2064, "bv": 2576, "bo": 2832,
      "g1": 3088, "be1": 3344, "b2": 3600, "g2": 3856, "be2": 4112, "b1": 4368}
LBW = 4376
FFW = DK * 1024 + F1T * D


def perceiver(nc, x_in, ctx_in, xq0_in, xq1_in, const_in, la_in, lb_in, ff_in, ex0_in, ex1_in, b1_in, own_in, b2_in, k_mem, v_mem, out):
    with ExitStack() as stack:
        def sb(name, shape, dt=F32):
            return stack.enter_context(nc.sbuf_tensor(name, shape, dt))

        names = {}

        def sem(name):
            if name not in names:
                names[name] = stack.enter_context(nc.semaphore(name))
            return names[name]

        ps = stack.enter_context(nc.psum_tensor("ps", [P, 8, 512], F32))
        raw = [sb(f"raw{s}", [P, RAW]) for s in range(SLOTS)]
        t_ha = [sb(f"t_ha{s}", [P, GK], F32R) for s in range(SLOTS)]
        t_la = [sb(f"t_la{s}", [P, GK], F32R) for s in range(SLOTS)]
        t_b = [sb(f"t_b{s}", [P, GK], F32R) for s in range(SLOTS)]
        t_e = [sb(f"t_e{s}", [CB + 2, GK], F32R) for s in range(SLOTS)]
        q_ha = sb("q_ha", [P, 2048], F32R)
        q_la = sb("q_la", [P, 1024], F32R)
        q_b = sb("q_b", [P, 1024], F32R)
        q_he = sb("q_he", [P, 1024], F32R)
        q_le = sb("q_le", [P, 2048], F32R)
        kk = (q_la, q_b)
        ke = (q_he, sb("ke", [P, 1024], F32R))
        probs = sb("probs", [P, W1])
        wide = sb("wide", [P, W1])
        run = wide[:, 0:2048]
        scr = wide[:, 2048:4096]
        half16 = scr.bitcast(BF16)
        ring = sb("ring", [P, 4 * W0])
        wa = sb("wa", [P, XQ0W])
        wx1 = sb("wx1", [P, XQ1W])
        cst = sb("cst", [P, CONSTW])
        wlb = sb("wlb", [P, LBW])
        wv_ha = sb("wv_ha", [P, 512], F32R)
        wv_la = sb("wv_la", [P, 512], F32R)
        wv_hb = sb("wv_hb", [P, 512], F32R)
        wv_lb = sb("wv_lb", [CB, 512], F32R)
        wk_ha = sb("wk_ha", [P, D], F32R)
        wk_la = sb("wk_la", [P, D], F32R)
        wk_hb = sb("wk_hb", [P, D], F32R)
        wk_he = sb("wk_he", [CB + 2, D], F32R)
        wk_le = sb("wk_le", [CB + 2, D], F32R)
        v_sb = [sb(f"v_sb{i}", [P, 512]) for i in range(2)]
        ones = sb("ones", [P, CB])
        x = sb("x", [P, D])
        xn = sb("xn", [P, D])
        xt = sb("xt", [P, D])
        ya = sb("ya", [P, D])
        yb = sb("yb", [P, D])
        qt = sb("qt", [P, 512])
        stat = sb("stat", [P, 8, 12])
        sm = sb("sm", [P, 256])
        idx = sb("idx", [P, 8], U32)
        b2 = sb("b2", [E1, D])
        m_t = sb("m_t", [16, P])
        sel = sb("sel", [E1, 4 * P])

        ident = cst[:, 0:128]

        def pieces(*parts):
            return [t[:, o * 1024:(o + 1) * 1024] for t, n in parts for o in range(n)]

        expert1 = [pieces((ring, 4)), pieces((ring[:, W1:2 * W1], 4)), pieces((probs, 4)), pieces((wide, 4)),
                   pieces((wlb[:, LBW - 2048:LBW], 2)) + pieces((ring, 4))[2:],
                   pieces((wx1[:, 2048:3072], 1)) + pieces((ring[:, W1:2 * W1], 4))[1:],
                   pieces((wx1, 2), (wlb, 2)), pieces((wa, 4))]
        places = [ring[:, i * W0:(i + 1) * W0] for i in range(4)] + [
            wa[:, 0:W0], wa[:, W0:2 * W0], probs[:, 0:W0], wide[:, 0:W0], wlb[:, 0:W0]]
        place0 = [(e % len(places), e // len(places) + 1) for e in range(E0)] + [(len(places) - 1, 2)]
        hot0, gates0, gates0_t = probs[:, W0:W0 + 512], probs[:, W0 + 512:W0 + 1024], probs[:, W0 + 1024:W0 + 1536]
        tokens0 = wide[:, W0:W0 + 1024]
        silu0 = [wide[:, W0 + 1024 + i * F0T * P:W0 + 1024 + (i + 1) * F0T * P] for i in range(2)]
        hid0 = [wlb[:, W0 + i * F0T * P:W0 + (i + 1) * F0T * P] for i in range(2)]
        hid0_t = [wlb[:, W0 + (2 + i) * F0T * P:W0 + (3 + i) * F0T * P] for i in range(2)]
        out0 = [probs[:, W0 + 1536:W0 + 1792], yb[:]]


        def w_sem(e, part):
            return (f"w{part + 1}_{e}", 32) if e in (4, 5) else (f"w_{e}", 64)

        rest = ring[:, 2 * W1:4 * W0]
        one_hot, gates = rest[:, 0:E1 * TOPK], rest[:, E1 * TOPK:2 * E1 * TOPK]
        b1 = rest[0:2 * E1, 2 * E1 * TOPK:2 * E1 * TOPK + 512]
        own = wa[0:2 * E1, FFW:FFW + 512]

        s_bank = ((0, 1), (0, 1, 3, 7))
        v_bank = (2, 3)
        stage = probs[:, 0:2048]
        kv_sb = run
        q_all = probs[:, 2048:4096]
        block = stack.enter_context(nc.Block())

        UNITS1 = (1, 2)
        DEPTH1 = (4, 2)
        BACK1 = (4, 1)

        def tile_buffer(layer, slot, j):
            return 2 * slot + j if layer == 0 else j

        def front_bank(layer, q):
            return q if layer == 0 else 4 * q

        def back_bank(layer, q):
            return 4 + q if layer == 0 else 2

        def unit_halves(tile, odd, rows=slice(0, CB)):
            return tile[rows, :].rearrange("p (b w k) -> p w b k", w=2, k=GK)[:, odd]

        def chain(eng, name):
            count = [0]

            def link(ins):
                count[0] += 1
                ins.then_inc(sem(name), 1)
                eng.wait_ge(sem(name), count[0])
            return link

        def ctx_count(phase, slot, g):
            per_phase = (GROUPS + 1) // 2 if slot == 0 else GROUPS // 2
            return 16 * (phase * per_phase + 1) + 8 * (g - slot)

        def kv_count(slot, g):
            return 16 + 8 * (g - slot)

        def groups(eng, body):
            body(0, 0, True)
            body(1, 1, True)
            with eng.Fori(1, GROUPS // 2) as i:
                body(2 * i, 0, False)
                body(2 * i + 1, 1, False)
            body(GROUPS - 1, 0, False)

        @block.sync
        def _(sp):
            sp.dma_start(x[:], x_in).then_inc(sem("x_loaded"), 16)
            sp.dma_start(cst[:], const_in).then_inc(sem("const_loaded"), 16)
            wk0 = XQ0["wk"]
            sp.dma_start(wa[:, 0:wk0], xq0_in[:, 0:wk0]).then_inc(sem("wq0_loaded"), 16)
            sp.dma_start(wa[:, wk0:XQ0W], xq0_in[:, wk0:XQ0W]).then_inc(sem("xq0_loaded"), 16)
            def load(layer, g, slot, first):
                if not first:
                    sp.wait_ge(sem(f"hi{layer}"), g - 1)
                sp.dma_start(raw[slot][:], ctx_in[g]).then_inc(sem(f"ctx{slot}"), 16)

            def load_all(g, slot, first):
                if not first:
                    sp.wait_ge(sem("split0"), g - 1)
                sp.dma_start(raw[slot][:], ctx_in[g]).then_inc(sem(f"ctx{slot}"), 16)

            def store_kv(g, slot):
                sp.wait_ge(sem("staged"), 2 * g + 2)
                at = slot * 1024
                sp.dma_start(v_mem[g], stage[:, at:at + 512]).then_inc(sem(f"kv_out{slot}"), 16)
                sp.dma_start(k_mem[g], stage[:, at + 512:at + 1024]).then_inc(sem(f"kv_out{slot}"), 16)

            def load_kv(g, slot, first):
                at = slot * 1024
                if not first:
                    sp.wait_ge(sem("kk"), g - 1)
                sp.dma_start(kv_sb[:, at + 512:at + 1024], k_mem[g]).then_inc(sem(f"k_in{slot}"), 16)
                if not first:
                    sp.wait_ge(sem("v_sb1"), (g - 1) * GT)
                sp.dma_start(kv_sb[:, at:at + 512], v_mem[g]).then_inc(sem(f"v_in{slot}"), 16)

            def max_row(layer):
                sp.wait_ge(sem("max_t"), layer + 1)
                sp.dma_start(scr[CB:CB + 1, 0:HEADS[layer] * P], m_t[0:HEADS[layer], :]).then_inc(sem("max_row"), 16)

            groups(sp, lambda g, slot, first: load(0, g, slot, first))
            sp.wait_ge(sem("hi0"), GROUPS)
            load_all(0, 0, True)
            load_all(1, 1, True)
            max_row(0)
            with sp.Fori(1, GROUPS // 2) as i:
                load_all(2 * i, 0, False)
                load_all(2 * i + 1, 1, False)
            load_all(GROUPS - 1, 0, False)
            sp.wait_ge(sem("split0"), GROUPS)
            load(1, 0, 0, True)
            load(1, 1, 1, True)
            with sp.Fori(1, GROUPS // 2) as i:
                load(1, 2 * i, 0, False)
                store_kv(2 * i - 2, 0)
                load(1, 2 * i + 1, 1, False)
                store_kv(2 * i - 1, 1)
            load(1, GROUPS - 1, 0, False)
            store_kv(GROUPS - 3, 0)
            store_kv(GROUPS - 2, 1)
            store_kv(GROUPS - 1, 0)
            sp.wait_ge(sem("kv_out0"), 2 * kv_count(0, GROUPS - 1))
            sp.wait_ge(sem("kv_out1"), 2 * kv_count(1, GROUPS - 2))
            sp.wait_ge(sem("lanes_t"), 2)
            load_kv(0, 0, True)
            load_kv(1, 1, True)
            max_row(1)
            with sp.Fori(1, GROUPS // 2) as i:
                load_kv(2 * i, 0, False)
                load_kv(2 * i + 1, 1, False)
            load_kv(GROUPS - 1, 0, False)
            sp.wait_ge(sem("result"), 1)
            sp.dma_start(out, x[:]).then_inc(sem("stored"), 16)
            sp.wait_ge(sem("stored"), 16)

        @block.gpsimd
        def _(pool):

            def load0(e):
                place = place0[e][0]
                pool.dma_start(places[place], ex0_in[e]).then_inc(sem(f"place{place}"), 16)

            one = ones[:, 0:1].to_broadcast([P, GK])

            def round_hi(g, slot, first):
                pool.wait_ge(sem(f"ctx{slot}"), ctx_count(0, slot, g))
                if not first:
                    pool.wait_ge(sem("s1b_0"), (g - 1) * GT * UNITS1[0])
                pool.tensor_tensor(t_e[slot][0:CB, :], raw[slot][0:CB, GK:2 * GK], one[0:CB], ALU.mult)
                pool.tensor_tensor(t_ha[slot][:], raw[slot][:, 0:GK], one, ALU.mult).then_inc(sem("hi0"), 1)

            def split_all(g, slot, first):
                pool.wait_ge(sem(f"ctx{slot}"), ctx_count(2, slot, g))
                if not first:
                    pool.wait_ge(sem("v1"), g - 1)
                r = raw[slot]
                pool.tensor_tensor(t_e[slot][0:CB, :], r[0:CB, GK:2 * GK], one[0:CB], ALU.mult)
                pool.tensor_tensor(t_ha[slot][:], r[:, 0:GK], one, ALU.mult)
                pool.tensor_tensor(t_b[slot][:], r[:, GK:2 * GK], one, ALU.mult).then_inc(sem("part1"), 1)
                pool.wait_ge(sem("part1"), 2 * g + 1)
                pool.tensor_tensor(t_la[slot][:], r[:, 0:GK], t_ha[slot][:].bitcast(F32), ALU.subtract)\
                    .then_inc(sem("part1"), 1)
                pool.wait_ge(sem("part1"), 2 * g + 2)
                pool.tensor_tensor(t_b[slot][CB:P, :], r[CB:P, GK:2 * GK], t_b[slot][CB:P, :].bitcast(F32),
                                   ALU.subtract).then_inc(sem("hi1"), 1)
                pool.wait_ge(sem("hi1"), g + 1)

            pool.wait_ge(sem("ones"), 1)
            groups(pool, round_hi)
            pool.wait_ge(sem("shift"), 1)
            pool.dma_start(wlb[:, 0:2048], la_in).then_inc(sem("la_loaded"), 16)
            pool.dma_start(wx1[:], xq1_in).then_inc(sem("xq1_loaded"), 16)
            pool.dma_start(b2[:], b2_in).then_inc(sem("b2_loaded"), 16)
            for e in range(4):
                load0(e)
            pool.wait_ge(sem("x_done"), 1)
            load0(4)
            load0(5)
            pool.wait_ge(sem("s_a"), 4)
            load0(6)
            pool.wait_ge(sem("o_a"), 1)
            load0(7)
            pool.wait_ge(sem("x_done"), 2)
            load0(8)
            pool.wait_ge(sem("down_s"), 1)
            load0(9)
            pool.wait_ge(sem("down0"), 1)
            for e in range(10, 14):
                load0(e)
            pool.wait_ge(sem("down0"), 2)
            for e in range(14, E0 + 1):
                load0(e)
            pool.wait_ge(sem("split0"), GROUPS)
            pool.wait_ge(sem("pv0"), 2 * TILES)
            groups(pool, split_all)
            pool.wait_ge(sem("lanes"), 2)
            for s in range(SLOTS):
                pool.memset(ke[s][CB:CB + 1, :].bitcast(F32), 1.0).then_inc(sem("ke_ones"), 1)
            pool.wait_ge(sem("down0"), 4)
            pool.wait_ge(sem("x_done"), 3)

            def load1(e, some=range(4)):
                for i in some:
                    pool.dma_start(expert1[e][i], ex1_in[e, :, i * 1024:(i + 1) * 1024])\
                        .then_inc(sem(w_sem(e, i // 2)[0]), 16)

            pool.dma_start(b1, b1_in).then_inc(sem("b1_loaded"), 16)
            pool.dma_start(own, own_in).then_inc(sem("own_loaded"), 16)
            later = [(wlb, lb_in, o, min(o + 1024, LBW), "lb_loaded") for o in range(0, LBW, 1024)]
            later += [(wa, ff_in, o, o + 1024, "ff_loaded") for o in range(0, FFW, 1024)]
            later += [(e, i) for e in range(2) for i in range(4)]
            for n, item in enumerate(later):
                pool.wait_ge(sem("v_sb1"), 4 + 2 * n)
                if len(item) == 2:
                    load1(item[0], (item[1],))
                else:
                    place, src, lo, hi, name = item
                    pool.dma_start(place[:, lo:hi], src[:, lo:hi]).then_inc(sem(name), 16)
            pool.wait_ge(sem("x_done"), 4)
            load1(2)
            load1(3)
            load1(5, range(1))
            load1(6, range(2))
            pool.wait_ge(sem("y"), 4)
            load1(6, range(2, 4))
            pool.wait_ge(sem("y"), 5)
            load1(7)
            pool.wait_ge(sem("x_done"), 5)
            load1(4, range(2))
            pool.wait_ge(sem("up1"), 2)
            load1(5, range(1, 2))
            pool.wait_ge(sem("down1"), 1)
            load1(4, range(2, 4))
            load1(5, range(2, 4))

        @block.scalar
        def _(act):
            def root(n):
                act.wait_ge(sem("var"), n + 1)
                act.activation(stat[:, n, 9:10], stat[:, n, 8:9], ACT.Sqrt).then_inc(sem("std"), 1)

            def keep_half(layer, t, q, first):
                units, depth = UNITS1[layer], DEPTH1[layer]
                if not first:
                    act.wait_ge(sem(f"run{layer}"), t - depth + 1)
                for u in range(units):
                    act.wait_ge(sem(f"s1b_{layer}"), t * units + u + 1)
                    c = (q * units + u) * 512
                    act.copy(half16[:, c:c + 512], ps[:, back_bank(layer, q) + u, :]).then_inc(sem(f"half{layer}"), 1)

            def exps(layer, t, j, first):
                units = HEADS[layer] // 4
                if layer == 0:
                    act.wait_ge(sem("v_psum0"), t + 1)
                    if not first:
                        act.wait_ge(sem("pv0"), (t - 1) * units)
                    act.copy(v_sb[j][:], ps[:, v_bank[j], :]).then_inc(sem("v_sb0"), 1)
                    if not first:
                        act.wait_ge(sem("lsum"), t - 1)
                for u in range(units):
                    n = t * units + u
                    act.wait_ge(sem(f"s2_{layer}"), n + 1)
                    if not first:
                        act.wait_ge(sem(f"pv{layer}"), n + 1 - 2 * units)
                    act.activation(probs[:, j * 2048 + u * 512:j * 2048 + (u + 1) * 512], ps[:, s_bank[layer][u], :],
                                   ACT.Exp).then_inc(sem(f"exp{layer}"), 1)

            def keep_keys(g, slot, first):
                act.wait_ge(sem("k1"), g + 1)
                if not first:
                    act.wait_ge(sem("s1b_1"), (g - 1) * GT * UNITS1[1])
                act.copy(ke[slot][:, 0:512], ps[:, 6, :]).then_inc(sem("keys1"), 1)
                if not first:
                    act.wait_ge(sem(f"kv_out{slot}"), 2 * kv_count(slot, g - 2))
                act.copy(stage[:, slot * 1024 + 512:(slot + 1) * 1024], ps[:, 6, :]).then_inc(sem("staged"), 1)

            def keep_values(g, slot):
                act.wait_ge(sem("v1"), g + 1)
                act.copy(stage[:, slot * 1024:slot * 1024 + 512], ps[:, 7, :]).then_inc(sem("staged"), 1)

            def pass1(layer):
                def body(g, slot, first, last=False):
                    if layer == 1 and not last:
                        keep_keys(g + 1, 1 - slot, first and slot == 0)
                    for j in range(GT):
                        q = tile_buffer(layer, slot, j)
                        keep_half(layer, g * GT + j, q, first and (slot == 0 or layer == 0))
                        if layer == 1 and j == 0 and not last:
                            keep_values(g + 1, 1 - slot)
                if layer == 1:
                    keep_keys(0, 0, True)
                    keep_values(0, 0)
                body(0, 0, True)
                body(1, 1, True)
                with act.Fori(1, GROUPS // 2) as i:
                    body(2 * i, 0, False)
                    body(2 * i + 1, 1, False)
                body(GROUPS - 1, 0, False, True)

            def pass2(layer):
                def body(g, slot, first):
                    for j in range(GT):
                        exps(layer, g * GT + j, j, first and slot == 0)
                groups(act, body)

            def cross(layer):
                root(3 * layer)
                pass1(layer)
                if layer == 1:
                    act.wait_ge(sem("q_all"), 1)
                    act.copy(q_ha[:], q_all).then_inc(sem("q_hi"), 1)
                pass2(layer)

            cross(0)
            root(1)
            for c in range(4):
                act.wait_ge(sem("logit_a"), c + 1)
                act.activation(run[:, c * 512:(c + 1) * 512], run[:, c * 512:(c + 1) * 512], ACT.Exp)\
                   .then_inc(sem("prob_a"), 1)
            for c in range(4):
                act.wait_ge(sem("pt_psum"), c + 1)
                act.copy(scr[:, c * 512:(c + 1) * 512], ps[:, 2 + c, :]).then_inc(sem("pt"), 1)
            root(2)
            act.wait_ge(sem("logit_r"), 1)
            act.activation(sm[:, 16:32], sm[:, 0:16], ACT.Exp).then_inc(sem("prob_r"), 1)

            act.wait_ge(sem("up_s"), 1)
            act.activation(silu0[0], ps[:, 0, 0:F0T * P], ACT.Silu).then_inc(sem("silu_s"), 1)
            for b in range(4):
                act.wait_ge(sem("up0"), b + 1)
                act.wait_ge(sem("hid_s"), 1)
                if b >= 2:
                    act.wait_ge(sem("hid0"), b - 1)
                act.activation(silu0[b % 2], ps[:, 2 + 2 * (b % 2), 0:F0T * P], ACT.Silu).then_inc(sem("silu"), 1)

            cross(1)
            root(4)
            act.wait_ge(sem("elu_in"), 1)
            act.activation(raw[1][:, 0:512], raw[1][:, 0:512], ACT.Exp).then_inc(sem("elu_exp"), 1)
            act.wait_ge(sem("norm_in"), 1)
            act.activation(sm[:, 32:64], sm[:, 0:32], ACT.Sqrt).then_inc(sem("norm_out"), 1)
            root(5)
            act.wait_ge(sem("ff_up"), 1)
            for m in range(F1T):
                last = act.activation(raw[m // 4][:, (m % 4) * P:(m % 4 + 1) * P],
                                      ps[:, m // 4, (m % 4) * P:(m % 4 + 1) * P], ACT.Gelu,
                                      bias=wlb[:, LB["b1"] + m:LB["b1"] + m + 1])
            last.then_inc(sem("ff_hid"), 1)
            root(6)
            root(7)
            act.wait_ge(sem("logit_r"), 2)
            act.activation(sm[:, 16:24], sm[:, 0:8], ACT.Exp).then_inc(sem("prob_r"), 1)
            for i in range(4):
                act.wait_ge(sem("up1"), i + 1)
                if i >= 2:
                    act.wait_ge(sem("h_t"), i - 1)
                act.activation(raw[i % 2][:], ps[:, i, :], ACT.Gelu).then_inc(sem("gelu1"), 1)

        @block.tensor
        def _(pe):
            def keep_warm(n, bank=3):
                for _ in range(n):
                    pe.matmul(ps[:, bank, 0:P], ident, ident, start=True, stop=True)

            def turn_x(n, k, src, fill=10, bank=3):
                keep_warm(fill, bank)
                pe.wait_ge(sem("xn"), n + 1)
                pe.transpose(ps[:, 7, 0:128], src[:, 0:128], ident)
                pe.transpose(ps[:, 7, 128:256], src[:, 128:256], ident).then_inc(sem("xt_psum"), 1)
                keep_warm(2, bank)
                pe.wait_ge(sem("xt"), k + 1)

            def mm(o, l, r, k, n, **more):
                return pe.matmul(o, l, r, start=(k == 0), stop=(k == n - 1), **more)

            def fold():
                pe.wait_ge(sem("wq0_loaded"), 16)
                inner = HEADS[0] * HD[0]
                for b in range(4):
                    for k in range(DK):
                        c = XQ0["wq"] + k * inner + b * P
                        last = mm(ps[:, 0, b * P:(b + 1) * P], wa[:, c:c + P], xt[:, k * P:(k + 1) * P], k, DK)
                last.then_inc(sem("q_psum"), 1)
                pe.wait_ge(sem("q_diag"), 1)
                pe.wait_ge(sem("xq0_loaded"), 16)
                for c in range(2):
                    for part, (o, m) in enumerate(((0, P), (P, P), (2 * P, CB + 1))):
                        for b in range(2 * c, 2 * c + 2):
                            last = mm(ps[0:m, 1 + 3 * c + part, (b % 2) * 256:(b % 2) * 256 + 256],
                                      wa[:, XQ0["wk"] + b * QS + o:XQ0["wk"] + b * QS + o + m],
                                      scr[:, b * 256:(b + 1) * 256], 0, 1)
                    last.then_inc(sem("q_folded"), 1)
                pe.wait_ge(sem("q_chunk"), 2)

            def queries1():
                pe.wait_ge(sem("xq1_loaded"), 16)
                for u in range(UNITS):
                    for k in range(DK):
                        c = XQ1["wq"] + k * 512 + u * P
                        last = mm(ps[:, 0, u * P:(u + 1) * P], wx1[:, c:c + P], xt[:, k * P:(k + 1) * P], k, DK)
                last.then_inc(sem("q_psum"), 1)

            def keys1(g, slot, first):
                pe.wait_ge(sem("hi1"), g + 1)
                if not first:
                    pe.wait_ge(sem("keys1"), g)
                    pe.wait_ge(sem("staged"), 2 * g - 1)
                for b in range(2):
                    o = ps[:, 6, b * GK:(b + 1) * GK]
                    ws = slice(b * P, (b + 1) * P)
                    mm(o, wk_ha[:, ws], t_ha[slot][:], 0, 5)
                    mm(o, wk_la[:, ws], t_ha[slot][:], 1, 5)
                    mm(o, wk_ha[:, ws], t_la[slot][:], 2, 5)
                    mm(o, wk_hb[:, ws], t_b[slot][:], 3, 5)
                    last = mm(o, wk_le[:, ws], t_e[slot][:], 4, 5)
                last.then_inc(sem("k1"), 1)

            def values1(g, slot, first):
                if not first:
                    pe.wait_ge(sem("staged"), 2 * g)
                for j in range(GT):
                    ks = slice(j * P, (j + 1) * P)
                    o = ps[:, 7, j * D:(j + 1) * D]
                    mm(o, t_ha[slot][:, ks], wv_ha[:, 0:D], 0, 5)
                    mm(o, t_ha[slot][:, ks], wv_la[:, 0:D], 1, 5)
                    mm(o, t_la[slot][:, ks], wv_ha[:, 0:D], 2, 5)
                    mm(o, t_b[slot][:, ks], wv_hb[:, 0:D], 3, 5)
                    last = mm(o, t_b[slot][0:CB, ks], wv_lb[:, 0:D], 4, 5)
                last.then_inc(sem("v1"), 1)

            def cross(layer):
                heads = HEADS[layer]
                units2 = heads // 4
                turn_x(3 * layer, 3 * layer, xn, fill=(0, 11)[layer])
                if layer == 0:
                    fold()
                else:
                    queries1()

                def scores1(g, slot, first, after=False):
                    if layer == 0:
                        pe.wait_ge(sem("hi0"), g + 1)
                    else:
                        if not after:
                            keys1(g + 1, 1 - slot, False)
                        pe.wait_ge(sem("keys1"), g + 1)
                    units, depth = UNITS1[layer], DEPTH1[layer]
                    for j in range(GT):
                        t = g * GT + j
                        q = tile_buffer(layer, slot, j)
                        ks = slice(j * P, (j + 1) * P)
                        fresh = first and t < depth
                        for n in range(2 * units):
                            cs = slice(n * 512, (n + 1) * 512)
                            if n >= units:
                                u = n - units
                                o = ps[:, back_bank(layer, q) + u, :]
                                if not (first and t < BACK1[layer]):
                                    pe.wait_ge(sem(f"half{layer}"), (t - BACK1[layer]) * units + u + 1)
                            else:
                                o = ps[:, front_bank(layer, q) + n, :]
                                if n == 0 and not fresh:
                                    pe.wait_ge(sem(f"front{layer}"), t - depth + 1)
                            if layer == 0:
                                mm(o, t_ha[slot][:, ks], q_ha[:, cs], 0, 2)
                                last = mm(o, t_e[slot][0:CB + 1, ks], q_he[0:CB + 1, cs], 1, 2)
                            else:
                                b, w = divmod(n, 2)
                                last = mm(o, ke[slot][:, b * GK + j * P:b * GK + (j + 1) * P],
                                          (q_la, q_b)[b][:, w * 512:(w + 1) * 512], 0, 1)
                            if n >= units:
                                last.then_inc(sem(f"s1b_{layer}"), 1)
                            elif n == units - 1:
                                last.then_inc(sem(f"s1a_{layer}"), 1)
                        if layer == 1 and j == 0 and not after:
                            values1(g + 1, 1 - slot, False)

                if layer == 1:
                    keys1(0, 0, True)
                    values1(0, 0, True)
                    pe.wait_ge(sem("q_diag"), 2)
                scores1(0, 0, True)
                scores1(1, 1, True)
                with pe.Fori(1, GROUPS // 2) as i:
                    scores1(2 * i, 0, False)
                    scores1(2 * i + 1, 1, False)
                scores1(GROUPS - 1, 0, False, True)

                def turn_lanes(heads, bank):
                    for n, h in enumerate(heads):
                        last = pe.transpose(ps[:, bank + n // 4, (n % 4) * P:(n % 4 + 1) * P],
                                            run[:, h * P:(h + 1) * P], ident)
                    return last

                pe.wait_ge(sem(f"front{layer}"), TILES)
                turn_lanes(range(heads // 2), (2, 6)[layer]).then_inc(sem("lanes_f"), 1)
                pe.wait_ge(sem("lanes"), layer + 1)
                turn_lanes(range(heads // 2, heads), (3, 0)[layer]).then_inc(sem("lanes_t"), 1)
                keep_warm((4, 8)[layer], 5)
                pe.wait_ge(sem("max_q"), layer + 1)
                pe.transpose(ps[0:heads, 4, 0:P], sm[:, 0:heads], ident).then_inc(sem("max_psum"), 1)

                def values(t, j, slot, skip):
                    if not skip:
                        pe.wait_ge(sem("v_sb0"), t - 1)
                    ks = slice(j * P, (j + 1) * P)
                    o = ps[:, v_bank[j], :]
                    mm(o, t_ha[slot][:, ks], wv_ha[:], 0, 5)
                    mm(o, t_ha[slot][:, ks], wv_la[:], 1, 5)
                    mm(o, t_la[slot][:, ks], wv_ha[:], 2, 5)
                    mm(o, t_b[slot][:, ks], wv_hb[:], 3, 5)
                    mm(o, t_b[slot][0:CB, ks], wv_lb[:], 4, 5).then_inc(sem("v_psum0"), 1)

                def scores2(t, j, slot, u, skip):
                    n = t * units2 + u
                    if not skip:
                        pe.wait_ge(sem(f"exp{layer}"), n + 1 - units2)
                    ks = slice(j * P, (j + 1) * P)
                    cs = slice(u * 512, (u + 1) * 512)
                    o = ps[:, s_bank[layer][u], :]
                    if layer == 0:
                        mm(o, t_ha[slot][:, ks], q_ha[:, cs], 0, 5)
                        mm(o, t_ha[slot][:, ks], q_la[:, cs], 1, 5)
                        mm(o, t_la[slot][:, ks], q_ha[:, cs], 2, 5)
                        mm(o, t_b[slot][:, ks], q_b[:, cs], 3, 5)
                        if skip and u == 0:
                            pe.wait_ge(sem("shift"), 1)
                        last = mm(o, t_e[slot][0:CB + 1, ks], q_le[0:CB + 1, cs], 4, 5)
                    else:
                        us = slice(u * GK + j * P, u * GK + (j + 1) * P)
                        mm(o, kk[slot][:, us], q_ha[:, cs], 0, 2)
                        if skip and u == 0:
                            pe.wait_ge(sem("ke_ones"), 2)
                            pe.wait_ge(sem("shift"), 2)
                        last = mm(o, ke[slot][0:CB + 1, us], q_le[0:CB + 1, cs], 1, 2)
                    last.then_inc(sem(f"s2_{layer}"), 1)

                def products(t, j, slot, u, start, stop):
                    pe.wait_ge(sem(f"exp{layer}"), t * units2 + u + 1)
                    if u == 0:
                        pe.wait_ge(sem(f"v_sb{layer}"), t + 1)
                    for k in range(4):
                        h = 4 * u + k
                        e = probs[:, j * 2048 + h * P:j * 2048 + (h + 1) * P]
                        if layer == 0:
                            last = pe.matmul(ps[64 * (k % 2):64 * (k % 2) + 64, 4, (h // 2) * P:(h // 2 + 1) * P],
                                             v_sb[j][:, h * 64:(h + 1) * 64], e,
                                             start=(start and h < 2), stop=stop, skip_group_check=True)
                        else:
                            last = pe.matmul(ps[32 * k:32 * k + 32, 4, u * P:(u + 1) * P], v_sb[j][:, h * 32:(h + 1) * 32],
                                             e, start=(start and u == 0), stop=stop, skip_group_check=True)
                    last.then_inc(sem(f"pv{layer}"), 1)

                def step(g, slot, j, first=False, last=False):
                    t = g * GT + j
                    ns, nj = (slot, 1) if j == 0 else (1 - slot, 0)
                    if j == 1 and not last:
                        pe.wait_ge(sem("split0" if layer == 0 else "kk"), g + 2)
                    if layer == 0 and not last:
                        values(t + 1, nj, ns, first and slot == 0 and j == 0)
                    for u in range(units2):
                        if not last:
                            scores2(t + 1, nj, ns, u, False)
                    for u in range(units2):
                        products(t, j, slot, u, first and slot == 0 and j == 0, last)

                def pair(g, slot, first):
                    step(g, slot, 0, first)
                    step(g, slot, 1, first)

                keep_warm((4, 12)[layer], 5)
                pe.wait_ge(sem("split0" if layer == 0 else "kk"), 1)
                if layer == 0:
                    values(0, 0, 0, True)
                for u in range(units2):
                    scores2(0, 0, 0, u, True)
                pair(0, 0, True)
                pair(1, 1, True)
                with pe.Fori(1, GROUPS // 2) as i:
                    pair(2 * i, 0, False)
                    pair(2 * i + 1, 1, False)
                step(GROUPS - 1, 0, 0)
                step(GROUPS - 1, 0, 1, last=True)

            pe.wait_ge(sem("const_loaded"), 16)
            cross(0)
            pe.wait_ge(sem("lsum"), TILES)
            for h in range(8):
                last = pe.matmul(ps[64 * (h % 2):64 * (h % 2) + 64, h // 2, 0:P], ones[:],
                                 run[:, h * P:(h + 1) * P], start=True, stop=True, skip_group_check=True)
                if h % 2 == 1:
                    last.then_inc(sem("den_psum"), 1)
            keep_warm(4, 7)
            for b in range(4):
                pe.wait_ge(sem("ot"), b + 1)
                last = mm(ps[:, 6, 0:D], qt[:, b * P:(b + 1) * P], wa[:, XQ0["wo"] + b * D:XQ0["wo"] + (b + 1) * D], b, 4)
            last.then_inc(sem("y"), 1)

            turn_x(1, 1, xn)
            pe.wait_ge(sem("la_loaded"), 16)
            for i, name in enumerate(("wq", "wk")):
                for b in range(2):
                    for k in range(DK):
                        c = LA[name] + k * D + b * P
                        mm(ps[:, 0, i * D + b * P:i * D + (b + 1) * P], wlb[:, c:c + P], xt[:, k * P:(k + 1) * P], k, DK)
            for k in range(DK):
                last = mm(ps[:, 1, 0:D], xt[:, k * P:(k + 1) * P], wlb[:, LA["wv"] + k * D:LA["wv"] + (k + 1) * D], k, DK)
            last.then_inc(sem("qkv_psum"), 1)
            keep_warm(14)
            pe.wait_ge(sem("k_diag"), 1)
            for c in range(4):
                mm(ps[:, 2 + c, :], qt[:, (c // 2) * P:(c // 2 + 1) * P], probs[:, c * 512:(c + 1) * 512], 0, 1)\
                    .then_inc(sem("s_a"), 1)
            keep_warm(5, 7)
            for c in range(4):
                pe.wait_ge(sem("prob_a"), c + 1)
                for h in range(4 * c, 4 * c + 4):
                    last = pe.transpose(ps[:, 2 + c, (h % 4) * P:(h % 4 + 1) * P], run[:, h * P:(h + 1) * P], ident)
                last.then_inc(sem("pt_psum"), 1)
            for c in range(4):
                pe.wait_ge(sem("pt"), c + 1)
                for k in range(4):
                    h = 4 * c + k
                    last = pe.matmul(ps[32 * k:32 * k + 32, 6, c * P:(c + 1) * P], v_sb[0][:, h * 32:(h + 1) * 32],
                                     scr[:, h * P:(h + 1) * P], start=True, stop=True, skip_group_check=True)
            last.then_inc(sem("o_a"), 1)
            pe.wait_ge(sem("o_sb"), 1)
            for u in range(4):
                last = pe.transpose(ps[:, 5, u * P:(u + 1) * P], qt[:, u * P:(u + 1) * P], ident)
            last.then_inc(sem("o_t"), 1)

            def project(n, src, w, at):
                keep_warm(4)
                pe.wait_ge(sem("head_out"), n + 1)
                pe.transpose(ps[:, 7, 0:128], src[:, 0:128], ident)
                pe.transpose(ps[:, 7, 128:256], src[:, 128:256], ident).then_inc(sem("head_t_psum"), 1)
                keep_warm(2)
                pe.wait_ge(sem("head_t"), n + 1)
                for k in range(DK):
                    last = mm(ps[:, 5, 0:D], xt[:, k * P:(k + 1) * P], w[:, at + k * D:at + (k + 1) * D], k, DK)
                last.then_inc(sem("y"), 1)

            project(0, yb, wlb, LA["wo"])

            turn_x(2, 2, xn)
            for k in range(DK):
                last = mm(ps[:, 6, 0:E0], xt[:, k * P:(k + 1) * P], cst[:, CONST["rw"] + k * E0:CONST["rw"] + (k + 1) * E0], k, DK)
            last.then_inc(sem("router"), 1)

            F0P = F0T * P

            def weights0(e):
                place, loads = place0[e]
                pe.wait_ge(sem(f"place{place}"), 16 * loads)
                return places[place]

            w = weights0(0)
            for i in range(2):
                for m in range(F0T):
                    for k in range(DK):
                        c = (i * DK + k) * F0P + m * P
                        last = mm(ps[:, i, m * P:(m + 1) * P], w[:, c:c + P], xt[:, k * P:(k + 1) * P], k, DK)
            last.then_inc(sem("up_s"), 1)
            pe.wait_ge(sem("chosen"), 1)
            pe.matmul(ps[:, 6, 32:32 + E0], cst[:, CONST["before"]:CONST["before"] + P], sm[:, 64:64 + E0],
                      start=True, stop=True).then_inc(sem("rank"), 1)
            pe.wait_ge(sem("hid_s"), 1)
            for m in range(F0T):
                last = pe.matmul(ps[:, 7, 0:D], qt[:, m * P:(m + 1) * P], w[:, 4 * F0P + m * D:4 * F0P + (m + 1) * D],
                                 start=(m == 0), stop=False, skip_group_check=True)
            last.then_inc(sem("down_s"), 1)
            pe.wait_ge(sem("one_hot"), 1)
            for k in range(DK):
                last = mm(ps[:, 4 + k, :], xn[:, k * P:(k + 1) * P], hot0, 0, 1)
            last.then_inc(sem("gathered"), 1)
            pe.wait_ge(sem("gates"), 1)
            for b in range(4):
                last = pe.transpose(ps[:, 0, b * P:(b + 1) * P], gates0[:, b * P:(b + 1) * P], ident)
            last.then_inc(sem("gates_t"), 1)

            def up0(b):
                if b >= 2:
                    pe.wait_ge(sem("hid0"), b - 1)
                ws = [weights0(1 + 4 * b + c) for c in range(4)]
                for i in range(2):
                    for k in range(DK):
                        for c in range(4):
                            at = k * 512 + (4 * b + c) * 32
                            last = pe.matmul(ps[32 * c:32 * c + 32, 2 + 2 * (b % 2) + i, 0:F0P], tokens0[:, at:at + 32],
                                             ws[c][:, (i * DK + k) * F0P:(i * DK + k + 1) * F0P], start=(k == 0),
                                             stop=(k == DK - 1), skip_group_check=True)
                last.then_inc(sem("up0"), 1)

            def turn0(b):
                pe.wait_ge(sem("hid0"), b + 1)
                if b >= 2:
                    pe.wait_ge(sem("ht0"), b - 1)
                else:
                    pe.wait_ge(sem("gates_sb"), 1)
                for m in range(F0T):
                    last = pe.transpose(ps[:, b % 2, m * P:(m + 1) * P], hid0[b % 2][:, m * P:(m + 1) * P], ident)
                last.then_inc(sem("h0_t"), 1)

            def down0(b):
                pe.wait_ge(sem("ht0"), b + 1)
                if b:
                    pe.wait_ge(sem("out0"), b)
                for m in range(F0T):
                    for c in range(4):
                        w = places[place0[1 + 4 * b + c][0]]
                        last = pe.matmul(ps[32 * c:32 * c + 32, 6, 0:D], hid0_t[b % 2][:, m * P + 32 * c:m * P + 32 * c + 32],
                                         w[:, 4 * F0P + m * D:4 * F0P + (m + 1) * D], start=(m == 0), stop=(m == F0T - 1),
                                         skip_group_check=True)
                last.then_inc(sem("down0"), 1)

            def spread0(b):
                pe.wait_ge(sem("out0"), b + 1)
                pe.matmul(ps[:, 7, 0:D], gates0_t[:, b * P:(b + 1) * P], out0[b % 2], start=False, stop=(b == 3),
                          skip_group_check=True).then_inc(sem("spread0"), 1)

            pe.wait_ge(sem("tokens"), 1)
            up0(0)
            turn0(0)
            down0(0)
            up0(1)
            turn0(1)
            spread0(0)
            down0(1)
            keep_warm(20, 4)
            up0(2)
            spread0(1)
            turn0(2)
            down0(2)
            keep_warm(26, 2)
            up0(3)
            spread0(2)
            turn0(3)
            down0(3)
            spread0(3)

            cross(1)
            pe.wait_ge(sem("o_sb"), 2)
            for u in range(4):
                last = pe.transpose(ps[:, 5, u * P:(u + 1) * P], qt[:, u * P:(u + 1) * P], ident)
            last.then_inc(sem("o_t"), 1)
            project(1, yb, wx1, XQ1["wo"])

            turn_x(4, 4, xn)
            pe.wait_ge(sem("lb_loaded"), 16 * -(-LBW // 1024))
            for i, name in enumerate(("wq", "wk", "wv")):
                for k in range(DK):
                    last = mm(ps[:, i // 2, (i % 2) * D:(i % 2) * D + D], xt[:, k * P:(k + 1) * P],
                              wlb[:, LB[name] + k * D:LB[name] + (k + 1) * D], k, DK)
            last.then_inc(sem("qkv_psum"), 1)
            keep_warm(26)
            pe.wait_ge(sem("unit_qk"), 1)
            for b in range(2):
                mm(ps[:, 2, b * P:(b + 1) * P], qt[:, D + b * P:D + (b + 1) * P], ya[:, b * P:(b + 1) * P], 0, 1)
            for b in range(2):
                last = pe.transpose(ps[:, 3, b * P:(b + 1) * P], qt[:, b * P:(b + 1) * P], ident)
            last.then_inc(sem("kv_psum"), 1)
            keep_warm(4, 7)
            pe.wait_ge(sem("kv"), 1)
            for b in range(2):
                last = mm(ps[:, 4, b * P:(b + 1) * P], raw[0][:, b * P:(b + 1) * P], raw[0][:, D + b * P:D + (b + 1) * P], 0, 1)
            last.then_inc(sem("lin_psum"), 1)
            keep_warm(2, 7)
            pe.wait_ge(sem("lin"), 1)
            for b in range(2):
                last = mm(ps[:, 5, 0:D], yb[:, b * P:(b + 1) * P], wlb[:, LB["wo"] + b * D:LB["wo"] + (b + 1) * D], b, 2)
            last.then_inc(sem("y"), 1)
            turn_x(5, 5, ya, fill=14)
            pe.wait_ge(sem("ff_loaded"), 16 * (FFW // 1024))
            for m in range(F1T):
                for k in range(DK):
                    last = mm(ps[:, m // 4, (m % 4) * P:(m % 4 + 1) * P], wa[:, k * 1024 + m * P:k * 1024 + (m + 1) * P],
                              xt[:, k * P:(k + 1) * P], k, DK)
            last.then_inc(sem("ff_up"), 1)
            keep_warm(8)
            pe.wait_ge(sem("ff_hid"), 1)
            for m in range(F1T):
                last = mm(ps[:, 5, 0:D], raw[m // 4][:, (m % 4) * P:(m % 4 + 1) * P],
                          wa[:, 2048 + m * D:2048 + (m + 1) * D], m, F1T)
            last.then_inc(sem("y"), 1)

            pe.wait_ge(sem("b1_loaded"), 16)
            pe.wait_ge(sem("own_loaded"), 16)
            for i in range(4):
                at = (i % 2) * 2 * P + (i // 2) * P
                pe.matmul(ps[:, i, :], own[:, at:at + P], b1, start=True, stop=False, skip_group_check=True)
            turn_x(7, 6, xn, fill=6, bank=4)
            for k in range(DK):
                last = mm(ps[:, 6, 0:E1], xt[:, k * P:(k + 1) * P], wlb[:, LB["wr"] + k * E1:LB["wr"] + (k + 1) * E1], k, DK)
            last.then_inc(sem("router"), 1)
            keep_warm(4, 5)
            pe.wait_ge(sem("scores_r"), 1)
            pe.transpose(ps[0:E1, 6, 128:256], sm[:, 32:32 + E1], ident).then_inc(sem("scores_t"), 1)
            keep_warm(14, 5)
            pe.wait_ge(sem("picked"), 1)
            pe.transpose(ps[:, 6, 256:256 + E1], sel[:, 3 * P:4 * P], ident[0:E1, 0:E1])
            pe.transpose(ps[:, 6, 256 + E1:256 + 2 * E1], sel[:, 2 * P:3 * P], ident[0:E1, 0:E1]).then_inc(sem("weights_psum"), 1)
            pe.wait_ge(sem("b2_loaded"), 16)
            pe.matmul(ps[:, 7, 0:D], sel[:, 3 * P:4 * P], b2[:], start=True, stop=False, skip_group_check=True)
            keep_warm(1, 5)
            pe.wait_ge(sem("taken"), 1)
            pe.matmul(ps[:, 6, 272:272 + E1], cst[:, CONST["before"]:CONST["before"] + P], sm[:, 88:96], start=True,
                      stop=True).then_inc(sem("rank"), 1)
            keep_warm(4, 5)
            pe.wait_ge(sem("one_hot"), 2)
            for k in range(DK):
                last = mm(ps[:, 4, k * D:(k + 1) * D], xn[:, k * P:(k + 1) * P], one_hot, 0, 1)
            last.then_inc(sem("gathered"), 1)
            pe.wait_ge(sem("gates"), 2)
            for b in range(2):
                last = pe.transpose(ps[:, 5, b * P:(b + 1) * P], gates[:, b * P:(b + 1) * P], ident)
            last.then_inc(sem("gates_t"), 1)

            def up1(b):
                for half in range(2):
                    for k in range(DK):
                        for c in range(4):
                            e = 4 * b + c
                            if half == 0 and k == 0:
                                pe.wait_ge(sem(w_sem(e, 0)[0]), w_sem(e, 0)[1])
                            last = pe.matmul(ps[32 * c:32 * c + 32, 2 * b + half, :], qt[:, k * D + e * TOPK:k * D + (e + 1) * TOPK],
                                             expert1[e][k][:, half * 512:(half + 1) * 512], start=False, stop=(k == DK - 1),
                                             skip_group_check=True)
                    last.then_inc(sem("up1"), 1)

            def turn1(b):
                for half in range(2):
                    pe.wait_ge(sem("gelu1"), 2 * b + half + 1)
                    if b:
                        pe.wait_ge(sem("ht"), half + 1)
                    elif half:
                        pe.wait_ge(sem("gates_sb"), 2)
                    for m in range(4):
                        last = pe.transpose(ps[:, 4 + half, m * P:(m + 1) * P], raw[half][:, m * P:(m + 1) * P], ident)
                    last.then_inc(sem("h_t"), 1)

            def down1(b):
                bank = (6, 0)[b]
                for m in range(F1T):
                    if m % 4 == 0:
                        pe.wait_ge(sem("ht"), 2 * b + m // 4 + 1)
                    for c in range(4):
                        if m == 0:
                            pe.wait_ge(sem(w_sem(4 * b + c, 1)[0]), w_sem(4 * b + c, 1)[1])
                        last = pe.matmul(ps[32 * c:32 * c + 32, bank, 0:D],
                                         v_sb[m // 4][:, (m % 4) * P + 32 * c:(m % 4) * P + 32 * c + 32],
                                         expert1[4 * b + c][2 + m // 4][:, (m % 4) * D:(m % 4 + 1) * D],
                                         start=(m == 0), stop=(m == F1T - 1), skip_group_check=True)
                last.then_inc(sem("down1"), 1)

            def spread1(b):
                pe.wait_ge(sem("out_sb"), b + 1)
                last = pe.matmul(ps[:, 7, 0:D], yb[:, b * P:(b + 1) * P], (ya, xt)[b][:], start=False, stop=(b == 1),
                                 skip_group_check=True)
                return last

            keep_warm(3, 6)
            pe.wait_ge(sem("tokens"), 2)
            up1(0)
            turn1(0)
            down1(0)
            up1(1)
            turn1(1)
            spread1(0)
            keep_warm(12, 3)
            down1(1)
            spread1(1).then_inc(sem("moe_out"), 1)

        @block.vector
        def _(dve):
            link = chain(dve, "dve_step")
            dve.wait_ge(sem("x_loaded"), 16)

            def norm(n, src, dst, eps, scale=None, shift=None):
                link(dve.bn_stats(stat[:, n, 0:6], src[:]))
                link(dve.bn_aggr(stat[:, n, 6:8], stat[:, n, 0:6]))
                dve.tensor_scalar(stat[:, n, 8:9], stat[:, n, 7:8], eps, None, ALU.add).then_inc(sem("var"), 1)
                dve.wait_ge(sem("std"), n + 1)
                link(dve.reciprocal(stat[:, n, 10:11], stat[:, n, 9:10]))
                last = dve.tensor_scalar(dst[:], src[:], stat[:, n, 6:7], stat[:, n, 10:11], ALU.subtract, ALU.mult)
                if scale is not None:
                    link(last)
                    link(dve.tensor_tensor(dst[:], dst[:], scale, ALU.mult))
                    last = dve.tensor_tensor(dst[:], dst[:], shift, ALU.add)
                last.then_inc(sem("xn"), 1)
                dve.wait_ge(sem("xn"), n + 1)

            def take_xt(k):
                dve.wait_ge(sem("xt_psum"), k + 1)
                dve.tensor_copy(xt[:], ps[:, 7, 0:D]).then_inc(sem("xt"), 1)

            def spread(ap, n):
                return ap.unsqueeze(2).to_broadcast([P, ap.shape[1], n])

            def fold():
                for s in range(SLOTS):
                    link(dve.memset(t_e[s][CB:CB + 2, :].bitcast(F32), 1.0))
                dve.memset(ones[:], 1.0).then_inc(sem("ones"), 1)
                clear_maxima(0)
                dve.wait_ge(sem("const_loaded"), 16)
                dve.wait_ge(sem("q_psum"), 1)
                link(dve.tensor_scalar(qt[:], ps[:, 0, :], float(HD[0]) ** -0.5, None, ALU.mult))
                for b in range(4):
                    last = dve.tensor_tensor(
                        scr[:, b * 2 * P:(b + 1) * 2 * P].rearrange("p (h q) -> p h q", h=2),
                        qt[:, b * P:(b + 1) * P].unsqueeze(1).to_broadcast([P, 2, P]),
                        spread(cst[:, CONST["mask2"]:CONST["mask2"] + 2], P), ALU.mult)
                last.then_inc(sem("q_diag"), 1)
                for c in range(2):
                    dve.wait_ge(sem("q_folded"), c + 1)
                    b = 1 + 3 * c
                    cs = slice(c * 512, (c + 1) * 512)
                    dve.tensor_copy(q_ha[:, cs], ps[:, b, :])
                    dve.tensor_copy(q_b[:, cs], ps[:, b + 1, :])
                    link(dve.tensor_copy(q_he[0:CB + 1, cs], ps[0:CB + 1, b + 2, :]))
                    dve.tensor_tensor(q_la[:, cs], ps[:, b, :], q_ha[:, cs].bitcast(F32), ALU.subtract)
                    dve.tensor_tensor(q_le[0:CB, cs], ps[0:CB, b + 2, :], q_he[0:CB, cs].bitcast(F32), ALU.subtract)\
                       .then_inc(sem("q_chunk"), 1)

            def clear_maxima(layer, which=(0, 1)):
                half = HEADS[layer] * 64
                for w in which:
                    link(dve.memset((run[:, 0:half], half16[:, 2048:2048 + half])[w], LOWEST))

            def queries1():
                dve.wait_ge(sem("q_psum"), 2)
                for u in range(UNITS):
                    link(dve.tensor_scalar(qt[:, u * P:(u + 1) * P], ps[:, 0, u * P:(u + 1) * P],
                                           wx1[:, XQ1["bq"] + u:XQ1["bq"] + u + 1], float(HD[1]) ** -0.5, ALU.add, ALU.mult))
                def diagonal(out, u, rows):
                    n = rows.stop - rows.start
                    return dve.tensor_tensor(
                        out.rearrange("p (h q) -> p h q", h=4), qt[rows, u * P:(u + 1) * P].unsqueeze(1).to_broadcast([n, 4, P]),
                        cst[rows, CONST["mask4"]:CONST["mask4"] + 4].unsqueeze(2).to_broadcast([n, 4, P]), ALU.mult)

                for u in range(UNITS):
                    rows = slice((u % 2) * CB, (u % 2 + 1) * CB)
                    last = diagonal((q_la, q_b)[u // 2][rows, (u % 2) * 512:(u % 2 + 1) * 512], u, rows)
                last.then_inc(sem("q_diag"), 1)
                for u in range(UNITS):
                    last = diagonal(q_all[:, u * 512:(u + 1) * 512], u, slice(0, P))
                last.then_inc(sem("q_all"), 1)
                dve.wait_ge(sem("q_all"), 1)

            def value_his(n, va, vb):
                link(dve.tensor_copy(wv_ha[:, 0:n], va))
                link(dve.tensor_copy(wv_hb[:, 0:n], vb))

            def value_los(n, va, vb):
                link(dve.tensor_tensor(wv_la[:, 0:n], va, wv_ha[:, 0:n].bitcast(F32), ALU.subtract))
                link(dve.tensor_tensor(wv_lb[:, 0:n], vb[0:CB, :], wv_hb[0:CB, 0:n].bitcast(F32), ALU.subtract))

            def key_parts():
                ka, kb = wx1[:, XQ1["wka"]:XQ1["wka"] + D], wx1[:, XQ1["wkb"]:XQ1["wkb"] + D]
                two = slice(CB, CB + 2)
                bk = wx1[two, XQ1["bk"]:XQ1["bk"] + D]
                link(dve.tensor_copy(wk_ha[:], ka))
                link(dve.tensor_copy(wk_hb[:], kb))
                link(dve.tensor_copy(wk_he[0:CB, :], kb[0:CB, :]))
                link(dve.tensor_tensor(wk_la[:], ka, wk_ha[:].bitcast(F32), ALU.subtract))
                link(dve.tensor_tensor(wk_le[0:CB, :], kb[0:CB, :], wk_he[0:CB, :].bitcast(F32), ALU.subtract))
                link(dve.tensor_copy(wk_he[two, :], bk))
                link(dve.tensor_tensor(yb[two, 0:D], bk, wk_he[two, :].bitcast(F32), ALU.subtract))
                link(dve.tensor_scalar(yb[two, 0:D], yb[two, 0:D], cst[two, CONST["pick"] + 1:CONST["pick"] + 2], None, ALU.mult))
                link(dve.scalar_tensor_tensor(wk_le[two, :], wk_he[two, :].bitcast(F32),
                                              cst[two, CONST["pick"]:CONST["pick"] + 1], yb[two, 0:D], ALU.mult, ALU.add))
                link(dve.tensor_copy(wk_he[two, :], wk_le[two, :].bitcast(F32)))

            def cross(layer):
                heads = HEADS[layer]
                units2 = heads // 4
                half = heads * 64
                norm(3 * layer, x, xn, 1e-5)
                take_xt(3 * layer)
                if layer == 0:
                    fold()
                else:
                    queries1()
                run16 = half16[:, 2048:2048 + half]

                def maxima(g, slot, first):
                    for j in range(GT):
                        t = g * GT + j
                        dve.wait_ge(sem(f"s1a_{layer}"), t + 1)
                        if not (first and slot == 0 and j == 0):
                            dve.wait_ge(sem(f"front{layer}"), t)
                        r = run[:, 0:half]
                        q = tile_buffer(layer, slot, j)
                        b = front_bank(layer, q)
                        dve.tensor_tensor(r, ps[:, b:b + half // 512, :].rearrange("p b n -> p (b n)"), r, ALU.max)\
                           .then_inc(sem(f"front{layer}"), 1)
                        dve.wait_ge(sem(f"half{layer}"), (t + 1) * UNITS1[layer])
                        if not (first and slot == 0 and j == 0):
                            dve.wait_ge(sem(f"run{layer}"), t)
                        dve.tensor_tensor(run16, half16[:, q * half:(q + 1) * half], run16, ALU.max)\
                           .then_inc(sem(f"run{layer}"), 1)

                groups(dve, maxima)
                dve.wait_ge(sem(f"run{layer}"), TILES)
                dve.tensor_copy(run[:, half:2 * half], run16).then_inc(sem("lanes"), 1)
                if layer == 0:
                    va, vb = wa[:, XQ0["wva"]:XQ0["wva"] + 512], wa[:, XQ0["wvb"]:XQ0["wvb"] + 512]
                    value_his(512, va, vb)
                else:
                    dve.wait_ge(sem("q_hi"), 1)
                    link(dve.tensor_tensor(q_le[0:CB, :], q_all[0:CB, :], q_ha[0:CB, :].bitcast(F32), ALU.subtract))
                for name, bank, at in (("lanes_f", (2, 6)[layer], 0), ("lanes_t", (3, 0)[layer], heads // 2)):
                    dve.wait_ge(sem(name), layer + 1)
                    last = dve.tensor_reduce(sm[:, at:at + heads // 2],
                                             ps[:, bank:bank + heads // 8, :].rearrange("p b (h n) -> p (b h) n", n=P),
                                             AX, ALU.max)
                    if at == 0:
                        link(last)
                last.then_inc(sem("max_q"), 1)
                dve.wait_ge(sem("max_psum"), layer + 1)
                dve.tensor_copy(m_t[0:heads, :], ps[0:heads, 4, 0:P]).then_inc(sem("max_t"), 1)
                if layer == 0:
                    value_los(512, va, vb)

                def split(g, slot, first):
                    dve.wait_ge(sem(f"ctx{slot}"), ctx_count(1, slot, g))
                    if not first:
                        dve.wait_ge(sem("v_psum0"), (g - 1) * GT)
                        dve.wait_ge(sem("s2_0"), (g - 1) * GT * units2)
                    r = raw[slot]
                    dve.tensor_copy(t_ha[slot][:], r[:, 0:GK])
                    dve.tensor_copy(t_e[slot][0:CB, :], r[0:CB, GK:2 * GK])
                    dve.tensor_copy(t_b[slot][:], r[:, GK:2 * GK]).then_inc(sem("part0"), 1)
                    dve.wait_ge(sem("part0"), g + 1)
                    dve.tensor_tensor(t_la[slot][:], r[:, 0:GK], t_ha[slot][:].bitcast(F32), ALU.subtract)
                    dve.tensor_tensor(t_b[slot][CB:P, :], r[CB:P, GK:2 * GK], t_b[slot][CB:P, :].bitcast(F32),
                                      ALU.subtract).then_inc(sem("split0"), 1)

                def keep_values(g, slot, j, first):
                    if j == 0:
                        dve.wait_ge(sem(f"v_in{slot}"), kv_count(slot, g))
                    t = g * GT + j
                    if not first:
                        dve.wait_ge(sem("pv1"), (t - 1) * units2)
                    v = kv_sb[:, slot * 1024 + j * D:slot * 1024 + (j + 1) * D]
                    dve.tensor_copy(v_sb[j][:].rearrange("p (h w) -> p h w", w=32)[:, :, 0:16],
                                    v.rearrange("p (h d) -> p h d", h=16)).then_inc(sem("v_sb1"), 1)

                def keep_keys(g, slot, first):
                    dve.wait_ge(sem(f"k_in{slot}"), kv_count(slot, g))
                    if not first:
                        dve.wait_ge(sem("s2_1"), (g - 1) * GT * units2)
                    at = (slice(0, CB), slice(CB, P))
                    keys = [kv_sb[at[w], slot * 1024 + 512:(slot + 1) * 1024].rearrange("p (b k) -> p b k", b=2)
                            for w in range(2)]
                    dve.tensor_copy(unit_halves(kk[slot], 0, at[0]), keys[0])
                    dve.tensor_copy(unit_halves(kk[slot], 1, at[1]), keys[1]).then_inc(sem("kk_hi"), 1)
                    dve.wait_ge(sem("kk_hi"), g + 1)
                    for w in range(2):
                        dve.tensor_tensor(unit_halves(kk[slot], w, at[1 - w]), keys[w],
                                          unit_halves(kk[slot], w, at[w]).bitcast(F32), ALU.subtract)
                    dve.tensor_copy(unit_halves(ke[slot], 0), unit_halves(kk[slot], 0, at[0]).bitcast(F32))
                    dve.tensor_copy(unit_halves(ke[slot], 1), unit_halves(kk[slot], 1, at[1]).bitcast(F32))\
                       .then_inc(sem("kk"), 1)

                def sum_lanes(t, j, first):
                    dve.wait_ge(sem("exp0"), (t + 1) * units2)
                    e = probs[:, j * 2048:j * 2048 + 1024]
                    if first:
                        dve.tensor_copy(run[:, 0:1024], e).then_inc(sem("lsum"), 1)
                    else:
                        dve.wait_ge(sem("lsum"), t)
                        dve.tensor_tensor(run[:, 0:1024], run[:, 0:1024], e, ALU.add).then_inc(sem("lsum"), 1)

                def tile(g, slot, j, first):
                    if layer == 0:
                        sum_lanes(g * GT + j, j, first and j == 0)
                    else:
                        keep_values(g, slot, j, first)

                def body(g, slot, first, last=False):
                    start = first and slot == 0
                    tile(g, slot, 0, start)
                    if not last:
                        (split if layer == 0 else keep_keys)(g + 1, 1 - slot, start)
                    tile(g, slot, 1, start)

                (split if layer == 0 else keep_keys)(0, 0, True)
                dve.wait_ge(sem("max_row"), 16 * (layer + 1))
                if layer == 0:
                    dve.tensor_tensor(q_le[CB:CB + 1, 0:1024], q_he[CB:CB + 1, :].bitcast(F32),
                                      scr[CB:CB + 1, 0:1024], ALU.subtract).then_inc(sem("shift"), 1)
                else:
                    dve.tensor_scalar(q_le[CB:CB + 1, :], scr[CB:CB + 1, :], -1.0, None, ALU.mult).then_inc(sem("shift"), 1)
                body(0, 0, True)
                body(1, 1, True)
                with dve.Fori(1, GROUPS // 2) as i:
                    body(2 * i, 0, False)
                    body(2 * i + 1, 1, False)
                body(GROUPS - 1, 0, False, True)
                dve.wait_ge(sem(f"pv{layer}"), TILES * units2)

            def add_y(n, bank, bias):
                dve.wait_ge(sem("y"), n + 1)
                link(dve.tensor_tensor(ya[:], ps[:, bank, 0:D], bias, ALU.add))
                dve.tensor_tensor(x[:], x[:], ya[:], ALU.add).then_inc(sem("x_done"), 1)

            def heads_out(n, bank):
                dve.tensor_copy(qt[:], ps[:, bank, :]).then_inc(sem("o_sb"), 1)
                dve.wait_ge(sem("o_t"), n + 1)
                heads = ps[:, 5, :].rearrange("p (h w) -> p h w", w=32)
                link(dve.reciprocal(sm[:, 32:48], heads[:, :, 16:17].rearrange("p h o -> p (h o)")))
                return dve.tensor_tensor(yb[:].rearrange("p (h d) -> p h d", h=16), heads[:, :, 0:16],
                                         spread(sm[:, 32:48], 16), ALU.mult)

            def head_t(n):
                dve.wait_ge(sem("head_t_psum"), n + 1)
                dve.tensor_copy(xt[:], ps[:, 7, 0:D]).then_inc(sem("head_t"), 1)

            cross(0)
            for b in range(4):
                dve.wait_ge(sem("den_psum"), b + 1)
                bs = slice(b * P, (b + 1) * P)
                link(dve.reciprocal(probs[:, bs], ps[:, b, 0:P]))
                dve.tensor_tensor(qt[:, bs], ps[:, 4, bs], probs[:, bs], ALU.mult).then_inc(sem("ot"), 1)
            add_y(0, 6, wa[:, XQ0["bo"]:XQ0["bo"] + D])
            dve.wait_ge(sem("x_done"), 1)

            norm(1, x, xn, 1e-5)
            take_xt(1)
            for i in range(2):
                link(dve.memset(v_sb[i][:], 0.0))
                link(dve.memset(v_sb[i][:].rearrange("p (h w) -> p h w", w=32)[:, :, 16:17], 1.0))
            dve.wait_ge(sem("qkv_psum"), 1)
            link(dve.tensor_scalar(qt[:, 0:D], ps[:, 0, 0:D], 0.25, None, ALU.mult))
            link(dve.tensor_copy(qt[:, D:2 * D], ps[:, 0, D:2 * D]))
            link(dve.tensor_copy(v_sb[0][:].rearrange("p (h w) -> p h w", w=32)[:, :, 0:16],
                                 ps[:, 1, 0:D].rearrange("p (h d) -> p h d", h=16)))
            for b in range(2):
                last = dve.tensor_tensor(probs[:, b * 1024:(b + 1) * 1024].rearrange("p (h q) -> p h q", h=8),
                                         qt[:, D + b * P:D + (b + 1) * P].unsqueeze(1).to_broadcast([P, 8, P]),
                                         spread(cst[:, CONST["mask8"]:CONST["mask8"] + 8], P), ALU.mult)
            last.then_inc(sem("k_diag"), 1)
            dve.wait_ge(sem("xq1_loaded"), 16)
            key_parts()
            value_his(D, wx1[:, XQ1["wva"]:XQ1["wva"] + D], wx1[:, XQ1["wvb"]:XQ1["wvb"] + D])
            value_los(D, wx1[:, XQ1["wva"]:XQ1["wva"] + D], wx1[:, XQ1["wvb"]:XQ1["wvb"] + D])
            run3 = run.rearrange("p (h n) -> p h n", h=16)
            causal = cst[:, CONST["causal"]:CONST["causal"] + P].unsqueeze(1).to_broadcast([P, 4, P])
            for c in range(4):
                dve.wait_ge(sem("s_a"), c + 1)
                r4 = run3[:, 4 * c:4 * c + 4]
                link(dve.tensor_tensor(r4, ps[:, 2 + c, :].rearrange("p (h n) -> p h n", n=P), causal, ALU.add))
                link(dve.tensor_reduce(sm[:, 4 * c:4 * c + 4], r4, AX, ALU.max))
                dve.tensor_tensor(r4, r4, spread(sm[:, 4 * c:4 * c + 4], P), ALU.subtract).then_inc(sem("logit_a"), 1)
            dve.wait_ge(sem("o_a"), 1)
            heads_out(0, 6).then_inc(sem("head_out"), 1)
            head_t(0)
            dve.wait_ge(sem("y"), 2)
            dve.tensor_tensor(x[:], ps[:, 5, 0:D], x[:], ALU.add).then_inc(sem("x_done"), 1)
            dve.wait_ge(sem("x_done"), 2)

            def softmax_small(n, width, bias):
                dve.wait_ge(sem("router"), n + 1)
                lg = sm[:, 0:width]
                if bias is None:
                    link(dve.tensor_copy(lg, ps[:, 6, 0:width]))
                else:
                    link(dve.tensor_tensor(lg, ps[:, 6, 0:width], bias, ALU.add))
                link(dve.tensor_reduce(sm[:, 48:49], lg, AX, ALU.max))
                dve.tensor_scalar(lg, lg, sm[:, 48:49], None, ALU.subtract).then_inc(sem("logit_r"), 1)
                dve.wait_ge(sem("prob_r"), n + 1)
                link(dve.tensor_reduce(sm[:, 49:50], sm[:, 16:16 + width], AX, ALU.add))
                link(dve.reciprocal(sm[:, 50:51], sm[:, 49:50]))
                last = dve.tensor_scalar(sm[:, 32:32 + width], sm[:, 16:16 + width], sm[:, 50:51], None, ALU.mult)
                return last

            norm(2, x, xn, 1e-5)
            take_xt(2)
            link(softmax_small(0, E0, cst[:, CONST["rb"]:CONST["rb"] + E0]))
            pr = sm[:, 32:32 + E0]
            link(dve.max(sm[:, 112:120], pr))
            link(dve.max_index(idx[:], sm[:, 112:120], pr))
            link(dve.tensor_copy(sm[:, 120:122], idx[:, 0:2]))
            iota = cst[:, CONST["iota"]:CONST["iota"] + E0]
            link(dve.tensor_scalar(sm[:, 128:144], iota, sm[:, 120:121], None, ALU.is_equal))
            link(dve.tensor_scalar(sm[:, 144:160], iota, sm[:, 121:122], None, ALU.is_equal))
            dve.tensor_tensor(sm[:, 64:80], sm[:, 128:144], sm[:, 144:160], ALU.add).then_inc(sem("chosen"), 1)
            link(dve.tensor_tensor(sm[:, 51:52], sm[:, 112:113], sm[:, 113:114], ALU.add))
            link(dve.tensor_scalar(sm[:, 52:53], sm[:, 51:52], 1e-9, None, ALU.add))
            link(dve.reciprocal(sm[:, 53:54], sm[:, 52:53]))
            link(dve.tensor_scalar(sm[:, 54:56], sm[:, 112:114], sm[:, 53:54], None, ALU.mult))
            link(dve.tensor_scalar(sm[:, 128:144], sm[:, 128:144], sm[:, 54:55], None, ALU.mult))
            link(dve.scalar_tensor_tensor(sm[:, 160:176], sm[:, 144:160], sm[:, 55:56], sm[:, 128:144], ALU.mult, ALU.add))
            dve.wait_ge(sem("rank"), 1)
            link(dve.scalar_tensor_tensor(sm[:, 176:192], ps[:, 6, 32:32 + E0], float(CAP), sm[:, 160:176],
                                          ALU.is_lt, ALU.mult))

            link(dve.tensor_copy(sm[:, 192:208], ps[:, 6, 32:32 + E0]))
            link(dve.scalar_tensor_tensor(sm[:, 208:224], sm[:, 192:208], float(CAP), sm[:, 64:80], ALU.is_lt, ALU.mult))
            dve.wait_ge(sem("silu_s"), 1)
            dve.tensor_tensor(qt[:, 0:F0T * P], ps[:, 1, 0:F0T * P], silu0[0], ALU.mult).then_inc(sem("hid_s"), 1)
            hot3 = hot0.rearrange("p (e s) -> p e s", e=E0)
            slots = cst[:, CONST["slot"]:CONST["slot"] + 32].unsqueeze(1).to_broadcast([P, E0, 32])
            link(dve.tensor_tensor(hot3, slots, spread(sm[:, 192:208], 32), ALU.is_equal))
            dve.tensor_tensor(hot3, hot3, spread(sm[:, 208:224], 32), ALU.mult).then_inc(sem("one_hot"), 1)
            dve.wait_ge(sem("one_hot"), 1)
            dve.tensor_tensor(gates0.rearrange("p (e s) -> p e s", e=E0), hot3, spread(sm[:, 176:192], 32), ALU.mult)\
               .then_inc(sem("gates"), 1)
            dve.wait_ge(sem("gathered"), 1)
            dve.tensor_copy(tokens0, ps[:, 4:6, :].rearrange("p b n -> p (b n)")).then_inc(sem("tokens"), 1)
            dve.wait_ge(sem("gates_t"), 1)
            dve.tensor_copy(gates0_t, ps[:, 0, :]).then_inc(sem("gates_sb"), 1)

            def hidden0(b):
                dve.wait_ge(sem("silu"), b + 1)
                if b >= 2:
                    dve.wait_ge(sem("h0_t"), b - 1)
                dve.tensor_tensor(hid0[b % 2], ps[:, 3 + 2 * (b % 2), 0:F0T * P], silu0[b % 2], ALU.mult)\
                   .then_inc(sem("hid0"), 1)

            def turned0(b):
                dve.wait_ge(sem("h0_t"), b + 1)
                if b >= 2:
                    dve.wait_ge(sem("down0"), b - 1)
                dve.tensor_copy(hid0_t[b % 2], ps[:, b % 2, 0:F0T * P]).then_inc(sem("ht0"), 1)

            def keep_out0(b):
                dve.wait_ge(sem("down0"), b + 1)
                if b >= 2:
                    dve.wait_ge(sem("spread0"), b - 1)
                dve.tensor_copy(out0[b % 2], ps[:, 6, 0:D]).then_inc(sem("out0"), 1)

            hidden0(0)
            turned0(0)
            keep_out0(0)
            hidden0(1)
            turned0(1)
            keep_out0(1)
            for q in (q_la, q_b):
                dve.memset(q[CB:P, 0:512].bitcast(F32), 0.0)
                dve.memset(q[0:CB, 512:1024].bitcast(F32), 0.0)
            clear_maxima(1, (0,))
            hidden0(2)
            turned0(2)
            keep_out0(2)
            hidden0(3)
            turned0(3)
            clear_maxima(1, (1,))
            keep_out0(3)
            link(dve.tensor_tensor(x[:], x[:], xn[:], ALU.add))
            dve.wait_ge(sem("spread0"), 4)
            dve.tensor_tensor(x[:], ps[:, 7, 0:D], x[:], ALU.add).then_inc(sem("x_done"), 1)
            dve.wait_ge(sem("x_done"), 3)

            cross(1)
            link(heads_out(1, 4))
            dve.tensor_tensor(yb[:], yb[:], wx1[:, XQ1["bv"]:XQ1["bv"] + D], ALU.add).then_inc(sem("head_out"), 1)
            head_t(1)
            add_y(2, 5, wx1[:, XQ1["bo"]:XQ1["bo"] + D])
            dve.wait_ge(sem("x_done"), 4)

            def lb(name, n=D):
                return wlb[:, LB[name]:LB[name] + n]

            norm(4, x, xn, 1e-5)
            take_xt(4)
            dve.wait_ge(sem("qkv_psum"), 2)
            link(dve.tensor_tensor(qt[:], ps[:, 0, :], lb("bqk", 512), ALU.add))
            link(dve.tensor_tensor(ya[:], ps[:, 1, 0:D], lb("bv"), ALU.add))
            dve.tensor_scalar(raw[1][:, 0:512], qt[:], 0.0, None, ALU.min).then_inc(sem("elu_in"), 1)
            dve.wait_ge(sem("elu_exp"), 1)
            link(dve.tensor_scalar(raw[0][:, 0:512], raw[1][:, 0:512], -1.0, None, ALU.add))
            link(dve.scalar_tensor_tensor(qt[:], qt[:], 0.0, raw[0][:, 0:512], ALU.max, ALU.add))
            link(dve.tensor_tensor(raw[0][:, 0:512], qt[:], qt[:], ALU.mult))
            dve.tensor_reduce(sm[:, 0:32], raw[0][:, 0:512].rearrange("p (h d) -> p h d", h=32), AX, ALU.add)\
               .then_inc(sem("norm_in"), 1)
            dve.wait_ge(sem("norm_out"), 1)
            link(dve.reciprocal(sm[:, 64:96], sm[:, 32:64]))
            qt3 = qt[:].rearrange("p (h d) -> p h d", h=32)
            dve.tensor_tensor(qt3, qt3, spread(sm[:, 64:96], 16), ALU.mult).then_inc(sem("unit_qk"), 1)
            dve.wait_ge(sem("kv_psum"), 1)
            diag = spread(cst[:, CONST["mask8"]:CONST["mask8"] + 8], 16)
            for b in range(2):
                link(dve.scalar_tensor_tensor(raw[0][:, b * P:(b + 1) * P].rearrange("p (h d) -> p h d", h=8),
                                              ps[:, 2, b * P:(b + 1) * P].rearrange("p (h d) -> p h d", h=8), 0.25, diag,
                                              ALU.mult, ALU.mult))
            dve.tensor_copy(raw[0][:, D:2 * D], ps[:, 3, 0:D]).then_inc(sem("kv"), 1)
            dve.wait_ge(sem("lin_psum"), 1)
            dve.tensor_copy(yb[:], ps[:, 4, 0:D]).then_inc(sem("lin"), 1)
            dve.wait_ge(sem("y"), 4)
            link(dve.tensor_tensor(ya[:], ps[:, 5, 0:D], lb("bo"), ALU.add))
            link(dve.tensor_tensor(yb[:], ya[:], xn[:], ALU.add))
            norm(5, yb, ya, 1e-12, lb("g1"), lb("be1"))
            take_xt(5)
            dve.wait_ge(sem("y"), 5)
            link(dve.tensor_tensor(yb[:], ps[:, 5, 0:D], lb("b2"), ALU.add))
            link(dve.tensor_tensor(yb[:], yb[:], ya[:], ALU.add))
            norm(6, yb, ya, 1e-12, lb("g2"), lb("be2"))
            dve.tensor_tensor(x[:], x[:], ya[:], ALU.add).then_inc(sem("x_done"), 1)
            dve.wait_ge(sem("x_done"), 5)

            norm(7, x, xn, 1e-5)
            take_xt(6)
            softmax_small(1, E1, None).then_inc(sem("scores_r"), 1)
            dve.wait_ge(sem("scores_t"), 1)
            link(dve.tensor_copy(sel[:, 0:P], ps[0:E1, 6, 128:256]))
            link(dve.tensor_copy(sel[:, P:2 * P], ps[0:E1, 6, 128:256]))
            for r in range(TOPK // 8):
                cur, nxt = 1 + r % 2, 1 + (r + 1) % 2
                link(dve.max(sm[0:E1, 64:72], sel[:, cur * P:(cur + 1) * P]))
                link(dve.match_replace(sel[:, nxt * P:(nxt + 1) * P], sm[0:E1, 64:72], sel[:, cur * P:(cur + 1) * P], -1.0))
            link(dve.scalar_tensor_tensor(sel[:, 3 * P:4 * P], sel[:, nxt * P:(nxt + 1) * P], 0.0, sel[:, 0:P],
                                          ALU.is_lt, ALU.mult))
            assert nxt == 1
            dve.tensor_scalar(sel[:, 2 * P:3 * P], sel[:, P:2 * P], 0.0, None, ALU.is_lt).then_inc(sem("picked"), 1)
            dve.wait_ge(sem("weights_psum"), 1)
            dve.tensor_copy(sm[:, 80:96], ps[:, 6, 256:272]).then_inc(sem("taken"), 1)
            dve.wait_ge(sem("taken"), 1)
            dve.wait_ge(sem("rank"), 2)
            link(dve.tensor_copy(sm[:, 96:104], ps[:, 6, 272:280]))
            hot3 = one_hot.rearrange("p (e s) -> p e s", e=E1)
            slots = cst[:, CONST["slot"]:CONST["slot"] + TOPK].unsqueeze(1).to_broadcast([P, E1, TOPK])
            link(dve.tensor_tensor(hot3, slots, spread(sm[:, 96:104], TOPK), ALU.is_equal))
            dve.tensor_tensor(hot3, hot3, spread(sm[:, 88:96], TOPK), ALU.mult).then_inc(sem("one_hot"), 1)
            dve.wait_ge(sem("one_hot"), 2)
            dve.tensor_tensor(gates.rearrange("p (e s) -> p e s", e=E1), hot3, spread(sm[:, 80:88], TOPK), ALU.mult)\
               .then_inc(sem("gates"), 1)
            dve.wait_ge(sem("gathered"), 2)
            dve.tensor_copy(qt[:], ps[:, 4, :]).then_inc(sem("tokens"), 1)
            dve.wait_ge(sem("gates_t"), 2)
            dve.tensor_copy(yb[:], ps[:, 5, 0:D]).then_inc(sem("gates_sb"), 1)
            for b in range(2):
                for half in range(2):
                    dve.wait_ge(sem("h_t"), 2 * b + half + 1)
                    if b:
                        dve.wait_ge(sem("down1"), 1)
                    dve.tensor_copy(v_sb[half][:], ps[:, 4 + half, :]).then_inc(sem("ht"), 1)
                dve.wait_ge(sem("down1"), b + 1)
                dve.tensor_copy((ya, xt)[b][:], ps[:, (6, 0)[b], 0:D]).then_inc(sem("out_sb"), 1)
            dve.wait_ge(sem("moe_out"), 1)
            dve.tensor_tensor(x[:], ps[:, 7, 0:D], x[:], ALU.add).then_inc(sem("result"), 1)


def tiles(w, n=P):
    k = w.shape[0] // n
    return w.reshape(k, n, w.shape[1]).transpose(1, 0, 2).reshape(n, -1)


def rows(v):
    return np.broadcast_to(np.asarray(v).reshape(1, -1), (P, np.asarray(v).size))


def twice(w):
    u = w.reshape(w.shape[0], UNITS, 1, CB)
    return np.broadcast_to(u, (w.shape[0], UNITS, 2, CB)).reshape(w.shape[0], -1)


def xq0_pack(wq, wk, wv, wo, bo):
    nb = wq.shape[1] // P
    kt = wk.T.reshape(nb, P, C)
    kt = np.concatenate([kt[:, :, 0:P], kt[:, :, P:], kt[:, :, P:], kt[:, :, P:], np.zeros((nb, P, 1), wk.dtype)], 2)
    return np.concatenate([tiles(wq), kt.transpose(1, 0, 2).reshape(P, -1), wv[0:P], np.concatenate([wv[P:], wv[P:]], 0),
                           tiles(wo), rows(bo)], 1)


def xq1_pack(wq, wk, wv, wo, bo, bq, bk, bv):
    return np.concatenate([tiles(twice(wq)), wk[0:P], np.concatenate([wk[P:], wk[P:]], 0), rows(bk),
                           rows(bv), twice(bq.reshape(1, -1)).reshape(UNITS, P).T, wv[0:P],
                           np.concatenate([wv[P:], wv[P:]], 0), tiles(wo), rows(bo)], 1)


def constants():
    p = np.arange(P)
    f = np.float32
    return (np.eye(P, dtype=f), (p[:, None] < p[None, :]).astype(f),
            np.where(p[None, :] > p[:, None], f(-1e30), f(0)).astype(f),
            (p[:, None] // 64 == np.arange(2)[None, :]).astype(f),
            (p[:, None] // 16 == np.arange(8)[None, :]).astype(f),
            np.broadcast_to(np.arange(E0, dtype=f)[None, :], (P, E0))), (
            (p[:, None] % 64 // 16 == np.arange(4)[None, :]).astype(f),
            (p[:, None] == CB + np.arange(2)[None, :]).astype(f),
            np.broadcast_to(np.arange(TOPK, dtype=f)[None, :], (P, TOPK)))


def owners():
    col = np.arange(4 * P)
    owner = col // (2 * P) * E1 + col // P % 2 * 4 + col % P // TOPK
    return (np.arange(2 * E1)[:, None] == owner[None, :]).astype(np.float32)


def kernel(**inputs):
    import concourse.bacc as bacc
    from concourse.bass_utils import run_bass_kernel_spmd

    a = {k: np.asarray(v) for k, v in inputs.items()}
    ctx = a["ctx_768"].reshape(GROUPS, P, GT, C)
    turned = ctx.transpose(0, 3, 2, 1)
    pack = np.concatenate([turned[:, 0:P].reshape(GROUPS, P, GK),
                           np.concatenate([turned[:, P:], turned[:, P:]], 1).reshape(GROUPS, P, GK)], 2)
    first, last = constants()

    def wide_f(w):
        return np.concatenate([w, np.zeros((*w.shape[:-1], F0T * P - F0), w.dtype)], -1)

    def expert0(g, u, d):
        dp = np.concatenate([d, np.zeros((F0T * P - F0, D), d.dtype)], 0)
        return np.concatenate([tiles(wide_f(g)), tiles(wide_f(u)), tiles(dp)], 1)

    ex0 = np.stack([expert0(a["L0_ffn_sw_gate"], a["L0_ffn_sw_up"], a["L0_ffn_sw_down"])]
                   + [expert0(a["L0_ffn_w_gate"][e], a["L0_ffn_w_up"][e], a["L0_ffn_w_down"][e]) for e in range(E0)])
    ex1 = np.stack([np.concatenate([tiles(a["L1_ffn_W1"][e]), tiles(a["L1_ffn_W2"][e])], 1)
                    for e in range(E1)])
    L1 = {k[8:]: v for k, v in a.items() if k.startswith("L1_attn_")}
    arrays = {
        "x_in": a["x"][0],
        "ctx_in": pack,
        "xq0_in": xq0_pack(a["L0_xattn_Wq"], a["L0_xattn_Wk"], a["L0_xattn_Wv"], a["L0_xattn_Wo"], a["L0_xattn_bo"]),
        "xq1_in": xq1_pack(*(a["L1_xattn_" + n] for n in ("Wq", "Wk", "Wv", "Wo", "bo", "bq", "bk", "bv"))),
        "const_in": np.concatenate([*first, rows(a["L0_ffn_router_b"]), tiles(a["L0_ffn_router_w"]), *last], 1),
        "la_in": np.concatenate([tiles(a["L0_attn_" + n].T) for n in ("Wq", "Wk", "Wv", "Wo")], 1),
        "lb_in": np.concatenate([tiles(L1["Wq"]), tiles(L1["Wk"]), tiles(L1["Wv"]), tiles(L1["Wo"]), tiles(a["L1_ffn_Wr"]),
                                 rows(L1["bq"]), rows(L1["bk"]), rows(L1["bv"]), rows(L1["bo"]), rows(L1["g1"]),
                                 rows(L1["be1"]), rows(L1["b2"]), rows(L1["g2"]), rows(L1["be2"]),
                                 L1["b1"].reshape(F1T, P).T], 1),
        "ff_in": np.concatenate([tiles(L1["W1"]), tiles(L1["W2"])], 1),
        "ex0_in": ex0,
        "ex1_in": ex1,
        "b1_in": a["L1_ffn_b1"].reshape(E1, 2, 512).transpose(1, 0, 2).reshape(2 * E1, 512),
        "own_in": owners(),
        "b2_in": a["L1_ffn_b2"],
    }
    nc = bacc.Bacc("TRN2", target_bir_lowering=False, num_devices=1)
    given, aps = {}, []
    for name, v in arrays.items():
        v = np.ascontiguousarray(v)
        given[name] = v
        aps.append(nc.dram_tensor(name, v.shape, mybir.dt.from_np(v.dtype), kind="ExternalInput").ap())
    out = nc.dram_tensor("out", (P, D), F32, kind="ExternalOutput").ap()
    k_mem = nc.dram_tensor("k_mem", (GROUPS, P, 2 * GK), F32).ap()
    v_mem = nc.dram_tensor("v_mem", (GROUPS, P, 2 * GK), F32).ap()
    perceiver(nc, *aps, k_mem, v_mem, out)
    r = run_bass_kernel_spmd(nc, [given], core_ids=[0])
    return r.results[0]["out"].reshape(1, P, D)
```
